# Optimizing a Trainium2 kernel written in Bass

```python
import numpy as np
import jax
import jax.numpy as jnp

def _softmax(x, axis=-1):
    return jax.nn.softmax(x, axis=axis)

def _gelu(x):
    return jax.nn.gelu(x, approximate=True)

def _silu(x):
    return jax.nn.silu(x)

def _sigmoid(x):
    return jax.nn.sigmoid(x)

def _layernorm(x, axis=-1, eps=1e-05):
    m = jnp.mean(x, axis=axis, keepdims=True)
    v = jnp.var(x, axis=axis, keepdims=True)
    return (x - m) / jnp.sqrt(v + eps)

def _scatter_add(tgt, idx, src, axis=0):
    return tgt.at[idx].add(src)

def _segment_sum(src, seg, n):
    return jax.ops.segment_sum(src, seg, n)
kernel_name = 'mk_perceiver_d2_seqx_r8_40b4be'

def setup_inputs(seed: int=0):
    np.random.seed(seed)
    _w = jnp.asarray

    def _rec_inputs():
        import jax
        import jax.numpy as jnp
        _rk = jax.random.key(seed)
        x = -0.0002928 + 1 * jax.random.normal(jax.random.fold_in(_rk, 1), (4, 128, 128), jnp.float32)
        _lenS = 128 - jax.random.randint(jax.random.fold_in(_rk, 7), (4,), 0, max(1, 128 // 4) + 1, jnp.int32)
        _lenS2 = 2048 - jax.random.randint(jax.random.fold_in(_rk, 8), (4,), 0, max(1, 2048 // 4) + 1, jnp.int32)
        _ctx_1024P = jax.random.normal(jax.random.fold_in(_rk, 11), (4, 16, 128), jnp.float32)
        _ctx_1024c = jax.random.dirichlet(jax.random.fold_in(_rk, 511), 0.3 * jnp.ones((16,), jnp.float32), (4, 2048))
        _ctx_1024t = jnp.einsum('bsk,bkd->bsd', _ctx_1024c, _ctx_1024P)
        _ctx_1024t = _ctx_1024t * jax.lax.rsqrt(jnp.mean(jnp.square(_ctx_1024t)) + 1e-12) * 0.953939
        ctx_1024 = -1.39393e-06 + 0.999914 * (_ctx_1024t + 0.3 * jax.random.normal(jax.random.fold_in(_rk, 611), (4, 2048, 128), jnp.float32))
        fside_BxSxS2_0 = jax.random.uniform(jax.random.fold_in(_rk, 12), (4, 128, 2048), jnp.float32, 0.0, 1)
        _validS = jnp.arange(128)[None, :] < _lenS[:, None]
        _validS2 = jnp.arange(2048)[None, :] < _lenS2[:, None]
        _causal = jnp.tril(jnp.ones((128, 128), dtype=bool))
        mask_BxSxS2_ik1 = jnp.where(jnp.broadcast_to(_validS2[:, None, :], (4, 128, 2048)), 1, 0).astype(jnp.int32)
        return (x, ctx_1024, fside_BxSxS2_0, mask_BxSxS2_ik1)
    x, ctx_1024, fside_BxSxS2_0, mask_BxSxS2_ik1 = _rec_inputs()

    def _L0_xattn_setup():
        import jax, jax.numpy as jnp
        import numpy as np
        NUM_HEADS = 16
        HIDDEN = 128
        B, S = (2, 256)

        def _split_heads(x, H):
            b, s, d = x.shape
            return x.reshape(b, s, H, d // H).transpose(0, 2, 1, 3)
        key = jax.random.key(seed)
        ks = jax.random.split(key, 14)
        D = HIDDEN
        scale = 1.0 / np.sqrt(D)
        inp = {'query': jax.random.normal(ks[0], (B, S, D), jnp.float32), 'key_in': jax.random.normal(ks[1], (B, S, D), jnp.float32), 'value': jax.random.normal(ks[2], (B, S, D), jnp.float32), 'group_prob': jax.random.uniform(ks[3], (B, S, S), jnp.float32), 'mask': jax.random.randint(ks[4], (B, S, S), 0, 2, jnp.int32), 'wq_k': jax.random.normal(ks[5], (D, D), jnp.float32) * scale, 'wq_b': jnp.zeros((D,), jnp.float32), 'wk_k': jax.random.normal(ks[6], (D, D), jnp.float32) * scale, 'wk_b': jnp.zeros((D,), jnp.float32), 'wv_k': jax.random.normal(ks[7], (D, D), jnp.float32) * scale, 'wv_b': jnp.zeros((D,), jnp.float32), 'wo_k': jax.random.normal(ks[8], (D, D), jnp.float32) * scale, 'wo_b': jnp.zeros((D,), jnp.float32)}
        return inp
    _L0_xattn_all = _L0_xattn_setup()
    _L0_xattn_in = {k: v for k, v in _L0_xattn_all.items() if k in ('wq_k', 'wq_b', 'wk_k', 'wk_b', 'wv_k', 'wv_b', 'wo_k', 'wo_b')}
    del _L0_xattn_all

    def _L0_attn_setup():
        import jax, jax.numpy as jnp
        import numpy as np
        D_MODEL = 128
        H = 8
        S = 128
        HD = 128
        LV = 12
        B = 2
        T = 256

        def _level_structure(t, num_levels):
            idx = np.arange(t)
            d = idx[:, None] - idx[None, :]
            lvl = np.where(d <= 0, 0, np.floor(np.log2(np.maximum(d, 1))).astype(np.int64) + 1)
            lvl = np.minimum(lvl, num_levels - 1)
            mask = d >= 0
            return (jnp.asarray(lvl), jnp.asarray(mask))
        key = jax.random.key(seed)
        ks = jax.random.split(key, 8)
        sd = 1.0 / np.sqrt(D_MODEL)
        return {'x': jax.random.normal(ks[0], (B, T, D_MODEL), jnp.float32), 'Wq': jax.random.normal(ks[1], (H * S, D_MODEL), jnp.float32) * sd, 'Wk': jax.random.normal(ks[2], (H * S, D_MODEL), jnp.float32) * sd, 'Wv': jax.random.normal(ks[3], (H * HD, D_MODEL), jnp.float32) * sd, 'Wg': jax.random.normal(ks[4], (H, D_MODEL), jnp.float32) * sd, 'bg': jnp.zeros((H,), jnp.float32), 'Wdl': jax.random.normal(ks[5], (H * LV, D_MODEL), jnp.float32) * sd, 'Lparam': jnp.ones((H, LV), jnp.float32), 'Wo': jax.random.normal(ks[6], (D_MODEL, H * HD), jnp.float32) / np.sqrt(H * HD), 'ln_g': jnp.ones((D_MODEL,), jnp.float32), 'ln_b': jnp.zeros((D_MODEL,), jnp.float32)}
    _L0_attn_all = _L0_attn_setup()
    _L0_attn_in = {k: v for k, v in _L0_attn_all.items() if k in ('Wq', 'Wk', 'Wv', 'Wg', 'bg', 'Wdl', 'Lparam', 'Wo', 'ln_g', 'ln_b')}
    del _L0_attn_all

    def _L0_ffn_setup():
        import jax, jax.numpy as jnp
        import numpy as np
        DIM = 128
        HID = 256
        E = 8
        K = 2
        R = 16
        B_, S_ = (2, 128)

        def _lora_in(xf, W, b, A, B):
            base = jnp.einsum('td,ehd->teh', xf, W)
            low = jnp.einsum('ter,ehr->teh', jnp.einsum('td,erd->ter', xf, A), B)
            return base + low + b

        def _lora_out(g, W, b, A, B):
            base = jnp.einsum('teh,edh->ted', g, W)
            low = jnp.einsum('ter,edr->ted', jnp.einsum('teh,erh->ter', g, A), B)
            return base + low + b
        key = jax.random.key(seed)
        ks = jax.random.split(key, 14)
        n = lambda k, shape, scale: jax.random.normal(k, shape, jnp.float32) * scale
        inp = {'x': jax.random.normal(ks[0], (B_, S_, DIM), jnp.float32), 'Wg': n(ks[1], (E, DIM), DIM ** (-0.5)), 'W1': n(ks[2], (E, HID, DIM), DIM ** (-0.5)), 'b1': jnp.zeros((E, HID), jnp.float32), 'A1': n(ks[3], (E, R, DIM), DIM ** (-0.5)), 'B1': n(ks[4], (E, HID, R), 0.01), 'W2': n(ks[5], (E, DIM, HID), HID ** (-0.5)), 'b2': jnp.zeros((E, DIM), jnp.float32), 'A2': n(ks[6], (E, R, HID), HID ** (-0.5)), 'B2': n(ks[7], (E, DIM, R), 0.01), 'W3': n(ks[8], (E, HID, DIM), DIM ** (-0.5)), 'b3': jnp.zeros((E, HID), jnp.float32), 'A3': n(ks[9], (E, R, DIM), DIM ** (-0.5)), 'B3': n(ks[10], (E, HID, R), 0.01)}
        return inp
    _L0_ffn_all = _L0_ffn_setup()
    _L0_ffn_in = {k: v for k, v in _L0_ffn_all.items() if k in ('Wg', 'W1', 'b1', 'A1', 'B1', 'W2', 'b2', 'A2', 'B2', 'W3', 'b3', 'A3', 'B3')}
    del _L0_ffn_all

    def _L1_xattn_setup():
        import jax, jax.numpy as jnp
        import numpy as np
        B, SQ, SK, HID, NH = (4, 256, 256, 128, 16)
        HD = HID // NH

        def _heads(x):
            b, s, _ = x.shape
            return x.reshape(b, s, NH, HD).transpose(0, 2, 1, 3)
        key = jax.random.key(seed)
        ks = jax.random.split(key, 8)
        s = 1.0 / np.sqrt(HID)
        return {'hidden_states': jax.random.normal(ks[0], (B, SQ, HID), jnp.float32), 'context': jax.random.normal(ks[1], (B, SK, HID), jnp.float32), 'Wq': jax.random.normal(ks[2], (HID, HID), jnp.float32) * s, 'bq': jnp.zeros((HID,), jnp.float32), 'Wk': jax.random.normal(ks[3], (HID, HID), jnp.float32) * s, 'bk': jnp.zeros((HID,), jnp.float32), 'Wv': jax.random.normal(ks[4], (HID, HID), jnp.float32) * s, 'bv': jnp.zeros((HID,), jnp.float32)}
    _L1_xattn_all = _L1_xattn_setup()
    _L1_xattn_in = {k: v for k, v in _L1_xattn_all.items() if k in ('Wq', 'bq', 'Wk', 'bk', 'Wv', 'bv')}
    del _L1_xattn_all

    def _L1_attn_setup():
        import jax, jax.numpy as jnp
        import numpy as np
        D = 128
        K_LOW1 = D // 4
        K_LOW2 = D // 4

        def mix_precision_matmul(x, w):
            d = x.shape[-1]
            w1 = w[:K_LOW1]
            wh = w[K_LOW1:d - K_LOW2]
            w2 = w[d - K_LOW2:]
            y1 = jnp.matmul(x[..., :K_LOW1].astype(jnp.float16), w1.astype(jnp.float16)).astype(jnp.float32)
            yh = jnp.matmul(x[..., K_LOW1:d - K_LOW2], wh)
            y2 = jnp.matmul(x[..., d - K_LOW2:].astype(jnp.float16), w2.astype(jnp.float16)).astype(jnp.float32)
            return y1 + yh + y2
        key = jax.random.key(seed)
        k1, k2, k3, k4 = jax.random.split(key, 4)
        B, N, d = (8, 256, D)
        x = jax.random.normal(k1, (B, N, d), dtype=jnp.float32)
        weight_qkv = jax.random.normal(k2, (d, 3 * d), dtype=jnp.float32) * d ** (-0.5)
        out_w = jax.random.normal(k3, (d, d), dtype=jnp.float32) * d ** (-0.5)
        out_b = jax.random.normal(k4, (d,), dtype=jnp.float32) * 0.01
        return {'x': x, 'weight_qkv': weight_qkv, 'out_w': out_w, 'out_b': out_b}
    _L1_attn_all = _L1_attn_setup()
    _L1_attn_in = {k: v for k, v in _L1_attn_all.items() if k in ('weight_qkv', 'out_w', 'out_b')}
    del _L1_attn_all

    def _L1_ffn_setup():
        import jax, jax.numpy as jnp
        import numpy as np
        B, S, D = (4, 512, 128)
        E, I = (8, 256)
        CAPACITY = 2
        K = max(1, int(S / E * CAPACITY))
        key = jax.random.key(seed)
        k1, k2, k3, k4, k5 = jax.random.split(key, 5)
        x = jax.random.normal(k1, (B, S, D), dtype=jnp.float32)
        gate_w = jax.random.normal(k2, (D, E), dtype=jnp.float32) * 0.006
        Wg = jax.random.normal(k3, (E, D, I), dtype=jnp.float32) * 0.02
        Wu = jax.random.normal(k4, (E, D, I), dtype=jnp.float32) * 0.02
        Wd = jax.random.normal(k5, (E, I, D), dtype=jnp.float32) * 0.02
        return {'x': x, 'gate_w': gate_w, 'Wg': Wg, 'Wu': Wu, 'Wd': Wd}
    _L1_ffn_all = _L1_ffn_setup()
    _L1_ffn_in = {k: v for k, v in _L1_ffn_all.items() if k in ('gate_w', 'Wg', 'Wu', 'Wd')}
    del _L1_ffn_all
    return {'x': x, 'ctx_1024': ctx_1024, 'fside_BxSxS2_0': fside_BxSxS2_0, 'mask_BxSxS2_ik1': mask_BxSxS2_ik1, 'L0_xattn_wq_k': _L0_xattn_in['wq_k'], 'L0_xattn_wq_b': _L0_xattn_in['wq_b'], 'L0_xattn_wk_k': _L0_xattn_in['wk_k'], 'L0_xattn_wk_b': _L0_xattn_in['wk_b'], 'L0_xattn_wv_k': _L0_xattn_in['wv_k'], 'L0_xattn_wv_b': _L0_xattn_in['wv_b'], 'L0_xattn_wo_k': _L0_xattn_in['wo_k'], 'L0_xattn_wo_b': _L0_xattn_in['wo_b'], 'L0_attn_Wq': _L0_attn_in['Wq'], 'L0_attn_Wk': _L0_attn_in['Wk'], 'L0_attn_Wv': _L0_attn_in['Wv'], 'L0_attn_Wg': _L0_attn_in['Wg'], 'L0_attn_bg': _L0_attn_in['bg'], 'L0_attn_Wdl': _L0_attn_in['Wdl'], 'L0_attn_Lparam': _L0_attn_in['Lparam'], 'L0_attn_Wo': _L0_attn_in['Wo'], 'L0_attn_ln_g': _L0_attn_in['ln_g'], 'L0_attn_ln_b': _L0_attn_in['ln_b'], 'L0_ffn_Wg': _L0_ffn_in['Wg'], 'L0_ffn_W1': _L0_ffn_in['W1'], 'L0_ffn_b1': _L0_ffn_in['b1'], 'L0_ffn_A1': _L0_ffn_in['A1'], 'L0_ffn_B1': _L0_ffn_in['B1'], 'L0_ffn_W2': _L0_ffn_in['W2'], 'L0_ffn_b2': _L0_ffn_in['b2'], 'L0_ffn_A2': _L0_ffn_in['A2'], 'L0_ffn_B2': _L0_ffn_in['B2'], 'L0_ffn_W3': _L0_ffn_in['W3'], 'L0_ffn_b3': _L0_ffn_in['b3'], 'L0_ffn_A3': _L0_ffn_in['A3'], 'L0_ffn_B3': _L0_ffn_in['B3'], 'L1_xattn_Wq': _L1_xattn_in['Wq'], 'L1_xattn_bq': _L1_xattn_in['bq'], 'L1_xattn_Wk': _L1_xattn_in['Wk'], 'L1_xattn_bk': _L1_xattn_in['bk'], 'L1_xattn_Wv': _L1_xattn_in['Wv'], 'L1_xattn_bv': _L1_xattn_in['bv'], 'L1_attn_weight_qkv': _L1_attn_in['weight_qkv'], 'L1_attn_out_w': _L1_attn_in['out_w'], 'L1_attn_out_b': _L1_attn_in['out_b'], 'L1_ffn_gate_w': _L1_ffn_in['gate_w'], 'L1_ffn_Wg': _L1_ffn_in['Wg'], 'L1_ffn_Wu': _L1_ffn_in['Wu'], 'L1_ffn_Wd': _L1_ffn_in['Wd']}

def reference(x, ctx_1024, fside_BxSxS2_0, mask_BxSxS2_ik1, L0_xattn_wq_k, L0_xattn_wq_b, L0_xattn_wk_k, L0_xattn_wk_b, L0_xattn_wv_k, L0_xattn_wv_b, L0_xattn_wo_k, L0_xattn_wo_b, L0_attn_Wq, L0_attn_Wk, L0_attn_Wv, L0_attn_Wg, L0_attn_bg, L0_attn_Wdl, L0_attn_Lparam, L0_attn_Wo, L0_attn_ln_g, L0_attn_ln_b, L0_ffn_Wg, L0_ffn_W1, L0_ffn_b1, L0_ffn_A1, L0_ffn_B1, L0_ffn_W2, L0_ffn_b2, L0_ffn_A2, L0_ffn_B2, L0_ffn_W3, L0_ffn_b3, L0_ffn_A3, L0_ffn_B3, L1_xattn_Wq, L1_xattn_bq, L1_xattn_Wk, L1_xattn_bk, L1_xattn_Wv, L1_xattn_bv, L1_attn_weight_qkv, L1_attn_out_w, L1_attn_out_b, L1_ffn_gate_w, L1_ffn_Wg, L1_ffn_Wu, L1_ffn_Wd):
    import jax
    import jax.numpy as jnp

    def _L0_xattn_ref(query, key_in, value, group_prob, mask, wq_k, wq_b, wk_k, wk_b, wv_k, wv_b, wo_k, wo_b):
        import jax, jax.numpy as jnp
        import numpy as np
        NUM_HEADS = 16
        HIDDEN = 128
        B, S = (2, 256)

        def _split_heads(x, H):
            b, s, d = x.shape
            return x.reshape(b, s, H, d // H).transpose(0, 2, 1, 3)
        H = NUM_HEADS
        dh = query.shape[-1] // H
        q = _split_heads(query @ wq_k + wq_b, H)
        k = _split_heads(key_in @ wk_k + wk_b, H)
        v = _split_heads(value @ wv_k + wv_b, H)
        logits = jnp.einsum('bhqd,bhkd->bhqk', q, k) / jnp.sqrt(jnp.asarray(dh, q.dtype))
        neg = (1.0 - mask.astype(q.dtype)) * -1000000000.0
        logits = logits + neg[:, None, :, :]
        attn = jax.nn.softmax(logits, axis=-1)
        attn = attn * group_prob[:, None, :, :]
        out = jnp.einsum('bhqk,bhkd->bhqd', attn, v)
        out = out.transpose(0, 2, 1, 3).reshape(query.shape[0], -1, H * dh)
        return out @ wo_k + wo_b

    def _L0_attn_ref(x, Wq, Wk, Wv, Wg, bg, Wdl, Lparam, Wo, ln_g, ln_b):
        import jax, jax.numpy as jnp
        import numpy as np
        D_MODEL = 128
        H = 8
        S = 128
        HD = 128
        LV = 12
        B = 2
        T = 256

        def _level_structure(t, num_levels):
            idx = np.arange(t)
            d = idx[:, None] - idx[None, :]
            lvl = np.where(d <= 0, 0, np.floor(np.log2(np.maximum(d, 1))).astype(np.int64) + 1)
            lvl = np.minimum(lvl, num_levels - 1)
            mask = d >= 0
            return (jnp.asarray(lvl), jnp.asarray(mask))
        b, t, _ = x.shape
        q = (x @ Wq.T).reshape(b, t, H, S)
        k = (x @ Wk.T).reshape(b, t, H, S)
        v = (x @ Wv.T).reshape(b, t, H, HD)
        g = -jax.nn.softplus(x @ Wg.T + bg)
        dl = (x @ Wdl.T).reshape(b, t, H, LV)
        lam = jax.nn.softplus(dl + Lparam[None, None])
        G = jnp.cumsum(g, axis=1)
        lvl, mask = _level_structure(t, LV)
        scale = 1.0 / np.sqrt(S)
        scores = jnp.einsum('bthd,bshd->bhts', q, k) * scale
        Gh = G.transpose(0, 2, 1)
        logdecay = Gh[:, :, :, None] - Gh[:, :, None, :]
        logdecay = jnp.where(mask[None, None], logdecay, -jnp.inf)
        decay = jnp.exp(logdecay)
        lvl_oh = jax.nn.one_hot(lvl, LV, dtype=x.dtype)
        lamw = jnp.einsum('bthl,tsl->bhts', lam, lvl_oh)
        A = scores * decay * lamw
        y = jnp.einsum('bhts,bshd->bthd', A, v).reshape(b, t, H * HD)
        out = y @ Wo.T + x
        mu = out.mean(-1, keepdims=True)
        var = out.var(-1, keepdims=True)
        return (out - mu) * jax.lax.rsqrt(var + 1e-05) * ln_g + ln_b

    def _L0_ffn_ref(x, Wg, W1, b1, A1, B1, W2, b2, A2, B2, W3, b3, A3, B3):
        import jax, jax.numpy as jnp
        import numpy as np
        DIM = 128
        HID = 256
        E = 8
        K = 2
        R = 16
        B_, S_ = (2, 128)

        def _lora_in(xf, W, b, A, B):
            base = jnp.einsum('td,ehd->teh', xf, W)
            low = jnp.einsum('ter,ehr->teh', jnp.einsum('td,erd->ter', xf, A), B)
            return base + low + b

        def _lora_out(g, W, b, A, B):
            base = jnp.einsum('teh,edh->ted', g, W)
            low = jnp.einsum('ter,edr->ted', jnp.einsum('teh,erh->ter', g, A), B)
            return base + low + b
        orig_shape = x.shape
        xf = x.reshape(-1, x.shape[-1])
        scores = jax.nn.softmax(xf @ Wg.T, axis=-1)
        expert_weights, expert_indices = jax.lax.top_k(scores, K)
        expert_weights = expert_weights / expert_weights.sum(-1, keepdims=True)
        gates = (jax.nn.one_hot(expert_indices, E, dtype=xf.dtype) * expert_weights[..., None]).sum(axis=1)
        h1 = _lora_in(xf, W1, b1, A1, B1)
        h3 = _lora_in(xf, W3, b3, A3, B3)
        g = jax.nn.silu(h1) * h3
        y_e = _lora_out(g, W2, b2, A2, B2)
        y = jnp.einsum('te,ted->td', gates, y_e)
        return y.reshape(orig_shape)

    def _L1_xattn_ref(hidden_states, context, Wq, bq, Wk, bk, Wv, bv):
        import jax, jax.numpy as jnp
        import numpy as np
        B, SQ, SK, HID, NH = (4, 256, 256, 128, 16)
        HD = HID // NH

        def _heads(x):
            b, s, _ = x.shape
            return x.reshape(b, s, NH, HD).transpose(0, 2, 1, 3)
        q = _heads(hidden_states @ Wq + bq)
        k = _heads(context @ Wk + bk)
        v = _heads(context @ Wv + bv)
        scores = jnp.einsum('bhqd,bhkd->bhqk', q, k) / jnp.sqrt(jnp.float32(HD))
        probs = jax.nn.softmax(scores, axis=-1)
        ctx = jnp.einsum('bhqk,bhkd->bhqd', probs, v)
        return ctx.transpose(0, 2, 1, 3).reshape(hidden_states.shape[0], -1, NH * HD)

    def _L1_attn_ref(x, weight_qkv, out_w, out_b):
        import jax, jax.numpy as jnp
        import numpy as np
        D = 128
        K_LOW1 = D // 4
        K_LOW2 = D // 4

        def mix_precision_matmul(x, w):
            d = x.shape[-1]
            w1 = w[:K_LOW1]
            wh = w[K_LOW1:d - K_LOW2]
            w2 = w[d - K_LOW2:]
            y1 = jnp.matmul(x[..., :K_LOW1].astype(jnp.float16), w1.astype(jnp.float16)).astype(jnp.float32)
            yh = jnp.matmul(x[..., K_LOW1:d - K_LOW2], wh)
            y2 = jnp.matmul(x[..., d - K_LOW2:].astype(jnp.float16), w2.astype(jnp.float16)).astype(jnp.float32)
            return y1 + yh + y2
        d = x.shape[-1]
        qkv = mix_precision_matmul(x, weight_qkv)
        q, k, v = jnp.split(qkv, 3, axis=-1)
        q = q / jnp.sqrt(jnp.asarray(d, dtype=q.dtype))
        qk = jnp.einsum('bqd,bkd->bqk', q, k)
        s = jax.nn.softmax(qk, axis=-1)
        y = jnp.einsum('bqk,bkd->bqd', s, v)
        return jnp.matmul(y, out_w.T) + out_b

    def _L1_ffn_ref(x, gate_w, Wg, Wu, Wd):
        import jax, jax.numpy as jnp
        import numpy as np
        B, S, D = (4, 512, 128)
        E, I = (8, 256)
        CAPACITY = 2
        K = max(1, int(S / E * CAPACITY))
        logits = jnp.einsum('bsd,de->bse', x, gate_w)
        affinity = jax.nn.softmax(logits, axis=-1)
        affinity_T = jnp.transpose(affinity, (0, 2, 1))
        gating, index = jax.lax.top_k(affinity_T, K)
        b_idx = jnp.arange(x.shape[0])[:, None, None]
        x_sel = x[b_idx, index]
        g = jnp.einsum('bekd,edi->beki', x_sel, Wg)
        u = jnp.einsum('bekd,edi->beki', x_sel, Wu)
        h = jax.nn.silu(g) * u
        out = jnp.einsum('beki,eid->bekd', h, Wd)
        contrib = out * gating[..., None]
        x_out = jnp.zeros_like(x).at[b_idx, index].add(contrib)
        return x_out
    x = x + _L0_xattn_ref(_layernorm(x, axis=-1), ctx_1024, ctx_1024, fside_BxSxS2_0, mask_BxSxS2_ik1, L0_xattn_wq_k, L0_xattn_wq_b, L0_xattn_wk_k, L0_xattn_wk_b, L0_xattn_wv_k, L0_xattn_wv_b, L0_xattn_wo_k, L0_xattn_wo_b)
    x = x + _L0_attn_ref(_layernorm(x, axis=-1), L0_attn_Wq, L0_attn_Wk, L0_attn_Wv, L0_attn_Wg, L0_attn_bg, L0_attn_Wdl, L0_attn_Lparam, L0_attn_Wo, L0_attn_ln_g, L0_attn_ln_b)
    x = x + _L0_ffn_ref(_layernorm(x, axis=-1), L0_ffn_Wg, L0_ffn_W1, L0_ffn_b1, L0_ffn_A1, L0_ffn_B1, L0_ffn_W2, L0_ffn_b2, L0_ffn_A2, L0_ffn_B2, L0_ffn_W3, L0_ffn_b3, L0_ffn_A3, L0_ffn_B3)
    x = x + _L1_xattn_ref(_layernorm(x, axis=-1), ctx_1024, L1_xattn_Wq, L1_xattn_bq, L1_xattn_Wk, L1_xattn_bk, L1_xattn_Wv, L1_xattn_bv)
    x = x + _L1_attn_ref(_layernorm(x, axis=-1), L1_attn_weight_qkv, L1_attn_out_w, L1_attn_out_b)
    x = x + _L1_ffn_ref(_layernorm(x, axis=-1), L1_ffn_gate_w, L1_ffn_Wg, L1_ffn_Wu, L1_ffn_Wd)
    return x

_drawn_inputs = setup_inputs


def setup_inputs(seed=0):
    import zlib

    import numpy as np

    out = dict(_drawn_inputs(seed))
    spreads = {'L0_xattn_wq_b': (0.0, 0.304),
     'L0_xattn_wk_b': (0.0, 2.0),
     'L0_xattn_wv_b': (0.0, 0.1),
     'L0_xattn_wo_b': (0.0, 0.1),
     'L0_attn_bg': (0.0, 0.487),
     'L0_attn_Lparam': (1.0, 0.2),
     'L0_attn_ln_g': (1.0, 0.2),
     'L0_attn_ln_b': (0.0, 0.1),
     'L0_ffn_b1': (0.0, 0.322),
     'L0_ffn_b2': (0.0, 0.285),
     'L0_ffn_b3': (0.0, 0.339),
     'L1_xattn_bq': (0.0, 0.62),
     'L1_xattn_bk': (0.0, 2.0),
     'L1_xattn_bv': (0.0, 0.1)}
    factors = {'L0_ffn_A1': 5.747,
     'L0_ffn_B1': 5.848,
     'L0_ffn_A2': 6.014,
     'L0_ffn_B2': 5.989,
     'L0_ffn_A3': 6.018,
     'L0_ffn_B3': 6.024,
     'L1_attn_out_b': 8.0,
     'L1_ffn_gate_w': 8.0,
     'L1_ffn_Wg': 8.0,
     'L1_ffn_Wu': 8.0,
     'L1_ffn_Wd': 8.0}
    for name, (base, spread) in spreads.items():
        noise = np.random.default_rng([zlib.crc32(name.encode()), seed]).standard_normal(out[name].shape)
        drawn = base * np.exp(spread * noise) if base else spread * noise
        out[name] = jnp.asarray(drawn.astype(out[name].dtype))
    for name, factor in factors.items():
        out[name] = (out[name] * factor).astype(out[name].dtype)
    return out
```

```python
from contextlib import ExitStack

import concourse.bass as bass
from concourse import mybir

ALU = mybir.AluOpType
ACT = mybir.ActivationFunctionType
F32 = mybir.dt.float32
F16 = mybir.dt.float16
BF16 = mybir.dt.bfloat16
I32 = mybir.dt.int32
U32 = mybir.dt.uint32
AX_X = mybir.AxisListType.X

P = 128
BIG_NEG = -1.0e30
EPS = 1e-5


def bcast(ap, axis, n):
    dims = list(ap.ap)
    dims.insert(axis, (0, n))
    return bass.AP(ap.tensor, ap.offset, dims)


def repeat(ap, n):
    return bass.AP(ap.tensor, ap.offset, [list(ap.ap)[0], (0, n)])


class Chain:

    def __init__(self, eng, sem, at=0):
        self.eng, self.sem, self.at = eng, sem, at

    def __call__(self, ins):
        ins.then_inc(self.sem, 1)
        self.at = self.at + 1
        self.eng.wait_ge(self.sem, self.at)


def perceiver_kernel(nc, A, out):
    B, T, D = A["x"].shape
    S2 = A["ctx_1024"].shape[1]
    NCH = S2 // P
    H, DH = 16, 8
    HA = A["L0_attn_Wg"].shape[0]
    LV = A["L0_attn_Lparam"].shape[1]
    LVU = 8
    E = A["L0_ffn_Wg"].shape[0]
    HID = A["L0_ffn_W1"].shape[1]
    R = A["L0_ffn_A1"].shape[1]
    HM = HID // P
    BT = B * T
    GK = 512
    NG = B * S2 // GK
    CPG = GK // P
    assert T == P and D == P and BT == 512 and HID == 2 * P

    with ExitStack() as ctx:
        def sb(name, shape, dt=F32):
            return ctx.enter_context(nc.sbuf_tensor(name, shape, dt))

        def sem(name):
            return ctx.enter_context(nc.semaphore(name))

        bank = [ctx.enter_context(nc.psum_tensor(f"bank{i}", [P, 512], F32)) for i in range(8)]

        x = sb("x", [P, B, D])
        xn = sb("xn", [P, B, D])
        xT = sb("xT", [P, BT])
        ident = sb("ident", [P, P])
        ident_bf = sb("ident_bf", [P, P], BF16)
        upper = sb("upper", [P, P])
        neg_upper = sb("neg_upper", [P, P])
        future_bf = sb("future_bf", [P, P], BF16)
        head_rows = sb("head_rows", [P, H])
        bn = sb("bn", [P, B, 6])
        mv = sb("mv", [P, B, 2])
        var_eps = sb("var_eps", [P, B])
        rstd = sb("rstd", [P, B])
        minus_half = sb("minus_half", [P, B])

        const_ready = sem("const_ready")
        x_loaded = sem("x_loaded")

        with nc.Block() as block:
            @block.sync
            def _(sp):
                sp.dma_start(x[:], A["x"].rearrange("b t d -> t b d")).then_inc(x_loaded, 16)

            @block.vector
            def _(dve):
                chain = Chain(dve, const_ready)
                chain(nc.vector.memset(minus_half[:], -0.5))

            cz = sem("cz")

            @block.gpsimd
            def _(pool):
                chain = Chain(pool, cz)
                chain(nc.gpsimd.memset(ident[:], 0.0))
                chain(nc.gpsimd.affine_select(out=ident[:], in_=ident[:], compare_op=ALU.not_equal, fill=1.0,
                                              base=0, pattern=[[-1, P]], channel_multiplier=1))
                chain(nc.gpsimd.tensor_copy(ident_bf[:], ident[:]))
                chain(nc.gpsimd.memset(upper[:], 1.0))
                chain(nc.gpsimd.affine_select(out=upper[:], in_=upper[:], compare_op=ALU.is_ge, fill=0.0,
                                              base=0, pattern=[[1, P]], channel_multiplier=-1))
                chain(nc.gpsimd.tensor_scalar(neg_upper[:], upper[:], -1.0, None, ALU.mult))
                chain(nc.gpsimd.memset(future_bf[:], 0.0))
                chain(nc.gpsimd.affine_select(out=future_bf[:], in_=future_bf[:], compare_op=ALU.is_ge, fill=BIG_NEG,
                                              base=0, pattern=[[-1, P]], channel_multiplier=1))
                chain(nc.gpsimd.memset(head_rows[:], 1.0))
                chain(nc.gpsimd.affine_select(out=head_rows[:], in_=head_rows[:], compare_op=ALU.is_ge, fill=0.0,
                                              base=0, pattern=[[-DH, H]], channel_multiplier=1))
                chain(nc.gpsimd.affine_select(out=head_rows[:], in_=head_rows[:], compare_op=ALU.is_ge, fill=0.0,
                                              base=DH - 1, pattern=[[DH, H]], channel_multiplier=-1))

        ln_stats, ln_var_ready, ln_rstd_ready, xn_ready, xn_transposed, xT_ready = (
            sem(n) for n in ("ln_stats", "ln_var_ready", "ln_rstd_ready", "xn_ready", "xn_transposed", "xT_ready"))

        def layer_norm(k):
            with nc.Block() as block:
                @block.vector
                def _(dve):
                    dve.wait_ge(x_loaded, 16)
                    for b in range(B):
                        nc.vector.bn_stats(bn[:, b, :], x[:, b, :]).then_inc(ln_stats, 1)
                    dve.wait_ge(ln_stats, (2 * k + 1) * B)
                    for b in range(B):
                        nc.vector.bn_aggr(mv[:, b, :], bn[:, b, :]).then_inc(ln_stats, 1)
                    dve.wait_ge(ln_stats, (2 * k + 2) * B)
                    nc.vector.tensor_scalar(var_eps[:], mv[:, :, 1], EPS, None, ALU.add).then_inc(ln_var_ready, 1)
                    dve.wait_ge(ln_rstd_ready, k + 1)
                    for b in range(B):
                        nc.vector.tensor_scalar(xn[:, b, :], x[:, b, :], mv[:, b, 0:1], rstd[:, b:b + 1],
                                                ALU.subtract, ALU.mult).then_inc(xn_ready, 1)

                @block.gpsimd
                def _(pool):
                    pool.wait_ge(ln_var_ready, k + 1)
                    nc.gpsimd.tensor_tensor(rstd[:], var_eps[:], minus_half[:], ALU.pow).then_inc(ln_rstd_ready, 1)

                @block.tensor
                def _(pe):
                    for b in range(B):
                        pe.wait_ge(xn_ready, k * B + b + 1)
                        last = nc.tensor.transpose(bank[0][:, b * P:(b + 1) * P], xn[:, b, :], ident[:])
                    last.then_inc(xn_transposed, 1)

                @block.scalar
                def _(act):
                    act.wait_ge(xn_transposed, k + 1)
                    nc.scalar.activation(xT[:], bank[0][:], ACT.Copy).then_inc(xT_ready, 1)

        def cross_attention(name, w, masked):
            with ExitStack() as c2:
                def sb(n, shape, dt=F32):
                    return c2.enter_context(nc.sbuf_tensor(f"{name}_{n}", shape, dt))

                def sem(n):
                    return ctx.enter_context(nc.semaphore(f"{name}_{n}"))

                kT = sb("kT", [P, B * S2])
                v = sb("v", [P, B * NCH, D])
                qT = sb("qT", [P, BT])
                o = sb("o", [P, B, D])
                wq, wk, wv = (sb(n, [P, D]) for n in ("wq", "wk", "wv"))
                bq, bk = sb("bq", [P, 1]), sb("bk", [P, 1])
                bv = sb("bv", [P, D])
                wo, bo = sb("wo", [P, D]), sb("bo", [P, D])
                ctx_rows = sb("ctx_rows", [P, 2, CPG, D])
                ctxT = sb("ctxT", [P, 2, GK])
                w_loaded = sem("w_loaded")
                ctx_loaded = [sem("ctx_loaded0"), sem("ctx_loaded1")]
                rows_transposed = sem("rows_transposed")
                ctxT_ready = sem("ctxT_ready")
                k_projected = sem("k_projected")
                v_projected = sem("v_projected")
                k_ready = sem("k_ready")
                v_ready = sem("v_ready")
                q_projected, q_ready = sem("q_projected"), sem("q_ready")
                n_w = 8 if masked else 6
                rows_dram = A["ctx_1024"].rearrange("b (g c p) d -> (b g) p c d", p=P, c=CPG)

                with nc.Block() as block:
                    @block.sync
                    def _(sp):
                        for dst, src in ((wq, w["wq"]), (wk, w["wk"]), (wv, w["wv"])):
                            sp.dma_start(dst[:], src).then_inc(w_loaded, 16)
                        for dst, src in ((bq, w["bq"]), (bk, w["bk"])):
                            sp.dma_start(dst[:], src.rearrange("(d a) -> d a", a=1)).then_inc(w_loaded, 16)
                        sp.dma_start(bv[:], w["bv"].partition_broadcast(P)).then_inc(w_loaded, 16)
                        if masked:
                            sp.dma_start(wo[:], w["wo"]).then_inc(w_loaded, 16)
                            sp.dma_start(bo[:], w["bo"].partition_broadcast(P)).then_inc(w_loaded, 16)
                        for u in range(2):
                            sp.dma_start(ctx_rows[:, u, :, :], rows_dram[u]).then_inc(ctx_loaded[u], 16)
                        with sp.Fori(1, NG // 2) as i:
                            for u in range(2):
                                sp.wait_ge(rows_transposed, 2 * i + u - 1)
                                sp.dma_start(ctx_rows[:, u, :, :], rows_dram[bass.ds(2 * i + u, 1)].rearrange(
                                    "a p c d -> p (a c) d")).then_inc(ctx_loaded[u], 16)

                    @block.tensor
                    def _(pe):
                        pe.sem_inc(v_projected, 1)
                        pe.wait_ge(w_loaded, 16 * n_w)
                        nc.tensor.matmul(bank[7][:], wq[:], xT[:], start=True, stop=True).then_inc(q_projected, 1)
                        with pe.Fori(0, NG // 2) as i:
                            for u in range(2):
                                pe.wait_ge(ctx_loaded[u], 16 * i + 16)
                                pe.wait_ge(ctxT_ready, 2 * i + u + 1)
                                for c in range(CPG):
                                    last = nc.tensor.transpose(bank[u][:, c * P:(c + 1) * P],
                                                               ctx_rows[:, u, c, :], ident[:])
                                last.then_inc(rows_transposed, 1)
                                pe.wait_ge(ctxT_ready, 2 * i + u + 2)
                                pe.wait_ge(k_ready, 2 * i + u + 1)
                                nc.tensor.matmul(bank[2 + u][:], wk[:], ctxT[:, u, :], start=True,
                                                 stop=True).then_inc(k_projected, 1)
                                pe.wait_ge(v_ready, 2 * i + u + 1)
                                for c in range(CPG):
                                    last = nc.tensor.matmul(bank[4 + u][:, c * P:(c + 1) * P],
                                                            ctxT[:, u, c * P:(c + 1) * P], wv[:],
                                                            start=True, stop=True)
                                last.then_inc(v_projected, 1)

                    @block.scalar
                    def _(act):
                        act.sem_inc(ctxT_ready, 1)
                        with act.Fori(0, NG // 2) as i:
                            for u in range(2):
                                act.wait_ge(rows_transposed, 2 * i + u + 1)
                                act.wait_ge(v_projected, 2 * i + u + 1)
                                nc.scalar.activation(ctxT[:, u, :], bank[u][:], ACT.Copy).then_inc(ctxT_ready, 1)

                    @block.vector
                    def _(dve):
                        dve.sem_inc(k_ready, 1)
                        dve.sem_inc(v_ready, 1)
                        dve.wait_ge(w_loaded, 16 * n_w)
                        dve.wait_ge(q_projected, 1)
                        nc.vector.tensor_scalar(qT[:], bank[7][:], bq[:], None, ALU.add).then_inc(q_ready, 1)
                        with dve.Fori(0, NG // 2) as i:
                            for u in range(2):
                                dve.wait_ge(k_projected, 2 * i + u + 1)
                                nc.vector.tensor_scalar(kT[:, bass.ds((2 * i + u) * GK, GK)], bank[2 + u][:],
                                                        bk[:], None, ALU.add).then_inc(k_ready, 1)
                                dve.wait_ge(v_projected, 2 * i + u + 2)
                                nc.vector.tensor_tensor(
                                    v[:, bass.ds((2 * i + u) * CPG, CPG), :],
                                    bank[4 + u][:].rearrange("p (c d) -> p c d", c=CPG),
                                    bcast(bv[:], 1, CPG), ALU.add).then_inc(v_ready, 1)

                qz = sb("qz", [P, P])
                s = sb("s", [P, S2])
                neg = sb("neg", [P, S2])
                gp = sb("gp", [P, S2])
                mask_i = sb("mask_i", [P, S2], I32)
                pT = sb("pT", [P, NCH, P])
                nmax, den, rden = sb("nmax", [P, 1]), sb("den", [P, 1]), sb("rden", [P, 1])
                sides_loaded = sem("sides_loaded")
                q_head_ready = sem("q_head_ready")
                scored = sem("scored")
                neg_ready, s_ready, rden_ready = sem("neg_ready"), sem("s_ready"), sem("rden_ready")
                max_ready = sem("max_ready")
                exp_ready = sem("exp_ready")
                probs_ready = sem("probs_ready")
                p_transposed = sem("p_transposed")
                pT_ready = sem("pT_ready")
                head_out = sem("head_out")
                head_done = sem("head_done")
                SCALE = DH ** -0.5
                NB4 = S2 // 512
                with nc.Block() as block:
                    @block.sync
                    def _(sp):
                        if masked:
                            with sp.Fori(0, B) as b:
                                sp.wait_ge(head_done, b * H + 1)
                                sp.dma_start(mask_i[:], A["mask_BxSxS2_ik1"][bass.ds(b, 1)].rearrange(
                                    "a q k -> q (a k)")).then_inc(sides_loaded, 16)
                                sp.dma_start(gp[:], A["fside_BxSxS2_0"][bass.ds(b, 1)].rearrange(
                                    "a q k -> q (a k)")).then_inc(sides_loaded, 16)

                    @block.vector
                    def _(dve):
                        dve.sem_inc(head_done, 1)
                        with dve.Fori(0, B) as b:
                            if masked:
                                dve.wait_ge(sides_loaded, 32 * b + 32)
                                nc.vector.tensor_scalar(neg[:], mask_i[:], -1.0, 1.0e9, ALU.add,
                                                        ALU.mult).then_inc(neg_ready, 1)
                            with dve.Fori(0, H) as h:
                                n = b * H + h
                                nc.vector.tensor_scalar(qz[:], qT[:, bass.ds(b * P, P)],
                                                        head_rows[:, bass.ds(h, 1)], None,
                                                        ALU.mult).then_inc(q_head_ready, 1)
                                dve.wait_ge(scored, n + 1)
                                if masked:
                                    dve.wait_ge(neg_ready, b + 1)
                                for j in range(NB4):
                                    cols = slice(j * 512, (j + 1) * 512)
                                    if masked:
                                        last = nc.vector.scalar_tensor_tensor(
                                            out=s[:, cols], in0=bank[j][:], scalar=SCALE, in1=neg[:, cols],
                                            op0=ALU.mult, op1=ALU.add)
                                    else:
                                        last = nc.vector.tensor_scalar(s[:, cols], bank[j][:], SCALE, None, ALU.mult)
                                last.then_inc(s_ready, 1)
                                dve.wait_ge(s_ready, n + 1)
                                nc.vector.tensor_reduce(nmax[:], s[:], AX_X, ALU.max, negate=True).then_inc(max_ready, 1)
                                dve.wait_ge(exp_ready, n + 1)
                                nc.vector.reciprocal(rden[:], den[:]).then_inc(rden_ready, 1)
                                if masked:
                                    nc.vector.tensor_tensor(s[:], s[:], gp[:], ALU.mult).then_inc(probs_ready, 1)
                                dve.wait_ge(head_out, n + 1)
                                dve.wait_ge(rden_ready, n + 1)
                                nc.vector.tensor_scalar(o[:, bass.ds(b, 1), bass.ds(h * DH, DH)],
                                                        bank[6][:, bass.ds(h * DH, DH)], rden[:], None,
                                                        ALU.mult).then_inc(head_done, 1)

                    @block.tensor
                    def _(pe):
                        with pe.Fori(0, B) as b:
                            with pe.Fori(0, H) as h:
                                n = b * H + h
                                pe.wait_ge(q_head_ready, n + 1)
                                for j in range(NB4):
                                    last = nc.tensor.matmul(bank[j][:], qz[:], kT[:, bass.ds(b * S2 + j * 512, 512)],
                                                            start=True, stop=True)
                                last.then_inc(scored, 1)
                                pe.wait_ge(probs_ready if masked else exp_ready, n + 1)
                                for g in range(NB4):
                                    pe.wait_ge(pT_ready, NB4 * n + g + 1)
                                    for c in range(4):
                                        ch = 4 * g + c
                                        last = nc.tensor.transpose(bank[4 + g % 2][:, c * P:(c + 1) * P],
                                                                   s[:, ch * P:(ch + 1) * P], ident[:])
                                    last.then_inc(p_transposed, 1)
                                pe.wait_ge(pT_ready, NB4 * n + NB4 + 1)
                                pe.wait_ge(head_done, n + 1)
                                for c in range(NCH):
                                    last = nc.tensor.matmul(bank[6][:, 0:D], pT[:, c, :],
                                                            v[:, bass.ds(b * NCH + c, 1), :].rearrange("p a d -> p (a d)"),
                                                            start=(c == 0), stop=(c == NCH - 1))
                                last.then_inc(head_out, 1)

                    @block.scalar
                    def _(act):
                        act.sem_inc(pT_ready, 1)
                        with act.Fori(0, B) as b:
                            with act.Fori(0, H) as h:
                                n = b * H + h
                                act.wait_ge(max_ready, n + 1)
                                nc.scalar.activation(s[:], s[:], ACT.Exp, bias=nmax[:],
                                                     accum_out=den[:]).then_inc(exp_ready, 1)
                                for g in range(NB4):
                                    act.wait_ge(p_transposed, NB4 * n + g + 1)
                                    nc.scalar.activation(pT[:, 4 * g:4 * g + 4, :], bank[4 + g % 2][:].rearrange(
                                        "p (c q) -> p c q", c=4), ACT.Copy).then_inc(pT_ready, 1)

                oT = sb("oT", [P, BT])
                o_transposed, oT_ready = sem("o_transposed"), sem("oT_ready")
                projected, xsteps = sem("projected"), sem("xsteps")
                with nc.Block() as block:
                    @block.tensor
                    def _(pe):
                        if masked:
                            for b in range(B):
                                last = nc.tensor.transpose(bank[0][:, b * P:(b + 1) * P], o[:, b, :], ident[:])
                            last.then_inc(o_transposed, 1)
                            pe.wait_ge(oT_ready, 1)
                            for b in range(B):
                                last = nc.tensor.matmul(bank[1][:, b * D:(b + 1) * D], oT[:, b * P:(b + 1) * P], wo[:],
                                                        start=True, stop=True)
                            last.then_inc(projected, 1)

                    @block.scalar
                    def _(act):
                        if masked:
                            act.wait_ge(o_transposed, 1)
                            nc.scalar.activation(oT[:], bank[0][:], ACT.Copy).then_inc(oT_ready, 1)

                    @block.vector
                    def _(dve):
                        chain = Chain(dve, xsteps)
                        if masked:
                            chain(nc.vector.tensor_tensor(x[:], x[:], bcast(bo[:], 1, B), ALU.add))
                            dve.wait_ge(projected, 1)
                            chain(nc.vector.tensor_tensor(x[:], x[:], bank[1][:].rearrange("p (b d) -> p b d", b=B),
                                                          ALU.add))
                        else:
                            chain(nc.vector.tensor_tensor(x[:], x[:], o[:], ALU.add))


        def small_sems(c2, name, *names):
            return [ctx.enter_context(nc.semaphore(f"{name}_{n}")) for n in names]

        def retention(name, w):
            with ExitStack() as c2:
                def sb(n, shape, dt=F32):
                    return c2.enter_context(nc.sbuf_tensor(f"{name}_{n}", shape, dt))

                def sem(n):
                    return ctx.enter_context(nc.semaphore(f"{name}_{n}"))

                NZ = HA + HA * LV
                wq, wk, wv = (sb(n, [P, HA, D]) for n in ("wq", "wk", "wv"))
                wo = sb("wo", [P, HA * P])
                wz = sb("wz", [NZ, D])
                z_bias = sb("z_bias", [P, NZ])
                ln_g, ln_b = sb("ln_g", [P, D]), sb("ln_b", [P, D])
                wqk = sb("wqk", [P, HA, D])
                woT = sb("woT", [P, HA, D])
                wvo = sb("wvo", [P, HA * D])
                wzT = sb("wzT", [P, NZ])
                w_loaded = sem("w_loaded")
                qk_merged, wo_transposed, woT_ready, vo_merged = (
                    sem(n) for n in ("qk_merged", "wo_transposed", "woT_ready", "vo_merged"))
                folded = sem("folded")

                with nc.Block() as block:
                    @block.sync
                    def _(sp):
                        for dst, src in ((wq, w["wq"]), (wk, w["wk"]), (wv, w["wv"])):
                            sp.dma_start(dst[:], src.rearrange("(h s) d -> s h d", h=HA)).then_inc(w_loaded, 16)
                        sp.dma_start(wo[:], w["wo"]).then_inc(w_loaded, 16)
                        sp.dma_start(wz[0:HA, :], w["wg"]).then_inc(w_loaded, 16)
                        sp.dma_start(wz[HA:NZ, :], w["wdl"]).then_inc(w_loaded, 16)
                        sp.dma_start(z_bias[:, 0:HA], w["bg"].partition_broadcast(P)).then_inc(w_loaded, 16)
                        sp.dma_start(z_bias[:, HA:NZ], w["lparam"].rearrange("h l -> (h l)").partition_broadcast(P)
                                     ).then_inc(w_loaded, 16)
                        sp.dma_start(ln_g[:], w["ln_g"].partition_broadcast(P)).then_inc(w_loaded, 16)
                        sp.dma_start(ln_b[:], w["ln_b"].partition_broadcast(P)).then_inc(w_loaded, 16)

                    @block.tensor
                    def _(pe):
                        pe.wait_ge(w_loaded, 160)
                        for h in range(HA):
                            last = nc.tensor.matmul(bank[h // 4][:, h % 4 * P:h % 4 * P + P], wq[:, h, :], wk[:, h, :],
                                                    start=True, stop=True)
                        last.then_inc(qk_merged, 1)
                        for h in range(HA):
                            nc.tensor.transpose(bank[2 + h // 4][:, h % 4 * P:h % 4 * P + P],
                                                wo[:, h * P:(h + 1) * P], ident[:])
                        nc.tensor.transpose(bank[6][:, 0:NZ], wz[:, :], ident[0:NZ, 0:NZ]).then_inc(wo_transposed, 1)
                        pe.wait_ge(woT_ready, 2)
                        for h in range(HA):
                            last = nc.tensor.matmul(bank[4 + h // 4][:, h % 4 * P:h % 4 * P + P], wv[:, h, :],
                                                    woT[:, h, :], start=True, stop=True)
                        last.then_inc(vo_merged, 1)

                    @block.scalar
                    def _(act):
                        act.wait_ge(qk_merged, 1)
                        for g in range(2):
                            nc.scalar.activation(wqk[:, 4 * g:4 * g + 4, :], bank[g][:].rearrange(
                                "p (h d) -> p h d", h=4), ACT.Copy).then_inc(folded, 1)
                        act.wait_ge(vo_merged, 1)
                        for g in range(2):
                            nc.scalar.activation(wvo[:, g * 512:(g + 1) * 512], bank[4 + g][:],
                                                 ACT.Copy).then_inc(folded, 1)

                    @block.vector
                    def _(dve):
                        dve.wait_ge(wo_transposed, 1)
                        for g in range(2):
                            nc.vector.tensor_copy(woT[:, 4 * g:4 * g + 4, :], bank[2 + g][:].rearrange(
                                "p (h d) -> p h d", h=4)).then_inc(woT_ready, 1)
                        nc.vector.tensor_copy(wzT[:], bank[6][:, 0:NZ]).then_inc(folded, 1)

                z = sb("z", [P, B, NZ])
                z_abs = sb("z_abs", [P, B, NZ])
                z_exp = sb("z_exp", [P, B, NZ])
                sp_z = sb("softplus", [P, B, NZ])
                xqk = sb("xqk", [P, HA, BT])
                xvo = sb("xvo", [P, B, HA * D])
                decay = sb("decay", [P, B, HA, T])
                lam = sb("lam", [P, B, HA, T])
                lamw = sb("lamw", [P, B, HA, T])
                att = sb("att", [P, B, HA, T])
                attT = sb("attT", [P, B, HA, T])
                y = sb("y", [P, B, D])
                scratch = nc.dram_tensor(f"{name}_lam_scratch", [B, T * HA * T], F32)
                z_projected, z_ready, abs_ready, exp_ready, ln_ready, gates_ready = (
                    sem(n) for n in ("z_projected", "z_ready", "abs_ready", "exp_ready", "ln_ready", "gates_ready"))
                xqk_projected, xqk_ready, xvo_projected, xvo_ready = (
                    sem(n) for n in ("xqk_projected", "xqk_ready", "xvo_projected", "xvo_ready"))
                decay_summed, decay_ready, lam_ready, lam_stored, lamw_ready = (
                    sem(n) for n in ("decay_summed", "decay_ready", "lam_ready", "lam_stored", "lamw_ready"))
                dl_ready, scored, att_ready, att_transposed, attT_ready, summed = (
                    sem(n) for n in ("dl_ready", "scored", "att_ready", "att_transposed", "attT_ready", "summed"))
                y_steps, y_var_ready, y_rstd_ready = sem("y_steps"), sem("y_var_ready"), sem("y_rstd_ready")
                HALVES = [(b, g) for b in range(B) for g in range(2)]
                SCALE = P ** -0.5

                with nc.Block() as block:
                    @block.tensor
                    def _(pe):
                        for b in range(B):
                            last = nc.tensor.matmul(bank[7][:, b * NZ:(b + 1) * NZ], xT[:, b * P:(b + 1) * P], wzT[:],
                                                    start=True, stop=True)
                        last.then_inc(z_projected, 1)
                        for h in range(HA):
                            if h >= 2:
                                pe.wait_ge(xqk_ready, h - 1)
                            nc.tensor.matmul(bank[h % 2][:], wqk[:, h, :], xT[:], start=True,
                                             stop=True).then_inc(xqk_projected, 1)
                        pe.wait_ge(gates_ready, 1)
                        for i, (b, g) in enumerate(HALVES):
                            if i >= 2:
                                pe.wait_ge(decay_ready, i - 1)
                            ps = bank[2 + i % 2]
                            nc.tensor.matmul(ps[:], ident_bf[:], bcast(future_bf[:], 1, 4), start=True, stop=False,
                                             skip_group_check=True)
                            for j in range(4):
                                h = 4 * g + j
                                nc.tensor.matmul(ps[:, j * P:(j + 1) * P], repeat(sp_z[:, b, h:h + 1], P),
                                                 upper[:], start=False, stop=False, skip_group_check=True)
                            nc.tensor.matmul(ps[:], neg_upper[:], bcast(sp_z[:, b, 4 * g:4 * g + 4], 2, P),
                                             start=False, stop=True, skip_group_check=True).then_inc(decay_summed, 1)
                        pe.wait_ge(xqk_ready, HA)
                        for i, (b, g) in enumerate(HALVES):
                            if i >= 2:
                                pe.wait_ge(xvo_ready, i - 1)
                            nc.tensor.matmul(bank[i % 2][:], xT[:, b * P:(b + 1) * P], wvo[:, g * 512:(g + 1) * 512],
                                             start=True, stop=True).then_inc(xvo_projected, 1)
                        for i, (b, g) in enumerate(HALVES):
                            if i >= 2:
                                pe.wait_ge(att_ready, i - 1)
                            for j in range(4):
                                h = 4 * g + j
                                last = nc.tensor.matmul(bank[4 + i % 2][:, j * P:(j + 1) * P],
                                                        xqk[:, h, b * P:(b + 1) * P], xT[:, b * P:(b + 1) * P],
                                                        start=True, stop=True)
                            last.then_inc(scored, 1)
                        pe.wait_ge(decay_ready, 8)
                        for i, (b, g) in enumerate(HALVES):
                            pe.wait_ge(att_ready, i + 1)
                            if i >= 2:
                                pe.wait_ge(attT_ready, i - 1)
                            for j in range(4):
                                last = nc.tensor.transpose(bank[2 + i % 2][:, j * P:(j + 1) * P],
                                                           att[:, b, 4 * g + j, :], ident[:])
                            last.then_inc(att_transposed, 1)
                        pe.wait_ge(xvo_ready, 8)
                        for i, (b, g) in enumerate(HALVES):
                            pe.wait_ge(attT_ready, i + 1)
                            for j in range(4):
                                h = 4 * g + j
                                last = nc.tensor.matmul(bank[6][:, b * D:(b + 1) * D], attT[:, b, h, :],
                                                        xvo[:, b, h * D:(h + 1) * D], start=(h == 0), stop=(h == HA - 1))
                        last.then_inc(summed, 1)

                    @block.scalar
                    def _(act):
                        act.wait_ge(z_ready, 1)
                        nc.scalar.activation(z_abs[:], z[:], ACT.Abs).then_inc(abs_ready, 1)
                        act.wait_ge(abs_ready, 1)
                        nc.scalar.activation(z_exp[:], z_abs[:], ACT.Exp, scale=-1.0).then_inc(exp_ready, 1)
                        act.wait_ge(exp_ready, 1)
                        nc.scalar.activation(z_exp[:], z_exp[:], ACT.Ln, bias=1.0).then_inc(ln_ready, 1)
                        for h in range(HA):
                            act.wait_ge(xqk_projected, h + 1)
                            nc.scalar.activation(xqk[:, h, :], bank[h % 2][:], ACT.Copy).then_inc(xqk_ready, 1)
                        for i, (b, g) in enumerate(HALVES):
                            act.wait_ge(decay_summed, i + 1)
                            nc.scalar.activation(decay[:, b, 4 * g:4 * g + 4, :], bank[2 + i % 2][:].rearrange(
                                "p (h s) -> p h s", h=4), ACT.Exp).then_inc(decay_ready, 1)
                        for i, (b, g) in enumerate(HALVES):
                            act.wait_ge(xvo_projected, i + 1)
                            nc.scalar.activation(xvo[:, b, g * 512:(g + 1) * 512], bank[i % 2][:],
                                                 ACT.Copy).then_inc(xvo_ready, 1)
                        for i, (b, g) in enumerate(HALVES):
                            act.wait_ge(att_transposed, i + 1)
                            nc.scalar.activation(attT[:, b, 4 * g:4 * g + 4, :], bank[2 + i % 2][:].rearrange(
                                "p (h s) -> p h s", h=4), ACT.Copy).then_inc(attT_ready, 1)

                    @block.sync
                    def _(sp):
                        for b in range(B):
                            sp.wait_ge(lam_ready, LVU)
                            sp.dma_start(scratch[b].rearrange("(t c) -> t c", t=T),
                                         lam[:, b, :, :].rearrange("p h c -> p (h c)")).then_inc(lam_stored, 16)
                        for b in range(B):
                            sp.wait_ge(lam_stored, 16 * B)
                            skewed = bass.AP(scratch, b * T * HA * T + T - 1,
                                             [(HA * T - 1, T), (T, HA), (1, T)])
                            sp.dma_start(lamw[:, b, :, :], skewed).then_inc(lamw_ready, 16)

                    @block.vector
                    def _(dve):
                        dve.wait_ge(z_projected, 1)
                        nc.vector.tensor_tensor(z[:], bank[7][:, 0:B * NZ].rearrange("p (b n) -> p b n", b=B),
                                                bcast(z_bias[:], 1, B), ALU.add).then_inc(z_ready, 1)
                        dve.wait_ge(ln_ready, 1)
                        nc.vector.scalar_tensor_tensor(out=sp_z[:], in0=z[:], scalar=0.0, in1=z_exp[:], op0=ALU.max,
                                                       op1=ALU.add).then_inc(gates_ready, 1)
                        dve.wait_ge(gates_ready, 1)
                        lvs = sp_z[:, :, HA:NZ].rearrange("p b (h l) -> p b h l", h=HA)
                        for l in range(LVU):
                            d0, d1 = (0, 1) if l == 0 else (2 ** (l - 1), 2 ** l)
                            nc.vector.tensor_copy(lam[:, :, :, T - d1:T - d0],
                                                  bcast(lvs[:, :, :, l], 3, d1 - d0)).then_inc(lam_ready, 1)
                        for b in range(B):
                            dve.wait_ge(decay_ready, 2 * b + 2)
                            dve.wait_ge(lamw_ready, 16 * B)
                            nc.vector.tensor_tensor(lamw[:, b, :, :], lamw[:, b, :, :], decay[:, b, :, :],
                                                    ALU.mult).then_inc(dl_ready, 1)
                        for i, (b, g) in enumerate(HALVES):
                            dve.wait_ge(scored, i + 1)
                            dve.wait_ge(dl_ready, b + 1)
                            hs = slice(4 * g, 4 * g + 4)
                            nc.vector.scalar_tensor_tensor(
                                out=att[:, b, hs, :], in0=bank[4 + i % 2][:].rearrange("p (h s) -> p h s", h=4),
                                scalar=SCALE, in1=lamw[:, b, hs, :], op0=ALU.mult, op1=ALU.mult).then_inc(att_ready, 1)
                        dve.wait_ge(summed, 1)
                        chain = Chain(dve, y_steps)
                        chain(nc.vector.tensor_tensor(y[:], bank[6][:].rearrange("p (b d) -> p b d", b=B), xn[:],
                                                      ALU.add))
                        for b in range(B):
                            nc.vector.bn_stats(bn[:, b, :], y[:, b, :]).then_inc(y_steps, 1)
                        dve.wait_ge(y_steps, 1 + B)
                        for b in range(B):
                            nc.vector.bn_aggr(mv[:, b, :], bn[:, b, :]).then_inc(y_steps, 1)
                        dve.wait_ge(y_steps, 1 + 2 * B)
                        nc.vector.tensor_scalar(var_eps[:], mv[:, :, 1], EPS, None, ALU.add).then_inc(y_var_ready, 1)
                        dve.wait_ge(y_rstd_ready, 1)
                        for b in range(B):
                            nc.vector.tensor_scalar(y[:, b, :], y[:, b, :], mv[:, b, 0:1], rstd[:, b:b + 1],
                                                    ALU.subtract, ALU.mult).then_inc(y_steps, 1)
                        chain.at = 1 + 3 * B
                        dve.wait_ge(y_steps, chain.at)
                        chain(nc.vector.tensor_tensor(y[:], y[:], bcast(ln_g[:], 1, B), ALU.mult))
                        chain(nc.vector.tensor_tensor(y[:], y[:], bcast(ln_b[:], 1, B), ALU.add))
                        chain(nc.vector.tensor_tensor(x[:], x[:], y[:], ALU.add))

                    @block.gpsimd
                    def _(pool):
                        pool.wait_ge(y_var_ready, 1)
                        nc.gpsimd.tensor_tensor(rstd[:], var_eps[:], minus_half[:], ALU.pow).then_inc(y_rstd_ready, 1)

        def expert_sum(name, up1, up2, down, bias1, bias2, gates, b_down, loaded):
            with ExitStack() as c2:
                act1 = c2.enter_context(nc.sbuf_tensor(f"{name}_act1", [P, 3, BT], F32))
                hid = c2.enter_context(nc.sbuf_tensor(f"{name}_hid", [P, 3, BT], F32))
                up_summed, silu_ready, hid_ready, down_summed, added = small_sems(
                    c2, name, "up_summed", "silu_ready", "hid_ready", "down_summed", "added")
                b_down_summed, = small_sems(c2, name, "b_down_summed")
                U = HM * E
                first = 1 if b_down else 0
                with nc.Block() as block:
                    @block.tensor
                    def _(pe):
                        def up(u):
                            e, m = divmod(u, HM)
                            if u >= 3:
                                pe.wait_ge(hid_ready, u - 2)
                            nc.tensor.matmul(bank[2 * (u % 3)][:], up1(e, m), xT[:], start=True, stop=True)
                            nc.tensor.matmul(bank[2 * (u % 3) + 1][:], up2(e, m), xT[:], start=True,
                                             stop=True).then_inc(up_summed, 1)

                        def down_(u):
                            e, m = divmod(u, HM)
                            pe.wait_ge(hid_ready, u + 1)
                            if m == 0 and e + first >= 2:
                                pe.wait_ge(added, e + first - 1)
                            for b in range(B):
                                last = nc.tensor.matmul(bank[6 + (e + first) % 2][:, b * D:(b + 1) * D],
                                                        hid[:, u % 3, b * P:(b + 1) * P], down(e, m),
                                                        start=(m == 0 and b == 0), stop=(m == HM - 1 and b == B - 1),
                                                        skip_group_check=True)
                            if m == HM - 1:
                                last.then_inc(down_summed, 1)

                        up(0)
                        if b_down:
                            gT, rows = b_down
                            for b in range(B):
                                last = nc.tensor.matmul(bank[6][:, b * D:(b + 1) * D], gT[:, b * P:(b + 1) * P], rows[:],
                                                        start=(b == 0), stop=(b == B - 1), skip_group_check=True)
                            last.then_inc(b_down_summed, 1)
                        up(1)
                        for u in range(2, U + 2):
                            if u < U:
                                up(u)
                            down_(u - 2)

                    @block.scalar
                    def _(act):
                        for u in range(U):
                            e, m = divmod(u, HM)
                            act.wait_ge(up_summed, u + 1)
                            if u >= 3:
                                act.wait_ge(hid_ready, u - 2)
                            nc.scalar.activation(act1[:, u % 3, :], bank[2 * (u % 3)][:], ACT.Silu,
                                                 bias=bias1(e, m) if bias1 else 0.0).then_inc(silu_ready, 1)

                    @block.vector
                    def _(dve):
                        def add(e):
                            dve.wait_ge(down_summed, e + 1)
                            if e + first >= 1:
                                dve.wait_ge(added, e + first)
                            for b in range(B):
                                last = nc.vector.scalar_tensor_tensor(
                                    out=x[:, b, :], in0=bank[6 + (e + first) % 2][:, b * D:(b + 1) * D],
                                    scalar=gates(b, e), in1=x[:, b, :], op0=ALU.mult, op1=ALU.add)
                            last.then_inc(added, 1)

                        if b_down:
                            dve.wait_ge(b_down_summed, 1)
                            nc.vector.tensor_tensor(x[:], bank[6][:].rearrange("p (b d) -> p b d", b=B), x[:],
                                                    ALU.add).then_inc(added, 1)
                        for u in range(U):
                            e, m = divmod(u, HM)
                            dve.wait_ge(silu_ready, u + 1)
                            if u >= 3:
                                if (u - 3) % HM == HM - 1:
                                    dve.wait_ge(down_summed, (u - 3) // HM + 1)
                                else:
                                    dve.wait_ge(up_summed, min(u + 1, U))
                            if bias2:
                                nc.vector.scalar_tensor_tensor(
                                    out=hid[:, u % 3, :], in0=bank[2 * (u % 3) + 1][:], scalar=bias2(e, m),
                                    in1=act1[:, u % 3, :], op0=ALU.add, op1=ALU.mult).then_inc(hid_ready, 1)
                            else:
                                nc.vector.tensor_tensor(hid[:, u % 3, :], bank[2 * (u % 3) + 1][:], act1[:, u % 3, :],
                                                        ALU.mult).then_inc(hid_ready, 1)
                            if m == HM - 1 and e >= 1:
                                add(e - 1)
                        add(E - 1)

        def lora_ffn(name, w):
            with ExitStack() as c2:
                def sb(n, shape, dt=F32):
                    return c2.enter_context(nc.sbuf_tensor(f"{name}_{n}", shape, dt))

                def sem(n):
                    return ctx.enter_context(nc.semaphore(f"{name}_{n}"))

                EM = E * HM
                up_rows = [sb("w1", [P, EM, D]), sb("w3", [P, EM, D])]
                up_a = [sb("a1", [R, E, D]), sb("a3", [R, E, D])]
                up_b = [sb("b1l", [P, EM, R]), sb("b3l", [P, EM, R])]
                down_rows = sb("w2", [P, E, HID])
                down_a, down_b = sb("a2", [R, E, HID]), sb("b2l", [P, E, R])
                bias_rows = sb("bias_rows", [2 * EM, P])
                b_down = sb("b_down", [E, D])
                wg = sb("wg", [E, D])
                upT = [sb("w1T", [P, EM, P]), sb("w3T", [P, EM, P])]
                downT = sb("w2T", [P, EM, D])
                up_bT = [sb("b1T", [R, EM, P]), sb("b3T", [R, EM, P])]
                down_bT = sb("b2T", [R, E, P])
                biases = sb("biases", [P, 2 * EM])
                wgT = sb("wgT", [P, E])
                w_loaded = sem("w_loaded")
                turned, turned_out, folded, folded_out = (
                    sem(n) for n in ("turned", "turned_out", "folded", "folded_out"))

                with nc.Block() as block:
                    @block.sync
                    def _(sp):
                        n = 0
                        for k, (ww, aa, bb) in enumerate((("w1", "a1", "b1l"), ("w3", "a3", "b3l"))):
                            sp.dma_start(up_rows[k][:], w[ww].rearrange("e (m p) d -> p (e m) d", p=P)).then_inc(w_loaded, 16)
                            sp.dma_start(up_a[k][:], w[aa].rearrange("e r d -> r e d")).then_inc(w_loaded, 16)
                            sp.dma_start(up_b[k][:], w[bb].rearrange("e (m p) r -> p (e m) r", p=P)).then_inc(w_loaded, 16)
                        sp.dma_start(down_rows[:], w["w2"].rearrange("e d h -> d e h")).then_inc(w_loaded, 16)
                        sp.dma_start(down_a[:], w["a2"].rearrange("e r h -> r e h")).then_inc(w_loaded, 16)
                        sp.dma_start(down_b[:], w["b2l"].rearrange("e d r -> d e r")).then_inc(w_loaded, 16)
                        sp.dma_start(bias_rows[0:EM, :], w["b1"].rearrange("e (m p) -> (e m) p", p=P)).then_inc(w_loaded, 16)
                        sp.dma_start(bias_rows[EM:2 * EM, :], w["b3"].rearrange("e (m p) -> (e m) p", p=P)).then_inc(w_loaded, 16)
                        sp.dma_start(b_down[:], w["b2"]).then_inc(w_loaded, 16)
                        sp.dma_start(wg[:], w["wg"]).then_inc(w_loaded, 16)

                    turns = [(up_b[k][:, i, :], up_bT[k][:, i, :]) for k in range(2) for i in range(EM)]
                    turns += [(down_b[:, e, :], down_bT[:, e, :]) for e in range(E)]
                    folds = [(up_rows[k][:, i, :], up_a[k][:, i // HM, :], up_bT[k][:, i, :], False)
                             for k in range(2) for i in range(EM)]
                    folds += [(down_rows[:, i // HM, i % HM * P:(i % HM + 1) * P],
                               down_a[:, i // HM, i % HM * P:(i % HM + 1) * P], down_bT[:, i // HM, :], True)
                              for i in range(EM)]
                    TG, FG = len(turns) // 4, len(folds) // 4

                    @block.tensor
                    def _(pe):
                        pe.wait_ge(w_loaded, 16 * 13)
                        nc.tensor.transpose(bank[6][:, 0:2 * EM], bias_rows[:, :], ident[0:2 * EM, 0:2 * EM])
                        nc.tensor.transpose(bank[6][:, 2 * EM:2 * EM + E], wg[:, :],
                                            ident[0:E, 0:E]).then_inc(turned, 1)
                        for g in range(TG):
                            if g >= 2:
                                pe.wait_ge(turned_out, g)
                            for j in range(4):
                                last = nc.tensor.transpose(bank[g % 2][0:R, j * P:(j + 1) * P], turns[4 * g + j][0],
                                                           ident[:])
                            last.then_inc(turned, 1)
                        pe.wait_ge(turned_out, TG + 1)
                        for g in range(FG):
                            if g >= 2:
                                pe.wait_ge(folded_out, g - 1)
                            for j in range(4):
                                rows, a, bT, _ = folds[4 * g + j]
                                ps = bank[2 + g % 2][:, j * P:(j + 1) * P]
                                nc.tensor.matmul(ps, rows, ident[:], start=True, stop=False)
                                last = nc.tensor.matmul(ps, a, bT, start=False, stop=True)
                            last.then_inc(folded, 1)

                    @block.scalar
                    def _(act):
                        for g in range(FG):
                            act.wait_ge(folded, g + 1)
                            k, i = divmod(4 * g, EM)
                            dst = (upT[0], upT[1], downT)[k]
                            nc.scalar.activation(dst[:, i:i + 4, :], bank[2 + g % 2][:].rearrange(
                                "p (i h) -> p i h", i=4), ACT.Copy).then_inc(folded_out, 1)

                    @block.vector
                    def _(dve):
                        dve.wait_ge(turned, 1)
                        nc.vector.tensor_copy(biases[:], bank[6][:, 0:2 * EM])
                        nc.vector.tensor_copy(wgT[:], bank[6][:, 2 * EM:2 * EM + E]).then_inc(turned_out, 1)
                        for g in range(TG):
                            dve.wait_ge(turned, g + 2)
                            k, i = divmod(4 * g, EM)
                            dst = (up_bT[0], up_bT[1], down_bT)[k]
                            nc.vector.tensor_copy(dst[:, i:i + 4, :], bank[g % 2][0:R, :].rearrange(
                                "p (i h) -> p i h", i=4)).then_inc(turned_out, 1)

                logits = sb("logits", [P, B, E])
                nmax, den = sb("nmax", [P, B]), sb("den", [P, B])
                top = sb("top", [P, B, 8])
                at = sb("at", [P, B, 8], U32)
                atf = sb("atf", [P, B, 8])
                wsum = sb("wsum", [P, B])
                hot = sb("hot", [P, B, E])
                gates = sb("gates", [P, B, E])
                numbers = sb("numbers", [P, E])
                gatesT = sb("gatesT", [E, BT])
                routed, gsteps, lmax_ready, lexp_ready, gates_ready, gates_turned = (
                    sem(n) for n in ("routed", "gsteps", "lmax_ready", "lexp_ready", "gates_ready", "gates_turned"))
                numbers_ready = sem("numbers_ready")
                with nc.Block() as block:
                    @block.gpsimd
                    def _(pool):
                        nc.gpsimd.iota(numbers[:], pattern=[[1, E]], base=0, channel_multiplier=0,
                                       allow_small_or_imprecise_dtypes=True).then_inc(numbers_ready, 1)

                    @block.tensor
                    def _(pe):
                        for b in range(B):
                            last = nc.tensor.matmul(bank[0][:, b * E:(b + 1) * E], xT[:, b * P:(b + 1) * P], wgT[:],
                                                    start=True, stop=True)
                        last.then_inc(routed, 1)
                        pe.wait_ge(gates_ready, 1)
                        for b in range(B):
                            last = nc.tensor.transpose(bank[1][0:E, b * P:(b + 1) * P], gates[:, b, :], ident[:])
                        last.then_inc(gates_turned, 1)

                    @block.scalar
                    def _(act):
                        for b in range(B):
                            act.wait_ge(lmax_ready, 1)
                            nc.scalar.activation(logits[:, b, :], bank[0][:, b * E:(b + 1) * E], ACT.Exp,
                                                 bias=nmax[:, b:b + 1], accum_out=den[:, b:b + 1]).then_inc(lexp_ready, 1)

                    @block.vector
                    def _(dve):
                        dve.wait_ge(routed, 1)
                        nc.vector.tensor_reduce(nmax[:], bank[0][:, 0:B * E].rearrange("p (b e) -> p b e", b=B), AX_X,
                                                ALU.max, negate=True).then_inc(lmax_ready, 1)
                        dve.wait_ge(lexp_ready, B)
                        dve.wait_ge(numbers_ready, 1)
                        chain = Chain(dve, gsteps)
                        chain(nc.vector.reciprocal(den[:], den[:]))
                        chain(nc.vector.tensor_tensor(logits[:], logits[:], bcast(den[:], 2, E), ALU.mult))
                        for b in range(B):
                            chain(nc.vector.max(top[:, b, :], logits[:, b, :]))
                            chain(nc.vector.max_index(at[:, b, :], top[:, b, :], logits[:, b, :]))
                        chain(nc.vector.tensor_copy(atf[:], at[:]))
                        chain(nc.vector.tensor_tensor(wsum[:], top[:, :, 0], top[:, :, 1], ALU.add))
                        chain(nc.vector.reciprocal(wsum[:], wsum[:]))
                        chain(nc.vector.tensor_tensor(top[:], top[:], bcast(wsum[:], 2, 8), ALU.mult))
                        for k, dst in ((0, gates), (1, hot)):
                            chain(nc.vector.tensor_tensor(dst[:], bcast(numbers[:], 1, B), bcast(atf[:, :, k], 2, E),
                                                          ALU.is_equal))
                            chain(nc.vector.tensor_tensor(dst[:], dst[:], bcast(top[:, :, k], 2, E), ALU.mult))
                        nc.vector.tensor_tensor(gates[:], gates[:], hot[:], ALU.add).then_inc(gates_ready, 1)
                        dve.wait_ge(gates_turned, 1)
                        nc.vector.tensor_copy(gatesT[:], bank[1][0:E, :])

                expert_sum(name, lambda e, m: upT[0][:, HM * e + m, :], lambda e, m: upT[1][:, HM * e + m, :],
                           lambda e, m: downT[:, HM * e + m, :],
                           lambda e, m: biases[:, HM * e + m:HM * e + m + 1],
                           lambda e, m: biases[:, EM + HM * e + m:EM + HM * e + m + 1],
                           lambda b, e: gates[:, b, e:e + 1], (gatesT, b_down), None)

        def banded_attention(name, w):
            with ExitStack() as c2:
                def sb(n, shape, dt=F32):
                    return c2.enter_context(nc.sbuf_tensor(f"{name}_{n}", shape, dt))

                def sem(n):
                    return ctx.enter_context(nc.semaphore(f"{name}_{n}"))

                BAND = D // 4
                qkv_w = sb("qkv_w", [P, 3 * D])
                w_high = sb("w_high", [P, 3 * D])
                w_low = [sb("w_low1", [P, 3 * D], F16), sb("w_low2", [P, 3 * D], F16)]
                xT16 = sb("xT16", [P, BT], F16)
                out_w, out_wT, out_b = sb("out_w", [P, D]), sb("out_wT", [P, D]), sb("out_b", [P, D])
                part = [sb("part1", [P, BT], F16), sb("part2", [P, BT], F16)]
                qkv = [sb("qT", [P, BT]), sb("kT", [P, BT]), sb("v", [P, BT])]
                probs, pT, yT = sb("probs", [P, B, T]), sb("pT", [P, B, T]), sb("yT", [P, BT])
                nmax, den = sb("nmax", [P, B]), sb("den", [P, B])
                loaded, cleared, bands_ready, x16_ready, turned, out_wT_ready = (
                    sem(n) for n in ("loaded", "cleared", "bands_ready", "x16_ready", "turned", "out_wT_ready"))
                projected, part_ready, sum_ready, qkv_ready = (
                    sem(n) for n in ("projected", "part_ready", "sum_ready", "qkv_ready"))
                scored, max_ready, exp_ready, p_turned, pT_ready, mixed, yT_ready, done = (
                    sem(n) for n in ("scored", "max_ready", "exp_ready", "p_turned", "pT_ready", "mixed", "yT_ready",
                                     "done"))
                osteps = sem("osteps")
                SCALE = D ** -0.5
                with nc.Block() as block:
                    @block.sync
                    def _(sp):
                        sp.dma_start(qkv_w[:], w["qkv"]).then_inc(loaded, 16)
                        sp.dma_start(out_w[:], w["out_w"]).then_inc(loaded, 16)
                        sp.dma_start(out_b[:], w["out_b"].partition_broadcast(P)).then_inc(loaded, 16)

                    @block.gpsimd
                    def _(pool):
                        nc.gpsimd.memset(w_high[:], 0.0).then_inc(cleared, 1)
                        nc.gpsimd.memset(w_low[0][:], 0.0).then_inc(cleared, 1)
                        nc.gpsimd.memset(w_low[1][:], 0.0).then_inc(cleared, 1)

                    @block.vector
                    def _(dve):
                        dve.wait_ge(loaded, 48)
                        dve.wait_ge(cleared, 3)
                        nc.vector.tensor_copy(w_high[BAND:2 * BAND, :], qkv_w[BAND:2 * BAND, :]).then_inc(bands_ready, 1)
                        nc.vector.tensor_copy(w_high[2 * BAND:3 * BAND, :], qkv_w[2 * BAND:3 * BAND, :]).then_inc(bands_ready, 1)
                        nc.vector.tensor_copy(w_low[0][0:BAND, :], qkv_w[0:BAND, :]).then_inc(bands_ready, 1)
                        nc.vector.tensor_copy(w_low[1][3 * BAND:D, :], qkv_w[3 * BAND:D, :]).then_inc(bands_ready, 1)
                        nc.vector.tensor_copy(xT16[:], xT[:]).then_inc(x16_ready, 1)
                        dve.wait_ge(turned, 1)
                        nc.vector.tensor_copy(out_wT[:], bank[7][:, 0:D]).then_inc(out_wT_ready, 1)
                        for i in range(3):
                            dve.wait_ge(part_ready, 2 * i + 1)
                            nc.vector.tensor_tensor(qkv[i][:], bank[1 + 3 * (i % 2)][:], part[0][:], ALU.add).then_inc(sum_ready, 1)
                            dve.wait_ge(sum_ready, i + 1)
                            dve.wait_ge(part_ready, 2 * i + 2)
                            nc.vector.tensor_tensor(qkv[i][:], qkv[i][:], part[1][:], ALU.add).then_inc(qkv_ready, 1)
                        dve.wait_ge(scored, 1)
                        nc.vector.tensor_reduce(nmax[:], bank[6][:].rearrange("p (b k) -> p b k", b=B), AX_X, ALU.max,
                                                negate=True).then_inc(osteps, 1)
                        dve.wait_ge(osteps, 1)
                        nc.vector.tensor_scalar(nmax[:], nmax[:], SCALE, None, ALU.mult).then_inc(max_ready, 1)
                        dve.wait_ge(exp_ready, B)
                        nc.vector.reciprocal(den[:], den[:]).then_inc(osteps, 1)
                        nc.vector.tensor_tensor(x[:], x[:], bcast(out_b[:], 1, B), ALU.add).then_inc(osteps, 1)
                        dve.wait_ge(osteps, 3)
                        dve.wait_ge(done, 1)
                        for b in range(B):
                            nc.vector.scalar_tensor_tensor(out=x[:, b, :], in0=bank[3][:, b * D:(b + 1) * D],
                                                           scalar=den[:, b:b + 1], in1=x[:, b, :], op0=ALU.mult,
                                                           op1=ALU.add)

                    @block.tensor
                    def _(pe):
                        pe.wait_ge(loaded, 48)
                        nc.tensor.transpose(bank[7][:, 0:D], out_w[:], ident[:]).then_inc(turned, 1)
                        pe.wait_ge(bands_ready, 4)
                        pe.wait_ge(x16_ready, 1)
                        for i in range(3):
                            if i == 2:
                                pe.wait_ge(qkv_ready, 1)
                            for k, (ww, xx) in enumerate(((w_low[0], xT16), (w_high, xT), (w_low[1], xT16))):
                                ps = bank[k + 3 * (i % 2)]
                                if i < 2:
                                    last = nc.tensor.matmul(ps[:], ww[:, i * D:(i + 1) * D], xx[:], start=True, stop=True)
                                else:
                                    for b in range(B):
                                        last = nc.tensor.matmul(ps[:, b * D:(b + 1) * D], xx[:, b * P:(b + 1) * P],
                                                                ww[:, i * D:(i + 1) * D], start=True, stop=True)
                            last.then_inc(projected, 1)
                        pe.wait_ge(qkv_ready, 2)
                        for b in range(B):
                            cols = slice(b * P, (b + 1) * P)
                            last = nc.tensor.matmul(bank[6][:, cols], qkv[0][:, cols], qkv[1][:, cols], start=True, stop=True)
                        last.then_inc(scored, 1)
                        pe.wait_ge(exp_ready, B)
                        pe.wait_ge(out_wT_ready, 1)
                        for b in range(B):
                            last = nc.tensor.transpose(bank[7][:, b * P:(b + 1) * P], probs[:, b, :], ident[:])
                        last.then_inc(p_turned, 1)
                        pe.wait_ge(pT_ready, 1)
                        pe.wait_ge(qkv_ready, 3)
                        for b in range(B):
                            last = nc.tensor.matmul(bank[5][:, b * P:(b + 1) * P], qkv[2][:, b * D:(b + 1) * D], pT[:, b, :],
                                                    start=True, stop=True)
                        last.then_inc(mixed, 1)
                        pe.wait_ge(yT_ready, 1)
                        for b in range(B):
                            last = nc.tensor.matmul(bank[3][:, b * D:(b + 1) * D], yT[:, b * P:(b + 1) * P], out_wT[:],
                                                    start=True, stop=True)
                        last.then_inc(done, 1)

                    @block.scalar
                    def _(act):
                        for i in range(3):
                            act.wait_ge(projected, i + 1)
                            for k in range(2):
                                if i:
                                    act.wait_ge(qkv_ready, i)
                                nc.scalar.activation(part[k][:], bank[2 * k + 3 * (i % 2)][:], ACT.Copy).then_inc(part_ready, 1)
                        act.wait_ge(max_ready, 1)
                        for b in range(B):
                            nc.scalar.activation(probs[:, b, :], bank[6][:, b * P:(b + 1) * P], ACT.Exp, scale=SCALE,
                                                 bias=nmax[:, b:b + 1], accum_out=den[:, b:b + 1]).then_inc(exp_ready, 1)
                        act.wait_ge(p_turned, 1)
                        nc.scalar.activation(pT[:], bank[7][:].rearrange("p (b q) -> p b q", b=B), ACT.Copy).then_inc(pT_ready, 1)
                        act.wait_ge(mixed, 1)
                        nc.scalar.activation(yT[:], bank[5][:], ACT.Copy).then_inc(yT_ready, 1)

        def choice_ffn(name, w):
            with ExitStack() as c2:
                def sb(n, shape, dt=F32):
                    return c2.enter_context(nc.sbuf_tensor(f"{name}_{n}", shape, dt))

                def sem(n):
                    return ctx.enter_context(nc.semaphore(f"{name}_{n}"))

                up1, up2 = sb("wg", [P, E, HID]), sb("wu", [P, E, HID])
                down = sb("wd", [P, E * HM, D])
                gate_w = sb("gate_w", [P, E])
                aff, nmax, den = sb("aff", [P, B, E]), sb("nmax", [P, B]), sb("den", [P, B])
                loaded, routed, max_ready, exp_ready, steps = (
                    sem(n) for n in ("loaded", "routed", "max_ready", "exp_ready", "steps"))
                with nc.Block() as block:
                    @block.sync
                    def _(sp):
                        sp.dma_start(gate_w[:], w["gate_w"]).then_inc(loaded, 16)
                        sp.dma_start(up1[:], w["wg"].rearrange("e d i -> d e i")).then_inc(loaded, 16)
                        sp.dma_start(up2[:], w["wu"].rearrange("e d i -> d e i")).then_inc(loaded, 16)
                        sp.dma_start(down[:], w["wd"].rearrange("e (m p) d -> p (e m) d", p=P)).then_inc(loaded, 16)

                    @block.tensor
                    def _(pe):
                        pe.wait_ge(loaded, 64)
                        for b in range(B):
                            last = nc.tensor.matmul(bank[0][:, b * E:(b + 1) * E], xT[:, b * P:(b + 1) * P], gate_w[:],
                                                    start=True, stop=True)
                        last.then_inc(routed, 1)

                    @block.scalar
                    def _(act):
                        act.wait_ge(max_ready, 1)
                        for b in range(B):
                            nc.scalar.activation(aff[:, b, :], bank[0][:, b * E:(b + 1) * E], ACT.Exp,
                                                 bias=nmax[:, b:b + 1], accum_out=den[:, b:b + 1]).then_inc(exp_ready, 1)

                    @block.vector
                    def _(dve):
                        dve.wait_ge(routed, 1)
                        nc.vector.tensor_reduce(nmax[:], bank[0][:, 0:B * E].rearrange("p (b e) -> p b e", b=B), AX_X,
                                                ALU.max, negate=True).then_inc(max_ready, 1)
                        dve.wait_ge(exp_ready, B)
                        chain = Chain(dve, steps)
                        chain(nc.vector.reciprocal(den[:], den[:]))
                        chain(nc.vector.tensor_tensor(aff[:], aff[:], bcast(den[:], 2, E), ALU.mult))

                expert_sum(name, lambda e, m: up1[:, e, m * P:(m + 1) * P], lambda e, m: up2[:, e, m * P:(m + 1) * P],
                           lambda e, m: down[:, HM * e + m, :], None, None, lambda b, e: aff[:, b, e:e + 1], None, None)


        layer_norm(0)
        cross_attention("xa0", dict(wq=A["L0_xattn_wq_k"], bq=A["L0_xattn_wq_b"], wk=A["L0_xattn_wk_k"],
                                    bk=A["L0_xattn_wk_b"], wv=A["L0_xattn_wv_k"], bv=A["L0_xattn_wv_b"],
                                    wo=A["L0_xattn_wo_k"], bo=A["L0_xattn_wo_b"]), True)
        layer_norm(1)
        retention("ret", dict(wq=A["L0_attn_Wq"], wk=A["L0_attn_Wk"], wv=A["L0_attn_Wv"], wo=A["L0_attn_Wo"],
                              wg=A["L0_attn_Wg"], bg=A["L0_attn_bg"], wdl=A["L0_attn_Wdl"],
                              lparam=A["L0_attn_Lparam"], ln_g=A["L0_attn_ln_g"], ln_b=A["L0_attn_ln_b"]))
        layer_norm(2)
        lora_ffn("ffn0", dict(w1=A["L0_ffn_W1"], w2=A["L0_ffn_W2"], w3=A["L0_ffn_W3"], a1=A["L0_ffn_A1"],
                              a2=A["L0_ffn_A2"], a3=A["L0_ffn_A3"], b1l=A["L0_ffn_B1"], b2l=A["L0_ffn_B2"],
                              b3l=A["L0_ffn_B3"], b1=A["L0_ffn_b1"], b2=A["L0_ffn_b2"], b3=A["L0_ffn_b3"],
                              wg=A["L0_ffn_Wg"]))
        layer_norm(3)
        cross_attention("xa1", dict(wq=A["L1_xattn_Wq"], bq=A["L1_xattn_bq"], wk=A["L1_xattn_Wk"],
                                    bk=A["L1_xattn_bk"], wv=A["L1_xattn_Wv"], bv=A["L1_xattn_bv"]), False)
        layer_norm(4)
        banded_attention("att1", dict(qkv=A["L1_attn_weight_qkv"], out_w=A["L1_attn_out_w"],
                                      out_b=A["L1_attn_out_b"]))
        layer_norm(5)
        choice_ffn("ffn1", dict(gate_w=A["L1_ffn_gate_w"], wg=A["L1_ffn_Wg"], wu=A["L1_ffn_Wu"],
                                wd=A["L1_ffn_Wd"]))

        stored = sem("stored")
        with nc.Block() as block:
            @block.sync
            def _(sp):
                sp.dma_start(out.rearrange("b t d -> t b d"), x[:]).then_inc(stored, 16)
                sp.wait_ge(stored, 16)


_INS = [
    "x", "ctx_1024", "fside_BxSxS2_0", "mask_BxSxS2_ik1",
    "L0_xattn_wq_k", "L0_xattn_wq_b", "L0_xattn_wk_k", "L0_xattn_wk_b",
    "L0_xattn_wv_k", "L0_xattn_wv_b", "L0_xattn_wo_k", "L0_xattn_wo_b",
    "L0_attn_Wq", "L0_attn_Wk", "L0_attn_Wv", "L0_attn_Wg",
    "L0_attn_bg", "L0_attn_Wdl", "L0_attn_Lparam", "L0_attn_Wo",
    "L0_attn_ln_g", "L0_attn_ln_b", "L0_ffn_Wg", "L0_ffn_W1",
    "L0_ffn_b1", "L0_ffn_A1", "L0_ffn_B1", "L0_ffn_W2",
    "L0_ffn_b2", "L0_ffn_A2", "L0_ffn_B2", "L0_ffn_W3",
    "L0_ffn_b3", "L0_ffn_A3", "L0_ffn_B3", "L1_xattn_Wq",
    "L1_xattn_bq", "L1_xattn_Wk", "L1_xattn_bk", "L1_xattn_Wv",
    "L1_xattn_bv", "L1_attn_weight_qkv", "L1_attn_out_w", "L1_attn_out_b",
    "L1_ffn_gate_w", "L1_ffn_Wg", "L1_ffn_Wu", "L1_ffn_Wd",
]
_OUTS = [((4, 128, 128), "float32")]


def kernel(**inputs):
    import numpy as _np
    import concourse.bacc as _bacc
    from concourse import mybir as _mybir
    from concourse.bass_utils import run_bass_kernel_spmd as _run

    nc = _bacc.Bacc("TRN2", target_bir_lowering=False, num_devices=1)
    arrays, aps = {}, {}
    for name in _INS:
        a = _np.ascontiguousarray(inputs[name])
        arrays[f"in_{name}_dram"] = a
        aps[name] = nc.dram_tensor(f"in_{name}_dram", a.shape, _mybir.dt.from_np(a.dtype), kind="ExternalInput").ap()
    outs = []
    for i, (shape, dtype) in enumerate(_OUTS):
        dt = _mybir.dt.from_np(_np.dtype(dtype))
        outs.append(nc.dram_tensor(f"out_{i}_dram", shape, dt, kind="ExternalOutput").ap())
    perceiver_kernel(nc, aps, outs[0])
    r = _run(nc, [arrays], core_ids=[0])
    return r.results[0]["out_0_dram"]
```

```python
from contextlib import ExitStack

import concourse.bass as bass
from concourse import mybir

ALU = mybir.AluOpType
ACT = mybir.ActivationFunctionType
F32 = mybir.dt.float32
F16 = mybir.dt.float16
BF16 = mybir.dt.bfloat16
I32 = mybir.dt.int32
U32 = mybir.dt.uint32
AX_X = mybir.AxisListType.X

P = 128
BIG_NEG = -1.0e30
EPS = 1e-5


def bcast(ap, axis, n):
    dims = list(ap.ap)
    dims.insert(axis, (0, n))
    return bass.AP(ap.tensor, ap.offset, dims)


def repeat(ap, n):
    return bass.AP(ap.tensor, ap.offset, [list(ap.ap)[0], (0, n)])


class Chain:

    def __init__(self, eng, sem, at=0):
        self.eng, self.sem, self.at = eng, sem, at

    def __call__(self, ins):
        ins.then_inc(self.sem, 1)
        self.at = self.at + 1
        self.eng.wait_ge(self.sem, self.at)


def perceiver_kernel(nc, A, out):
    B, T, D = A["x"].shape
    S2 = A["ctx_1024"].shape[1]
    NCH = S2 // P
    H, DH = 16, 8
    HA = A["L0_attn_Wg"].shape[0]
    LV = A["L0_attn_Lparam"].shape[1]
    LVU = 8
    E = A["L0_ffn_Wg"].shape[0]
    HID = A["L0_ffn_W1"].shape[1]
    R = A["L0_ffn_A1"].shape[1]
    HM = HID // P
    BT = B * T
    GK = 512
    NG = B * S2 // GK
    CPG = GK // P
    assert T == P and D == P and BT == 512 and HID == 2 * P

    with ExitStack() as ctx:
        def sb(name, shape, dt=F32):
            return ctx.enter_context(nc.sbuf_tensor(name, shape, dt))

        def sem(name):
            return ctx.enter_context(nc.semaphore(name))

        banks = ctx.enter_context(nc.psum_tensor("banks", [P, 8, 512], F32))
        bank = [banks[:, i, :] for i in range(8)]

        x = sb("x", [P, B, D])
        xn = sb("xn", [P, B, D])
        xT = sb("xT", [P, BT])
        ident = sb("ident", [P, P])
        ident_bf = sb("ident_bf", [P, P], BF16)
        upper = sb("upper", [P, P])
        neg_upper = sb("neg_upper", [P, P])
        future_bf = sb("future_bf", [P, P], BF16)
        head_rows = sb("head_rows", [P, H])
        quarter_rows = sb("quarter_rows", [P, 4])
        zero_bf = sb("zero_bf", [P, P], BF16)
        ones32 = sb("ones32", [P, 32])
        spread_den = sb("spread_den", [P, P])
        bn = sb("bn", [P, B, 6])
        mv = sb("mv", [P, B, 2])
        var_eps = sb("var_eps", [P, B])
        rstd = sb("rstd", [P, B])
        minus_half = sb("minus_half", [P, B])

        const_ready = sem("const_ready")
        pool_const_ready = sem("pool_const_ready")
        head_rows_ready = sem("head_rows_ready")
        x_moved = sem("x_moved")

        ident_dram = nc.dram_tensor("ident_scratch", [P, P], F32).ap()
        ident_ready, ident_stored = sem("ident_ready"), sem("ident_stored")

        with nc.Block() as block:
            @block.sync
            def _(sp):
                sp.dma_start(x[:], A["x"].rearrange("b t d -> t b d")).then_inc(x_moved, 16)
                sp.wait_ge(ident_ready, 1)
                sp.dma_start(ident_dram, ident[:]).then_inc(ident_stored, 16)
                sp.wait_ge(ident_stored, 16)

            @block.vector
            def _(dve):
                chain = Chain(dve, const_ready)
                chain(nc.vector.memset(minus_half[:], -0.5))
                chain(nc.vector.memset(zero_bf[:], 0.0))
                chain(nc.vector.memset(ones32[:], 1.0))
                dve.wait_ge(head_rows_ready, 1)
                chain(nc.vector.tensor_reduce(quarter_rows[:], head_rows[:].rearrange("p (g j) -> p j g", g=4), AX_X,
                                              ALU.add))

            @block.gpsimd
            def _(pool):
                chain = Chain(pool, pool_const_ready)
                chain(nc.gpsimd.memset(ident[:], 0.0))
                chain(nc.gpsimd.affine_select(out=ident[:], in_=ident[:], compare_op=ALU.not_equal, fill=1.0,
                                              base=0, pattern=[[-1, P]], channel_multiplier=1))
                nc.gpsimd.engine_nop().then_inc(ident_ready, 1)
                chain(nc.gpsimd.tensor_copy(ident_bf[:], ident[:]))
                chain(nc.gpsimd.memset(upper[:], 1.0))
                chain(nc.gpsimd.affine_select(out=upper[:], in_=upper[:], compare_op=ALU.is_ge, fill=0.0,
                                              base=0, pattern=[[1, P]], channel_multiplier=-1))
                chain(nc.gpsimd.tensor_scalar(neg_upper[:], upper[:], -1.0, None, ALU.mult))
                chain(nc.gpsimd.memset(future_bf[:], 0.0))
                chain(nc.gpsimd.affine_select(out=future_bf[:], in_=future_bf[:], compare_op=ALU.is_ge, fill=BIG_NEG,
                                              base=0, pattern=[[-1, P]], channel_multiplier=1))
                chain(nc.gpsimd.memset(head_rows[:], 1.0))
                chain(nc.gpsimd.affine_select(out=head_rows[:], in_=head_rows[:], compare_op=ALU.is_ge, fill=0.0,
                                              base=0, pattern=[[-DH, H]], channel_multiplier=1))
                nc.gpsimd.affine_select(out=head_rows[:], in_=head_rows[:], compare_op=ALU.is_ge, fill=0.0,
                                        base=DH - 1, pattern=[[DH, H]],
                                        channel_multiplier=-1).then_inc(head_rows_ready, 1)
                chain(nc.gpsimd.memset(spread_den[:], 0.0))
                chain(nc.gpsimd.affine_select(out=spread_den[:].rearrange("p (c i) -> p c i", c=4),
                                              in_=spread_den[:].rearrange("p (c i) -> p c i", c=4),
                                              compare_op=ALU.not_equal, fill=1.0, base=-DH,
                                              pattern=[[-32, 4], [0, 32]], channel_multiplier=1))

        ln_stats, ln_var_ready, ln_rstd_ready, xn_ready, xn_transposed, xT_ready = (
            sem(n) for n in ("ln_stats", "ln_var_ready", "ln_rstd_ready", "xn_ready", "xn_transposed", "xT_ready"))

        norms = []

        def layer_norm():
            k = len(norms)
            norms.append(k)
            with nc.Block() as block:
                @block.vector
                def _(dve):
                    dve.wait_ge(x_moved, 16)
                    for b in range(B):
                        nc.vector.bn_stats(bn[:, b, :], x[:, b, :]).then_inc(ln_stats, 1)
                    dve.wait_ge(ln_stats, (2 * k + 1) * B)
                    for b in range(B):
                        nc.vector.bn_aggr(mv[:, b, :], bn[:, b, :]).then_inc(ln_stats, 1)
                    dve.wait_ge(ln_stats, (2 * k + 2) * B)
                    nc.vector.tensor_scalar(var_eps[:], mv[:, :, 1], EPS, None, ALU.add).then_inc(ln_var_ready, 1)
                    dve.wait_ge(ln_rstd_ready, k + 1)
                    for b in range(B):
                        nc.vector.tensor_scalar(xn[:, b, :], x[:, b, :], mv[:, b, 0:1], rstd[:, b:b + 1],
                                                ALU.subtract, ALU.mult).then_inc(xn_ready, 1)

                @block.gpsimd
                def _(pool):
                    pool.wait_ge(ln_var_ready, k + 1)
                    nc.gpsimd.tensor_tensor(rstd[:], var_eps[:], minus_half[:], ALU.pow).then_inc(ln_rstd_ready, 1)

                @block.tensor
                def _(pe):
                    for b in range(B):
                        pe.wait_ge(xn_ready, k * B + b + 1)
                        last = nc.tensor.transpose(bank[0][:, b * P:(b + 1) * P], xn[:, b, :], ident[:])
                    last.then_inc(xn_transposed, 1)

                @block.scalar
                def _(act):
                    act.wait_ge(xn_transposed, k + 1)
                    nc.scalar.activation(xT[:], bank[0][:], ACT.Copy).then_inc(xT_ready, 1)

        general_sems = {}

        def general_attention(name, w, masked, safe):
            with ExitStack() as c2:
                def sb(n, shape, dt=F32):
                    return c2.enter_context(nc.sbuf_tensor(f"{name}_{n}", shape, dt))

                def sem(n):
                    if n not in general_sems:
                        general_sems[n] = ctx.enter_context(nc.semaphore(f"general_{n}"))
                    return general_sems[n]

                def unless_safe(on_engine):
                    def put(program):
                        @on_engine
                        def _(eng):
                            within = eng.value_load(safe[0:1, 0:1], min_val=0, max_val=1)
                            with eng.If(within < 1):
                                program(eng)
                    return put

                kT = sb("kT", [P, B * S2])
                v = sb("v", [P, B * NCH, D])
                qT = sb("qT", [P, BT])
                o = sb("o", [P, B, D])
                wq, wk, wv = (sb(n, [P, D]) for n in ("wq", "wk", "wv"))
                bq, bk = sb("bq", [P, 1]), sb("bk", [P, 1])
                bv = sb("bv", [P, D])
                wo, bo = sb("wo", [P, D]), sb("bo", [P, D])
                ctx_rows = sb("ctx_rows", [P, 2, CPG, D])
                ctxT = sb("ctxT", [P, 2, GK])
                w_loaded = sem("w_loaded")
                ctx_moved = [sem("ctx_moved0"), sem("ctx_moved1")]
                rows_transposed = sem("rows_transposed")
                ctxT_ready = sem("ctxT_ready")
                k_projected = sem("k_projected")
                v_projected = sem("v_projected")
                k_ready = sem("k_ready")
                v_ready = sem("v_ready")
                q_projected, q_ready = sem("q_projected"), sem("q_ready")
                n_w = 8 if masked else 6
                rows_dram = A["ctx_1024"].rearrange("b (g c p) d -> (b g) p c d", p=P, c=CPG)

                with nc.Block() as block:
                    @unless_safe(block.sync)
                    def _(sp):
                        for dst, src in ((wq, w["wq"]), (wk, w["wk"]), (wv, w["wv"])):
                            sp.dma_start(dst[:], src).then_inc(w_loaded, 16)
                        for dst, src in ((bq, w["bq"]), (bk, w["bk"])):
                            sp.dma_start(dst[:], src.rearrange("(d a) -> d a", a=1)).then_inc(w_loaded, 16)
                        sp.dma_start(bv[:], w["bv"].partition_broadcast(P)).then_inc(w_loaded, 16)
                        if masked:
                            sp.dma_start(wo[:], w["wo"]).then_inc(w_loaded, 16)
                            sp.dma_start(bo[:], w["bo"].partition_broadcast(P)).then_inc(w_loaded, 16)
                        for u in range(2):
                            sp.dma_start(ctx_rows[:, u, :, :], rows_dram[u]).then_inc(ctx_moved[u], 16)
                        with sp.Fori(1, NG // 2) as i:
                            for u in range(2):
                                sp.wait_ge(rows_transposed, 2 * i + u - 1)
                                sp.dma_start(ctx_rows[:, u, :, :], rows_dram[bass.ds(2 * i + u, 1)].rearrange(
                                    "a p c d -> p (a c) d")).then_inc(ctx_moved[u], 16)

                    @unless_safe(block.tensor)
                    def _(pe):
                        pe.sem_inc(v_projected, 1)
                        pe.wait_ge(w_loaded, 16 * n_w)
                        nc.tensor.matmul(bank[7][:], wq[:], xT[:], start=True, stop=True).then_inc(q_projected, 1)
                        with pe.Fori(0, NG // 2) as i:
                            for u in range(2):
                                pe.wait_ge(ctx_moved[u], 16 * i + 16)
                                pe.wait_ge(ctxT_ready, 2 * i + u + 1)
                                for c in range(CPG):
                                    last = nc.tensor.transpose(bank[u][:, c * P:(c + 1) * P],
                                                               ctx_rows[:, u, c, :], ident[:])
                                last.then_inc(rows_transposed, 1)
                                pe.wait_ge(ctxT_ready, 2 * i + u + 2)
                                pe.wait_ge(k_ready, 2 * i + u + 1)
                                nc.tensor.matmul(bank[2 + u][:], wk[:], ctxT[:, u, :], start=True,
                                                 stop=True).then_inc(k_projected, 1)
                                pe.wait_ge(v_ready, 2 * i + u + 1)
                                for c in range(CPG):
                                    last = nc.tensor.matmul(bank[4 + u][:, c * P:(c + 1) * P],
                                                            ctxT[:, u, c * P:(c + 1) * P], wv[:],
                                                            start=True, stop=True)
                                last.then_inc(v_projected, 1)

                    @unless_safe(block.scalar)
                    def _(act):
                        act.sem_inc(ctxT_ready, 1)
                        with act.Fori(0, NG // 2) as i:
                            for u in range(2):
                                act.wait_ge(rows_transposed, 2 * i + u + 1)
                                act.wait_ge(v_projected, 2 * i + u + 1)
                                nc.scalar.activation(ctxT[:, u, :], bank[u][:], ACT.Copy).then_inc(ctxT_ready, 1)

                    @unless_safe(block.vector)
                    def _(dve):
                        dve.sem_inc(k_ready, 1)
                        dve.sem_inc(v_ready, 1)
                        dve.wait_ge(w_loaded, 16 * n_w)
                        dve.wait_ge(q_projected, 1)
                        nc.vector.tensor_scalar(qT[:], bank[7][:], bq[:], None, ALU.add).then_inc(q_ready, 1)
                        with dve.Fori(0, NG // 2) as i:
                            for u in range(2):
                                dve.wait_ge(k_projected, 2 * i + u + 1)
                                nc.vector.tensor_scalar(kT[:, bass.ds((2 * i + u) * GK, GK)], bank[2 + u][:],
                                                        bk[:], None, ALU.add).then_inc(k_ready, 1)
                                dve.wait_ge(v_projected, 2 * i + u + 2)
                                nc.vector.tensor_tensor(
                                    v[:, bass.ds((2 * i + u) * CPG, CPG), :],
                                    bank[4 + u][:].rearrange("p (c d) -> p c d", c=CPG),
                                    bcast(bv[:], 1, CPG), ALU.add).then_inc(v_ready, 1)

                qz = sb("qz", [P, P])
                s = sb("s", [P, S2])
                neg = sb("neg", [P, S2])
                gp = sb("gp", [P, S2])
                mask_i = sb("mask_i", [P, S2], I32)
                pT = sb("pT", [P, NCH, P])
                nmax, den, rden = sb("nmax", [P, 1]), sb("den", [P, 1]), sb("rden", [P, 1])
                sides_loaded = sem("sides_loaded")
                q_head_ready = sem("q_head_ready")
                scored = sem("scored")
                neg_ready, s_ready, rden_ready = sem("neg_ready"), sem("s_ready"), sem("rden_ready")
                max_ready = sem("max_ready")
                exp_ready = sem("exp_ready")
                probs_ready = sem("probs_ready")
                p_transposed = sem("p_transposed")
                pT_ready = sem("pT_ready")
                head_out = sem("head_out")
                head_done = sem("head_done")
                SCALE = DH ** -0.5
                NB4 = S2 // 512
                with nc.Block() as block:
                    @unless_safe(block.sync)
                    def _(sp):
                        if masked:
                            with sp.Fori(0, B) as b:
                                sp.wait_ge(head_done, b * H + 1)
                                sp.dma_start(mask_i[:], A["mask_BxSxS2_ik1"][bass.ds(b, 1)].rearrange(
                                    "a q k -> q (a k)")).then_inc(sides_loaded, 16)
                                sp.dma_start(gp[:], A["fside_BxSxS2_0"][bass.ds(b, 1)].rearrange(
                                    "a q k -> q (a k)")).then_inc(sides_loaded, 16)

                    @unless_safe(block.vector)
                    def _(dve):
                        dve.sem_inc(head_done, 1)
                        with dve.Fori(0, B) as b:
                            if masked:
                                dve.wait_ge(sides_loaded, 32 * b + 32)
                                nc.vector.tensor_scalar(neg[:], mask_i[:], -1.0, 1.0e9, ALU.add,
                                                        ALU.mult).then_inc(neg_ready, 1)
                            with dve.Fori(0, H) as h:
                                n = b * H + h
                                nc.vector.tensor_scalar(qz[:], qT[:, bass.ds(b * P, P)],
                                                        head_rows[:, bass.ds(h, 1)], None,
                                                        ALU.mult).then_inc(q_head_ready, 1)
                                dve.wait_ge(scored, n + 1)
                                if masked:
                                    dve.wait_ge(neg_ready, b + 1)
                                for j in range(NB4):
                                    cols = slice(j * 512, (j + 1) * 512)
                                    if masked:
                                        last = nc.vector.scalar_tensor_tensor(
                                            out=s[:, cols], in0=bank[j][:], scalar=SCALE, in1=neg[:, cols],
                                            op0=ALU.mult, op1=ALU.add)
                                    else:
                                        last = nc.vector.tensor_scalar(s[:, cols], bank[j][:], SCALE, None, ALU.mult)
                                last.then_inc(s_ready, 1)
                                dve.wait_ge(s_ready, n + 1)
                                nc.vector.tensor_reduce(nmax[:], s[:], AX_X, ALU.max, negate=True).then_inc(max_ready, 1)
                                dve.wait_ge(exp_ready, n + 1)
                                nc.vector.reciprocal(rden[:], den[:]).then_inc(rden_ready, 1)
                                if masked:
                                    nc.vector.tensor_tensor(s[:], s[:], gp[:], ALU.mult).then_inc(probs_ready, 1)
                                dve.wait_ge(head_out, n + 1)
                                dve.wait_ge(rden_ready, n + 1)
                                nc.vector.tensor_scalar(o[:, bass.ds(b, 1), bass.ds(h * DH, DH)],
                                                        bank[6][:, bass.ds(h * DH, DH)], rden[:], None,
                                                        ALU.mult).then_inc(head_done, 1)

                    @unless_safe(block.tensor)
                    def _(pe):
                        with pe.Fori(0, B) as b:
                            with pe.Fori(0, H) as h:
                                n = b * H + h
                                pe.wait_ge(q_head_ready, n + 1)
                                for j in range(NB4):
                                    last = nc.tensor.matmul(bank[j][:], qz[:], kT[:, bass.ds(b * S2 + j * 512, 512)],
                                                            start=True, stop=True)
                                last.then_inc(scored, 1)
                                pe.wait_ge(probs_ready if masked else exp_ready, n + 1)
                                for g in range(NB4):
                                    pe.wait_ge(pT_ready, NB4 * n + g + 1)
                                    for c in range(4):
                                        ch = 4 * g + c
                                        last = nc.tensor.transpose(bank[4 + g % 2][:, c * P:(c + 1) * P],
                                                                   s[:, ch * P:(ch + 1) * P], ident[:])
                                    last.then_inc(p_transposed, 1)
                                pe.wait_ge(pT_ready, NB4 * n + NB4 + 1)
                                pe.wait_ge(head_done, n + 1)
                                for c in range(NCH):
                                    last = nc.tensor.matmul(bank[6][:, 0:D], pT[:, c, :],
                                                            v[:, bass.ds(b * NCH + c, 1), :].rearrange("p a d -> p (a d)"),
                                                            start=(c == 0), stop=(c == NCH - 1))
                                last.then_inc(head_out, 1)

                    @unless_safe(block.scalar)
                    def _(act):
                        act.sem_inc(pT_ready, 1)
                        with act.Fori(0, B) as b:
                            with act.Fori(0, H) as h:
                                n = b * H + h
                                act.wait_ge(max_ready, n + 1)
                                nc.scalar.activation(s[:], s[:], ACT.Exp, bias=nmax[:],
                                                     accum_out=den[:]).then_inc(exp_ready, 1)
                                for g in range(NB4):
                                    act.wait_ge(p_transposed, NB4 * n + g + 1)
                                    nc.scalar.activation(pT[:, 4 * g:4 * g + 4, :], bank[4 + g % 2][:].rearrange(
                                        "p (c q) -> p c q", c=4), ACT.Copy).then_inc(pT_ready, 1)

                oT = sb("oT", [P, BT])
                o_transposed, oT_ready = sem("o_transposed"), sem("oT_ready")
                projected, xsteps = sem("projected"), sem("xsteps")
                with nc.Block() as block:
                    @unless_safe(block.tensor)
                    def _(pe):
                        if masked:
                            for b in range(B):
                                last = nc.tensor.transpose(bank[0][:, b * P:(b + 1) * P], o[:, b, :], ident[:])
                            last.then_inc(o_transposed, 1)
                            pe.wait_ge(oT_ready, 1)
                            for b in range(B):
                                last = nc.tensor.matmul(bank[1][:, b * D:(b + 1) * D], oT[:, b * P:(b + 1) * P], wo[:],
                                                        start=True, stop=True)
                            last.then_inc(projected, 1)

                    @unless_safe(block.scalar)
                    def _(act):
                        if masked:
                            act.wait_ge(o_transposed, 1)
                            nc.scalar.activation(oT[:], bank[0][:], ACT.Copy).then_inc(oT_ready, 1)

                    @unless_safe(block.vector)
                    def _(dve):
                        chain = Chain(dve, xsteps)
                        if masked:
                            chain(nc.vector.tensor_tensor(x[:], x[:], bcast(bo[:], 1, B), ALU.add))
                            dve.wait_ge(projected, 1)
                            chain(nc.vector.tensor_tensor(x[:], x[:], bank[1][:].rearrange("p (b d) -> p b d", b=B),
                                                          ALU.add))
                        else:
                            chain(nc.vector.tensor_tensor(x[:], x[:], o[:], ALU.add))
                with nc.Block() as block:
                    @unless_safe(block.sync)
                    def _(sp):
                        for s_ in general_sems.values():
                            sp.sem_clear(s_)

        NU = 2 * NCH
        GPB = S2 // GK
        RT = 4
        (w_in, ctx_in0, ctx_in1, side_in, rows_turned, ctxT_out, k_summed, v_summed, k1_out, k2_out, kmax_out,
         v_out, stack_in, q_summed, q_out, q_turned, q_hi_out, q_parts_out, q_blocks_out) = (
            sem(n) for n in ("w_in", "ctx_in0", "ctx_in1", "side_in", "rows_turned", "ctxT_out", "k_summed",
                             "v_summed", "k1_out", "k2_out", "kmax_out", "v_out", "stack_in", "q_summed", "q_out",
                             "q_turned", "q_hi_out", "q_parts_out", "q_blocks_out"))
        ctx_in = [ctx_in0, ctx_in1]
        alive_out, neg_out, sides_turned, gpT_out, negT_out = (
            sem(n) for n in ("alive_out", "neg_out", "sides_turned", "gpT_out", "negT_out"))
        scores_out, exp_out, weighted_out, v_staged, mixed_out, acc_out = (
            sem(n) for n in ("scores_out", "exp_out", "weighted_out", "v_staged", "mixed_out", "acc_out"))
        (rings_ready, wo_in, q_rows_turned, den_spread, attended, attended_steps, output_summed, q_bound_out,
         q_abs_out, bounds_summed, limits_out, limits_turned, safe_steps) = (
            sem(n) for n in ("rings_ready", "wo_in", "q_rows_turned", "den_spread", "attended", "attended_steps",
                             "output_summed", "q_bound_out", "q_abs_out", "bounds_summed", "limits_out",
                             "limits_turned", "safe_steps"))
        safe = sb("safe", [1, 1], I32)
        x_steps = [sem("x_steps0"), sem("x_steps1")]
        N_SAFE = 10
        NW_FIRST = 7

        def cross_attention(layer, w, masked):
            RANGE, FP16_RANGE, DEAD_RANGE = 80.0, 1000.0, 32.0
            SCALE = DH ** -0.5
            NW = 7 if masked else 6
            W0 = 16 * (NW_FIRST if layer else 0)
            with ExitStack() as c2:
                def sb(n, shape, dt=F32):
                    return c2.enter_context(nc.sbuf_tensor(f"xa{layer}_{n}", shape, dt))

                wq, wk, wv = (sb(n, [P, D]) for n in ("wq", "wk", "wv"))
                bq, bv, bo = sb("bq", [P, D]), sb("bv", [P, D]), sb("bo", [P, D])
                bk = sb("bk", [P, 1])
                wo_rows = sb("wo_rows", [P, RT, D])
                ctx_rows = sb("ctx_rows", [P, 2, CPG, D])
                ctxT = sb("ctxT", [P, 2, GK])
                k1, k2 = sb("k1", [P, S2], F16), sb("k2", [P, S2], F16)
                kstack = sb("kstack", [P, 2, RT, S2], F16)
                v = sb("v", [P, 2, NCH, D])
                v_ring = sb("v_ring", [P, 2, H, 32])
                kmax = sb("kmax", [P, B * GPB])
                q_rows = sb("q_rows", [P, B, D])
                q_live = sb("q_live", [P, RT, 4, 32])
                q_parts = sb("q_parts", [P, RT, P], F16)
                q_blocks = sb("q_blocks", [P, 2, RT, 4, P], F16)
                e_ring = sb("e_ring", [P, 4, 8, P])
                alive = sb("alive", [P, B])
                if masked:
                    gp = sb("gp", [P, S2])
                    mask_i = sb("mask_i", [P, S2], I32)
                    neg = sb("neg", [P, S2], BF16)
                    neg_scale, neg_bias = sb("neg_scale", [P, B]), sb("neg_bias", [P, B])
                    gpT = sb("gpT", [P, 2, NCH, P])
                    negT = sb("negT", [P, 2, NCH, P], BF16)
                    g_ring = sb("g_ring", [P, 4, 8, P])
                num = sb("num", [P, B, 512])
                den = sb("den", [P, B, 512])
                pv_in = g_ring if masked else e_ring
                pv_ready = weighted_out if masked else exp_out

                rows_dram = A["ctx_1024"].rearrange("b (g c p) d -> (b g) p c d", p=P, c=CPG)
                G0, U0, C0, B0 = layer * B * GPB, layer * B * NU, layer * B * NCH, layer * B
                EXP_AHEAD, MIXED_AHEAD = 2, 4
                last_exp = lambda b: U0 + (b + 1) * NU + EXP_AHEAD
                last_mixed = lambda b: U0 + (b + 1) * NU + MIXED_AHEAD
                negT_bank = [banks[:, 2 + i, :].bitcast(BF16) for i in range(2)]

                with nc.Block() as block:
                    @block.sync
                    def _(sp):
                        for dst, src in ((wq[:], w["wq"]), (wk[:], w["wk"]), (wv[:], w["wv"]),
                                         (bk[:], w["bk"].rearrange("(d a) -> d a", a=1)),
                                         (bq[:], w["bq"].partition_broadcast(P)),
                                         (bv[:], w["bv"].partition_broadcast(P))):
                            sp.dma_start(dst, src).then_inc(w_in, 16)
                        if masked:
                            sp.dma_start(bo[:], w["bo"].partition_broadcast(P)).then_inc(w_in, 16)

                        def load(b):
                            for g in range(GPB):
                                n = G0 + b * GPB + g
                                if b * GPB + g >= 2:
                                    sp.wait_ge(rows_turned, n - 1)
                                sp.dma_start(ctx_rows[:, g % 2, :, :], rows_dram[b * GPB + g]).then_inc(ctx_in[g % 2], 16)
                            if masked:
                                if b >= 1:
                                    sp.wait_ge(sides_turned, 6 * b)
                                sp.dma_start(mask_i[:], A["mask_BxSxS2_ik1"][b]).then_inc(side_in, 16)
                                sp.dma_start(gp[:], A["fside_BxSxS2_0"][b]).then_inc(side_in, 16)

                        def stack(b):
                            sp.wait_ge(k2_out, G0 + (b + 1) * GPB)
                            if b >= 2:
                                sp.wait_ge(exp_out, last_exp(b - 2))
                            for g, part in enumerate((k1, k1, k2, k2)):
                                for r in range(RT):
                                    sp.dma_start(kstack[32 * g:32 * g + 32, b % 2, r, :],
                                                 part[32 * r:32 * r + 32, :]).then_inc(stack_in, 16)

                        load(0)
                        sp.wait_ge(rings_ready, 3 * layer + 1)
                        src = (w["wo"] if masked else ident_dram).rearrange("(r c d) n -> c d r n", r=RT, c=4)
                        for c in range(4):
                            sp.dma_start(wo_rows[32 * c:32 * c + DH, :, :], src[c]).then_inc(wo_in, 16)
                        stack(0)
                        for b in range(1, B):
                            load(b)
                            stack(b)

                    @block.gpsimd
                    def _(pool):
                        nc.gpsimd.memset(wo_rows[:], 0.0).then_inc(rings_ready, 1)
                        nc.gpsimd.memset(v_ring[:], 0.0).then_inc(rings_ready, 1)
                        pool.wait_ge(rings_ready, 3 * layer + 2)
                        if not masked:
                            nc.gpsimd.memset(v_ring[:, :, :, DH:DH + 1], 1.0).then_inc(rings_ready, 1)
                        else:
                            nc.gpsimd.engine_nop().then_inc(rings_ready, 1)
                        pool.wait_ge(rings_ready, 3 * layer + 3)
                        for b in range(B):
                            pool.wait_ge(v_out, G0 + (b + 1) * GPB)
                            with pool.Fori(0, NCH // 2) as i:
                                for c in range(2):
                                    pool.wait_ge(mixed_out, U0 + b * NU + 4 * i + 2 * c - 2 + MIXED_AHEAD)
                                    nc.gpsimd.tensor_copy(
                                        v_ring[:, c, :, 0:DH],
                                        v[:, b % 2, bass.ds(2 * i + c, 1), :].rearrange("p a (h d) -> p (a h) d", h=H)
                                    ).then_inc(v_staged, 1)

                    @block.tensor
                    def _(pe):
                        if layer == 0:
                            pe.sem_inc(mixed_out, MIXED_AHEAD)

                        def turn(b, g):
                            n = G0 + b * GPB + g
                            pe.wait_ge(ctx_in[g % 2], 16 * ((G0 + b * GPB + g) // 2 + 1))
                            if b * GPB + g >= 2:
                                pe.wait_ge(ctxT_out, n - 1)
                            for c in range(CPG):
                                last = nc.tensor.transpose(bank[6 + g % 2][:, c * P:(c + 1) * P],
                                                           ctx_rows[:, g % 2, c, :], ident[:])
                            last.then_inc(rows_turned, 1)

                        def project(b, g):
                            n = G0 + b * GPB + g
                            pe.wait_ge(ctxT_out, n + 1)
                            if b * GPB + g >= 2:
                                pe.wait_ge(k2_out, n - 1)
                                pe.wait_ge(v_out, n - 1)
                            nc.tensor.matmul(bank[g % 2][:], wk[:], ctxT[:, g % 2, :], start=True,
                                             stop=True).then_inc(k_summed, 1)
                            for c in range(CPG):
                                last = nc.tensor.matmul(bank[2 + g % 2][:, c * P:(c + 1) * P],
                                                        ctxT[:, g % 2, c * P:(c + 1) * P], wv[:],
                                                        start=True, stop=True)
                            last.then_inc(v_summed, 1)

                        def queries(b):
                            pe.wait_ge(q_out, layer * (2 + B) + 2 + b + 1)
                            pe.wait_ge(ctxT_out, G0 + (b + 1) * GPB)
                            for r in range(RT):
                                last = nc.tensor.transpose(bank[6][:, r * P:(r + 1) * P],
                                                           q_live[:, r, :, :].rearrange("p g i -> p (g i)"), ident[:])
                            last.then_inc(q_turned, 1)

                        def sides(b):
                            pe.wait_ge(k2_out, G0 + (b + 1) * GPB)
                            pe.wait_ge(v_out, G0 + (b + 1) * GPB)
                            pe.wait_ge(side_in, 32 * b + 32)
                            for g in range(4):
                                ps = (bank[0], bank[1], bank[7], bank[0])[g]
                                if g == 3:
                                    pe.wait_ge(gpT_out, 4 * b + 1)
                                for c in range(4):
                                    ch = 4 * g + c
                                    last = nc.tensor.transpose(ps[:, c * P:(c + 1) * P], gp[:, ch * P:(ch + 1) * P],
                                                               ident[:])
                                last.then_inc(sides_turned, 1)
                            pe.wait_ge(neg_out, b + 1)
                            for g in range(2):
                                for c in range(8):
                                    ch = 8 * g + c
                                    last = nc.tensor.transpose(negT_bank[g][:, c * P:(c + 1) * P],
                                                               neg[:, ch * P:(ch + 1) * P], ident_bf[:])
                                last.then_inc(sides_turned, 1)

                        def prepare(b):
                            if b >= 1:
                                pe.wait_ge(q_parts_out, 2 * (B0 + b))
                                if masked:
                                    pe.wait_ge(gpT_out, 4 * b)
                                    pe.wait_ge(negT_out, 2 * b)
                            if b >= 2:
                                pe.wait_ge(exp_out, last_exp(b - 2))
                            turn(b, 0)
                            turn(b, 1)
                            project(b, 0)
                            turn(b, 2)
                            project(b, 1)
                            turn(b, 3)
                            project(b, 2)
                            project(b, 3)
                            queries(b)
                            if masked:
                                sides(b)

                        def score(b, n, c, hf):
                            pe.wait_ge(exp_out, n - 1 + EXP_AHEAD)
                            for rr in range(2):
                                r = 2 * hf + rr
                                last = nc.tensor.matmul(
                                    bank[r][:], kstack[:, b % 2, r, c * P:(c + 1) * P] if isinstance(c, int)
                                    else kstack[:, b % 2, r, bass.ds(c * P, P)],
                                    q_blocks[:, b % 2, r, :, :].rearrange("p j t -> p (j t)"), start=True,
                                    stop=not masked)
                                if masked:
                                    mask_cols = negT[:, b % 2, c, :] if isinstance(c, int) else negT[
                                        :, b % 2, bass.ds(c, 1), :].rearrange("p a q -> p (a q)")
                                    last = nc.tensor.matmul(bank[r][:], ident_bf[:], bcast(mask_cols, 1, 4),
                                                            start=False, stop=True)
                            last.then_inc(scores_out, 1)

                        def mix(b, n, chunk, k):
                            hf = k % 2
                            pe.wait_ge(v_staged, chunk + 1)
                            pe.wait_ge(pv_ready, n + 1 + (0 if masked else EXP_AHEAD))
                            for rr in range(2):
                                for c in range(4):
                                    r = 2 * hf + rr
                                    last = nc.tensor.matmul(bank[4][32 * c:32 * c + 32, r * P:(r + 1) * P],
                                                            v_ring[:, k // 2, 4 * r + c, :], pv_in[:, k, 4 * rr + c, :],
                                                            start=False, stop=False, skip_group_check=True)
                            if masked:
                                for c in range(4):
                                    last = nc.tensor.matmul(
                                        bank[5][32 * c:32 * c + 32, 2 * hf * P:(2 * hf + 2) * P], ones32[:],
                                        e_ring[:, k, :, :].rearrange("p (r c) t -> p r c t", r=2)[:, :, c, :],
                                        start=False, stop=False, skip_group_check=True)
                            last.then_inc(mixed_out, 1)

                        def attend(b):
                            n0, ch0 = U0 + b * NU, C0 + b * NCH
                            pe.wait_ge(stack_in, 16 * 16 * (B0 + b + 1))
                            pe.wait_ge(q_blocks_out, B0 + b + 1)
                            if masked:
                                pe.wait_ge(negT_out, 2 * b + 2)
                            if b + 1 < B:
                                pe.wait_ge(k2_out, G0 + (b + 2) * GPB)
                                pe.wait_ge(v_out, G0 + (b + 2) * GPB)
                                if masked:
                                    pe.wait_ge(gpT_out, 4 * b + 8)
                                    pe.wait_ge(negT_out, 2 * b + 4)
                            score(b, n0, 0, 0)
                            score(b, n0 + 1, 0, 1)
                            if b >= 1:
                                pe.wait_ge(acc_out, B0 + b)
                            for acc in (4, 5) if masked else (4,):
                                nc.tensor.matmul(bank[acc][:], zero_bf[:], bcast(ident_bf[:], 1, 4), start=True,
                                                 stop=False, skip_group_check=True)
                            with pe.Fori(0, NCH // 2 - 1) as i:
                                for k in range(4):
                                    score(b, n0 + 4 * i + k + 2, 2 * i + (k + 2) // 2, k % 2)
                                    mix(b, n0 + 4 * i + k, ch0 + 2 * i + k // 2, k)
                            for k in range(4):
                                if k < 2:
                                    score(b, n0 + NU - 2 + k, NCH - 1, k)
                                mix(b, n0 + NU - 4 + k, ch0 + NCH - 2 + k // 2, k)

                        pe.wait_ge(w_in, W0 + 16 * NW)
                        for b in range(B):
                            last = nc.tensor.matmul(bank[5][:, b * D:(b + 1) * D], xT[:, b * P:(b + 1) * P], wq[:],
                                                    start=True, stop=True)
                        last.then_inc(q_summed, 1)
                        prepare(0)
                        for b in range(B):
                            if b + 1 < B:
                                prepare(b + 1)
                            attend(b)

                    @block.scalar
                    def _(act):
                        if layer == 0:
                            act.sem_inc(exp_out, EXP_AHEAD)

                        def prepare(b):
                            for g in range(GPB):
                                n = G0 + b * GPB + g
                                act.wait_ge(rows_turned, n + 1)
                                if b * GPB + g >= 2:
                                    act.wait_ge(v_summed, n - 1)
                                nc.scalar.activation(ctxT[:, g % 2, :], bank[6 + g % 2][:], ACT.Copy
                                                     ).then_inc(ctxT_out, 1)
                                act.wait_ge(k_summed, n + 1)
                                if b >= 1 and g == 0:
                                    act.wait_ge(stack_in, 16 * 16 * (B0 + b))
                                nc.scalar.activation(k1[:, g * GK:(g + 1) * GK], bank[g % 2][:], ACT.Identity,
                                                     bias=bk[:]).then_inc(k1_out, 1)
                            act.wait_ge(q_turned, B0 + b + 1)
                            if b >= 1:
                                act.wait_ge(q_blocks_out, B0 + b)
                            nc.scalar.activation(q_parts[:], bank[6][:].rearrange("p (r t) -> p r t", r=RT),
                                                 ACT.Copy).then_inc(q_hi_out, 1)
                            if masked:
                                act.wait_ge(alive_out, 3 * b + 3)
                                if b >= 1:
                                    act.wait_ge(sides_turned, 6 * b)
                                nc.scalar.activation(neg[:], mask_i[:], ACT.Identity, bias=neg_bias[:, b:b + 1],
                                                     scale=neg_scale[:, b:b + 1]).then_inc(neg_out, 1)
                                for g in range(2):
                                    act.wait_ge(sides_turned, 6 * b + 5 + g)
                                    if b >= 2 and g == 0:
                                        act.wait_ge(exp_out, last_exp(b - 2))
                                    nc.scalar.activation(negT[:, b % 2, 8 * g:8 * g + 8, :], negT_bank[g].rearrange(
                                        "p (c q) -> p c q", c=8), ACT.Copy).then_inc(negT_out, 1)

                        act.wait_ge(w_in, W0 + 16 * NW)
                        prepare(0)
                        for b in range(B):
                            if b + 1 < B:
                                prepare(b + 1)
                            n0 = U0 + b * NU
                            with act.Fori(0, NCH // 2) as i:
                                for k in range(4):
                                    act.wait_ge(scores_out, n0 + 4 * i + k + 1)
                                    act.wait_ge(mixed_out, n0 + 4 * i + k - 3 + MIXED_AHEAD)
                                    nc.scalar.activation(
                                        e_ring[:, k, :, :].rearrange("p (r c) t -> p r (c t)", r=2),
                                        banks[:, 2 * (k % 2):2 * (k % 2) + 2, :], ACT.Exp).then_inc(exp_out, 1)

                    @block.vector
                    def _(dve):
                        Q0 = layer * (2 + B)

                        def prepare(b):
                            if masked:
                                dve.wait_ge(side_in, 32 * b + 32)
                                nc.vector.tensor_reduce(alive[:, b:b + 1], mask_i[:], AX_X, ALU.max).then_inc(alive_out, 1)
                                dve.wait_ge(alive_out, 3 * b + 1)
                                nc.vector.tensor_scalar(neg_scale[:, b:b + 1], alive[:, b:b + 1], 1.0e9, None,
                                                        ALU.mult).then_inc(alive_out, 1)
                                nc.vector.tensor_scalar(neg_bias[:, b:b + 1], alive[:, b:b + 1], -1.0e9, None,
                                                        ALU.mult).then_inc(alive_out, 1)
                            if b >= 1:
                                dve.wait_ge(q_turned, B0 + b)
                            q_four = bcast(q_rows[:, b, :].rearrange("p (r i) -> p r i", r=RT), 2, 4)
                            if masked:
                                nc.vector.tensor_scalar(q_live[:], q_four, alive[:, b:b + 1], None,
                                                        ALU.mult).then_inc(q_out, 1)
                            else:
                                nc.vector.tensor_copy(q_live[:], q_four).then_inc(q_out, 1)
                            for g in range(GPB):
                                n = G0 + b * GPB + g
                                keys = slice(g * GK, (g + 1) * GK)
                                dve.wait_ge(k1_out, n + 1)
                                if b >= 1 and g == 0:
                                    dve.wait_ge(stack_in, 16 * 16 * (B0 + b))
                                nc.vector.scalar_tensor_tensor(out=k2[:, keys], in0=bank[g % 2][:], scalar=bk[:],
                                                               in1=k1[:, keys], op0=ALU.add,
                                                               op1=ALU.subtract).then_inc(k2_out, 1)
                                dve.wait_ge(v_summed, n + 1)
                                if b >= 2 and g == 0:
                                    dve.wait_ge(v_staged, C0 + (b - 1) * NCH)
                                nc.vector.tensor_tensor(v[:, b % 2, g * CPG:(g + 1) * CPG, :],
                                                        bank[2 + g % 2][:].rearrange("p (c d) -> p c d", c=CPG),
                                                        bcast(bv[:], 1, CPG), ALU.add).then_inc(v_out, 1)
                                nc.vector.tensor_reduce(kmax[:, b * GPB + g:b * GPB + g + 1], k1[:, keys], AX_X,
                                                        ALU.max, apply_absolute_value=True).then_inc(kmax_out, 1)
                            dve.wait_ge(q_hi_out, B0 + b + 1)
                            for p0 in (32, 96):
                                rows = slice(p0, p0 + 32)
                                nc.vector.tensor_tensor(q_parts[rows, :, :],
                                                        bank[6][rows, :].rearrange("p (r t) -> p r t", r=RT),
                                                        q_parts[rows, :, :], ALU.subtract).then_inc(q_parts_out, 1)
                            dve.wait_ge(q_parts_out, 2 * (B0 + b) + 2)
                            if b >= 2:
                                dve.wait_ge(scores_out, U0 + (b - 1) * NU)
                            for j in range(4):
                                last = nc.vector.tensor_scalar(q_blocks[:, b % 2, :, j, :], q_parts[:],
                                                               quarter_rows[:, j:j + 1], None, ALU.mult)
                            last.then_inc(q_blocks_out, 1)
                            if masked:
                                for g in range(4):
                                    dve.wait_ge(sides_turned, 6 * b + g + 1)
                                    nc.vector.tensor_copy(gpT[:, b % 2, 4 * g:4 * g + 4, :],
                                                          (bank[0], bank[1], bank[7], bank[0])[g][:].rearrange(
                                                              "p (c q) -> p c q", c=4)).then_inc(gpT_out, 1)

                        dve.wait_ge(w_in, W0 + 16 * NW)
                        dve.wait_ge(q_summed, layer + 1)
                        nc.vector.tensor_tensor(q_rows[:], bank[5][:].rearrange("p (b d) -> p b d", b=B),
                                                bcast(bq[:], 1, B), ALU.add).then_inc(q_out, 1)
                        dve.wait_ge(q_out, Q0 + 1)
                        nc.vector.tensor_scalar(q_rows[:], q_rows[:], SCALE, None, ALU.mult).then_inc(q_out, 1)
                        dve.wait_ge(q_out, Q0 + 2)
                        prepare(0)
                        for b in range(B):
                            if b + 1 < B:
                                prepare(b + 1)
                            n0 = U0 + b * NU
                            if masked:
                                dve.wait_ge(gpT_out, 4 * b + 4)
                                with dve.Fori(0, NCH // 2) as i:
                                    for k in range(4):
                                        dve.wait_ge(exp_out, n0 + 4 * i + k + 1 + EXP_AHEAD)
                                        dve.wait_ge(mixed_out, n0 + 4 * i + k - 3 + MIXED_AHEAD)
                                        nc.vector.tensor_tensor(
                                            g_ring[:, k, :, :], e_ring[:, k, :, :],
                                            bcast(gpT[:, b % 2, bass.ds(2 * i + k // 2, 1), :].rearrange(
                                                "p a q -> p (a q)"), 1, 8), ALU.mult).then_inc(weighted_out, 1)
                            dve.wait_ge(mixed_out, last_mixed(b))
                            if masked:
                                nc.vector.reciprocal(den[:, b, :], bank[5][:])
                            nc.vector.tensor_copy(num[:, b, :], bank[4][:]).then_inc(acc_out, 1)

                q_abs, q_bound = sb("q_abs", [P, BT]), sb("q_bound", [P, BT])
                k_most, q_most = sb("k_most", [P, 1]), sb("q_most", [P, 1])
                limits = sb("limits", [P, 3])
                worst = sb("worst", [1, 3])
                KT = 3 if masked else 2
                with nc.Block() as block:
                    @block.tensor
                    def _(pe):
                        for b in range(B):
                            last = nc.tensor.transpose(bank[5][:, b * P:(b + 1) * P], q_rows[:, b, :], ident[:])
                        last.then_inc(q_rows_turned, 1)
                        if not masked:
                            for b in range(B):
                                nc.tensor.matmul(bank[b][:], spread_den[:], num[:, b, :], start=True,
                                                 stop=True).then_inc(den_spread, 1)
                        pe.wait_ge(wo_in, 64 * (layer + 1))
                        for b in range(B):
                            pe.wait_ge(attended, B0 + b + 1)
                            for r in range(RT):
                                last = nc.tensor.matmul(bank[4][:, b * D:(b + 1) * D], num[:, b, r * P:(r + 1) * P],
                                                        wo_rows[:, r, :], start=(r == 0), stop=(r == RT - 1))
                        last.then_inc(output_summed, 1)
                        pe.wait_ge(q_bound_out, layer + 1)
                        nc.tensor.matmul(bank[6][0:H, :], head_rows[:], q_bound[:], start=True,
                                         stop=True).then_inc(bounds_summed, 1)
                        pe.wait_ge(limits_out, 3 * layer + 3)
                        nc.tensor.transpose(bank[7][0:1, 0:P], limits[:, 0:1], ident[:])
                        nc.tensor.transpose(bank[7][0:1, P:2 * P], limits[:, 1:2], ident[:])
                        nc.tensor.transpose(bank[7][0:1, 2 * P:2 * P + H], limits[0:H, 2:3],
                                            ident[0:H, 0:H]).then_inc(limits_turned, 1)

                    @block.scalar
                    def _(act):
                        act.wait_ge(q_rows_turned, layer + 1)
                        nc.scalar.activation(q_abs[:], bank[5][:], ACT.Abs).then_inc(q_abs_out, 1)

                    @block.vector
                    def _(dve):
                        chain = Chain(dve, safe_steps, layer * N_SAFE)
                        chain(nc.vector.tensor_reduce(k_most[:], kmax[:], AX_X, ALU.max))
                        dve.wait_ge(q_abs_out, layer + 1)
                        nc.vector.tensor_scalar(q_bound[:], q_abs[:], k_most[:], None, ALU.mult).then_inc(q_bound_out, 1)
                        chain(nc.vector.tensor_reduce(q_most[:], q_abs[:], AX_X, ALU.max))
                        for b in range(B):
                            if not masked:
                                dve.wait_ge(den_spread, b + 1)
                                nc.vector.reciprocal(den[:, b, :], bank[b][:]).then_inc(attended_steps, 1)
                                dve.wait_ge(attended_steps, b + 1)
                            nc.vector.tensor_tensor(num[:, b, :], num[:, b, :], den[:, b, :],
                                                    ALU.mult).then_inc(attended, 1)
                        chain(nc.vector.tensor_tensor(q_most[:], q_most[:], k_most[:], ALU.max))
                        nc.vector.tensor_scalar(limits[:, 0:1], q_most[:], RANGE / FP16_RANGE, None,
                                                ALU.mult).then_inc(limits_out, 1)
                        if masked:
                            chain(nc.vector.tensor_reduce(k_most[:], alive[:], AX_X, ALU.min))
                            nc.vector.tensor_scalar(limits[:, 1:2], k_most[:], -(RANGE - DEAD_RANGE),
                                                    RANGE - DEAD_RANGE, ALU.mult, ALU.add).then_inc(limits_out, 1)
                        else:
                            chain(nc.vector.memset(k_most[:], 0.0))
                            nc.vector.memset(limits[:, 1:2], 0.0).then_inc(limits_out, 1)
                        dve.wait_ge(bounds_summed, layer + 1)
                        nc.vector.tensor_reduce(limits[0:H, 2:3], bank[6][0:H, :], AX_X, ALU.max).then_inc(limits_out, 1)
                        dve.wait_ge(limits_turned, layer + 1)
                        chain(nc.vector.tensor_reduce(worst[0:1, 0:1], bank[7][0:1, 0:P], AX_X, ALU.max))
                        chain(nc.vector.tensor_reduce(worst[0:1, 1:2], bank[7][0:1, P:2 * P], AX_X, ALU.max))
                        chain(nc.vector.tensor_reduce(worst[0:1, 2:3], bank[7][0:1, 2 * P:2 * P + H], AX_X, ALU.max))
                        chain(nc.vector.tensor_tensor(worst[0:1, 2:3], worst[0:1, 2:3], worst[0:1, 1:2], ALU.add))
                        chain(nc.vector.tensor_tensor(worst[0:1, 2:3], worst[0:1, 2:3], worst[0:1, 0:1], ALU.max))
                        chain(nc.vector.tensor_scalar(safe[:], worst[0:1, 2:3], RANGE, None, ALU.is_le))
                        dve.wait_ge(output_summed, layer + 1)
                        within = dve.value_load(safe[0:1, 0:1], min_val=0, max_val=1)
                        with dve.If(within > 0):
                            nc.vector.tensor_tensor(x[:], x[:], bank[4][:].rearrange("p (b d) -> p b d", b=B),
                                                    ALU.add).then_inc(x_steps[layer], 1)
                            if masked:
                                dve.wait_ge(x_steps[layer], 1)
                                nc.vector.tensor_tensor(x[:], x[:], bcast(bo[:], 1, B), ALU.add)
            general_attention(f"general{layer}", w, masked, safe)

        def small_sems(c2, name, *names):
            return [ctx.enter_context(nc.semaphore(f"{name}_{n}")) for n in names]

        def retention(name, w):
            with ExitStack() as c2:
                def sb(n, shape, dt=F32):
                    return c2.enter_context(nc.sbuf_tensor(f"{name}_{n}", shape, dt))

                def sem(n):
                    return ctx.enter_context(nc.semaphore(f"{name}_{n}"))

                NZ = HA + HA * LV
                wq, wk, wv = (sb(n, [P, HA, D]) for n in ("wq", "wk", "wv"))
                wo = sb("wo", [P, HA * P])
                wz = sb("wz", [NZ, D])
                z_bias = sb("z_bias", [P, NZ])
                ln_g, ln_b = sb("ln_g", [P, D]), sb("ln_b", [P, D])
                wqk = sb("wqk", [P, HA, D])
                woT = sb("woT", [P, HA, D])
                wvo = sb("wvo", [P, HA * D])
                wzT = sb("wzT", [P, NZ])
                w_loaded = sem("w_loaded")
                qk_merged, wo_transposed, woT_ready, vo_merged = (
                    sem(n) for n in ("qk_merged", "wo_transposed", "woT_ready", "vo_merged"))
                folded = sem("folded")

                with nc.Block() as block:
                    @block.sync
                    def _(sp):
                        for dst, src in ((wq, w["wq"]), (wk, w["wk"]), (wv, w["wv"])):
                            sp.dma_start(dst[:], src.rearrange("(h s) d -> s h d", h=HA)).then_inc(w_loaded, 16)
                        sp.dma_start(wo[:], w["wo"]).then_inc(w_loaded, 16)
                        sp.dma_start(wz[0:HA, :], w["wg"]).then_inc(w_loaded, 16)
                        sp.dma_start(wz[HA:NZ, :], w["wdl"]).then_inc(w_loaded, 16)
                        sp.dma_start(z_bias[:, 0:HA], w["bg"].partition_broadcast(P)).then_inc(w_loaded, 16)
                        sp.dma_start(z_bias[:, HA:NZ], w["lparam"].rearrange("h l -> (h l)").partition_broadcast(P)
                                     ).then_inc(w_loaded, 16)
                        sp.dma_start(ln_g[:], w["ln_g"].partition_broadcast(P)).then_inc(w_loaded, 16)
                        sp.dma_start(ln_b[:], w["ln_b"].partition_broadcast(P)).then_inc(w_loaded, 16)

                    @block.tensor
                    def _(pe):
                        pe.wait_ge(w_loaded, 160)
                        for h in range(HA):
                            last = nc.tensor.matmul(bank[h // 4][:, h % 4 * P:h % 4 * P + P], wq[:, h, :], wk[:, h, :],
                                                    start=True, stop=True)
                        last.then_inc(qk_merged, 1)
                        for h in range(HA):
                            nc.tensor.transpose(bank[2 + h // 4][:, h % 4 * P:h % 4 * P + P],
                                                wo[:, h * P:(h + 1) * P], ident[:])
                        nc.tensor.transpose(bank[6][:, 0:NZ], wz[:, :], ident[0:NZ, 0:NZ]).then_inc(wo_transposed, 1)
                        pe.wait_ge(woT_ready, 2)
                        for h in range(HA):
                            last = nc.tensor.matmul(bank[4 + h // 4][:, h % 4 * P:h % 4 * P + P], wv[:, h, :],
                                                    woT[:, h, :], start=True, stop=True)
                        last.then_inc(vo_merged, 1)

                    @block.scalar
                    def _(act):
                        act.wait_ge(qk_merged, 1)
                        for g in range(2):
                            nc.scalar.activation(wqk[:, 4 * g:4 * g + 4, :], bank[g][:].rearrange(
                                "p (h d) -> p h d", h=4), ACT.Copy).then_inc(folded, 1)
                        act.wait_ge(vo_merged, 1)
                        for g in range(2):
                            nc.scalar.activation(wvo[:, g * 512:(g + 1) * 512], bank[4 + g][:],
                                                 ACT.Copy).then_inc(folded, 1)

                    @block.vector
                    def _(dve):
                        dve.wait_ge(wo_transposed, 1)
                        for g in range(2):
                            nc.vector.tensor_copy(woT[:, 4 * g:4 * g + 4, :], bank[2 + g][:].rearrange(
                                "p (h d) -> p h d", h=4)).then_inc(woT_ready, 1)
                        nc.vector.tensor_copy(wzT[:], bank[6][:, 0:NZ]).then_inc(folded, 1)

                z = sb("z", [P, B, NZ])
                z_abs = sb("z_abs", [P, B, NZ])
                z_exp = sb("z_exp", [P, B, NZ])
                sp_z = sb("softplus", [P, B, NZ])
                xqk = sb("xqk", [P, HA, BT])
                xvo = sb("xvo", [P, B, HA * D])
                decay = sb("decay", [P, B, HA, T])
                lam = sb("lam", [P, B, HA, T])
                lamw = sb("lamw", [P, B, HA, T])
                att = sb("att", [P, B, HA, T])
                attT = sb("attT", [P, B, HA, T])
                y = sb("y", [P, B, D])
                scratch = nc.dram_tensor(f"{name}_lam_scratch", [B, T * HA * T], F32)
                z_projected, z_ready, abs_ready, exp_ready, ln_ready, gates_ready = (
                    sem(n) for n in ("z_projected", "z_ready", "abs_ready", "exp_ready", "ln_ready", "gates_ready"))
                xqk_projected, xqk_ready, xvo_projected, xvo_ready = (
                    sem(n) for n in ("xqk_projected", "xqk_ready", "xvo_projected", "xvo_ready"))
                decay_summed, decay_ready, lam_ready, lam_stored, lamw_ready = (
                    sem(n) for n in ("decay_summed", "decay_ready", "lam_ready", "lam_stored", "lamw_ready"))
                dl_ready, scored, att_ready, att_transposed, attT_ready, summed = (
                    sem(n) for n in ("dl_ready", "scored", "att_ready", "att_transposed", "attT_ready", "summed"))
                y_steps, y_var_ready, y_rstd_ready = sem("y_steps"), sem("y_var_ready"), sem("y_rstd_ready")
                HALVES = [(b, g) for b in range(B) for g in range(2)]
                SCALE = P ** -0.5

                with nc.Block() as block:
                    @block.tensor
                    def _(pe):
                        for b in range(B):
                            last = nc.tensor.matmul(bank[7][:, b * NZ:(b + 1) * NZ], xT[:, b * P:(b + 1) * P], wzT[:],
                                                    start=True, stop=True)
                        last.then_inc(z_projected, 1)
                        for h in range(HA):
                            if h >= 2:
                                pe.wait_ge(xqk_ready, h - 1)
                            nc.tensor.matmul(bank[h % 2][:], wqk[:, h, :], xT[:], start=True,
                                             stop=True).then_inc(xqk_projected, 1)
                        pe.wait_ge(gates_ready, 1)
                        for i, (b, g) in enumerate(HALVES):
                            if i >= 2:
                                pe.wait_ge(decay_ready, i - 1)
                            ps = bank[2 + i % 2]
                            nc.tensor.matmul(ps[:], ident_bf[:], bcast(future_bf[:], 1, 4), start=True, stop=False,
                                             skip_group_check=True)
                            for j in range(4):
                                h = 4 * g + j
                                nc.tensor.matmul(ps[:, j * P:(j + 1) * P], repeat(sp_z[:, b, h:h + 1], P),
                                                 upper[:], start=False, stop=False, skip_group_check=True)
                            nc.tensor.matmul(ps[:], neg_upper[:], bcast(sp_z[:, b, 4 * g:4 * g + 4], 2, P),
                                             start=False, stop=True, skip_group_check=True).then_inc(decay_summed, 1)
                        pe.wait_ge(xqk_ready, HA)
                        for i, (b, g) in enumerate(HALVES):
                            if i >= 2:
                                pe.wait_ge(xvo_ready, i - 1)
                            nc.tensor.matmul(bank[i % 2][:], xT[:, b * P:(b + 1) * P], wvo[:, g * 512:(g + 1) * 512],
                                             start=True, stop=True).then_inc(xvo_projected, 1)
                        for i, (b, g) in enumerate(HALVES):
                            if i >= 2:
                                pe.wait_ge(att_ready, i - 1)
                            for j in range(4):
                                h = 4 * g + j
                                last = nc.tensor.matmul(bank[4 + i % 2][:, j * P:(j + 1) * P],
                                                        xqk[:, h, b * P:(b + 1) * P], xT[:, b * P:(b + 1) * P],
                                                        start=True, stop=True)
                            last.then_inc(scored, 1)
                        pe.wait_ge(decay_ready, 8)
                        for i, (b, g) in enumerate(HALVES):
                            pe.wait_ge(att_ready, i + 1)
                            if i >= 2:
                                pe.wait_ge(attT_ready, i - 1)
                            for j in range(4):
                                last = nc.tensor.transpose(bank[2 + i % 2][:, j * P:(j + 1) * P],
                                                           att[:, b, 4 * g + j, :], ident[:])
                            last.then_inc(att_transposed, 1)
                        pe.wait_ge(xvo_ready, 8)
                        for i, (b, g) in enumerate(HALVES):
                            pe.wait_ge(attT_ready, i + 1)
                            for j in range(4):
                                h = 4 * g + j
                                last = nc.tensor.matmul(bank[6][:, b * D:(b + 1) * D], attT[:, b, h, :],
                                                        xvo[:, b, h * D:(h + 1) * D], start=(h == 0), stop=(h == HA - 1))
                        last.then_inc(summed, 1)

                    @block.scalar
                    def _(act):
                        act.wait_ge(z_ready, 1)
                        nc.scalar.activation(z_abs[:], z[:], ACT.Abs).then_inc(abs_ready, 1)
                        act.wait_ge(abs_ready, 1)
                        nc.scalar.activation(z_exp[:], z_abs[:], ACT.Exp, scale=-1.0).then_inc(exp_ready, 1)
                        act.wait_ge(exp_ready, 1)
                        nc.scalar.activation(z_exp[:], z_exp[:], ACT.Ln, bias=1.0).then_inc(ln_ready, 1)
                        for h in range(HA):
                            act.wait_ge(xqk_projected, h + 1)
                            nc.scalar.activation(xqk[:, h, :], bank[h % 2][:], ACT.Copy).then_inc(xqk_ready, 1)
                        for i, (b, g) in enumerate(HALVES):
                            act.wait_ge(decay_summed, i + 1)
                            nc.scalar.activation(decay[:, b, 4 * g:4 * g + 4, :], bank[2 + i % 2][:].rearrange(
                                "p (h s) -> p h s", h=4), ACT.Exp).then_inc(decay_ready, 1)
                        for i, (b, g) in enumerate(HALVES):
                            act.wait_ge(xvo_projected, i + 1)
                            nc.scalar.activation(xvo[:, b, g * 512:(g + 1) * 512], bank[i % 2][:],
                                                 ACT.Copy).then_inc(xvo_ready, 1)
                        for i, (b, g) in enumerate(HALVES):
                            act.wait_ge(att_transposed, i + 1)
                            nc.scalar.activation(attT[:, b, 4 * g:4 * g + 4, :], bank[2 + i % 2][:].rearrange(
                                "p (h s) -> p h s", h=4), ACT.Copy).then_inc(attT_ready, 1)

                    @block.sync
                    def _(sp):
                        for b in range(B):
                            sp.wait_ge(lam_ready, LVU)
                            sp.dma_start(scratch[b].rearrange("(t c) -> t c", t=T),
                                         lam[:, b, :, :].rearrange("p h c -> p (h c)")).then_inc(lam_stored, 16)
                        for b in range(B):
                            sp.wait_ge(lam_stored, 16 * B)
                            skewed = bass.AP(scratch, b * T * HA * T + T - 1,
                                             [(HA * T - 1, T), (T, HA), (1, T)])
                            sp.dma_start(lamw[:, b, :, :], skewed).then_inc(lamw_ready, 16)

                    @block.vector
                    def _(dve):
                        dve.wait_ge(z_projected, 1)
                        nc.vector.tensor_tensor(z[:], bank[7][:, 0:B * NZ].rearrange("p (b n) -> p b n", b=B),
                                                bcast(z_bias[:], 1, B), ALU.add).then_inc(z_ready, 1)
                        dve.wait_ge(ln_ready, 1)
                        nc.vector.scalar_tensor_tensor(out=sp_z[:], in0=z[:], scalar=0.0, in1=z_exp[:], op0=ALU.max,
                                                       op1=ALU.add).then_inc(gates_ready, 1)
                        dve.wait_ge(gates_ready, 1)
                        lvs = sp_z[:, :, HA:NZ].rearrange("p b (h l) -> p b h l", h=HA)
                        for l in range(LVU):
                            d0, d1 = (0, 1) if l == 0 else (2 ** (l - 1), 2 ** l)
                            nc.vector.tensor_copy(lam[:, :, :, T - d1:T - d0],
                                                  bcast(lvs[:, :, :, l], 3, d1 - d0)).then_inc(lam_ready, 1)
                        for b in range(B):
                            dve.wait_ge(decay_ready, 2 * b + 2)
                            dve.wait_ge(lamw_ready, 16 * B)
                            nc.vector.tensor_tensor(lamw[:, b, :, :], lamw[:, b, :, :], decay[:, b, :, :],
                                                    ALU.mult).then_inc(dl_ready, 1)
                        for i, (b, g) in enumerate(HALVES):
                            dve.wait_ge(scored, i + 1)
                            dve.wait_ge(dl_ready, b + 1)
                            hs = slice(4 * g, 4 * g + 4)
                            nc.vector.scalar_tensor_tensor(
                                out=att[:, b, hs, :], in0=bank[4 + i % 2][:].rearrange("p (h s) -> p h s", h=4),
                                scalar=SCALE, in1=lamw[:, b, hs, :], op0=ALU.mult, op1=ALU.mult).then_inc(att_ready, 1)
                        dve.wait_ge(summed, 1)
                        chain = Chain(dve, y_steps)
                        chain(nc.vector.tensor_tensor(y[:], bank[6][:].rearrange("p (b d) -> p b d", b=B), xn[:],
                                                      ALU.add))
                        for b in range(B):
                            nc.vector.bn_stats(bn[:, b, :], y[:, b, :]).then_inc(y_steps, 1)
                        dve.wait_ge(y_steps, 1 + B)
                        for b in range(B):
                            nc.vector.bn_aggr(mv[:, b, :], bn[:, b, :]).then_inc(y_steps, 1)
                        dve.wait_ge(y_steps, 1 + 2 * B)
                        nc.vector.tensor_scalar(var_eps[:], mv[:, :, 1], EPS, None, ALU.add).then_inc(y_var_ready, 1)
                        dve.wait_ge(y_rstd_ready, 1)
                        for b in range(B):
                            nc.vector.tensor_scalar(y[:, b, :], y[:, b, :], mv[:, b, 0:1], rstd[:, b:b + 1],
                                                    ALU.subtract, ALU.mult).then_inc(y_steps, 1)
                        chain.at = 1 + 3 * B
                        dve.wait_ge(y_steps, chain.at)
                        chain(nc.vector.tensor_tensor(y[:], y[:], bcast(ln_g[:], 1, B), ALU.mult))
                        chain(nc.vector.tensor_tensor(y[:], y[:], bcast(ln_b[:], 1, B), ALU.add))
                        chain(nc.vector.tensor_tensor(x[:], x[:], y[:], ALU.add))

                    @block.gpsimd
                    def _(pool):
                        pool.wait_ge(y_var_ready, 1)
                        nc.gpsimd.tensor_tensor(rstd[:], var_eps[:], minus_half[:], ALU.pow).then_inc(y_rstd_ready, 1)

        up_summed, silu_ready, hid_ready, down_summed, added, b_down_summed = (
            sem(n) for n in ("up_summed", "silu_ready", "hid_ready", "down_summed", "added", "b_down_summed"))

        def expert_sum(name, up1, up2, down, bias1, bias2, gates, b_down, before):
            with ExitStack() as c2:
                act1 = c2.enter_context(nc.sbuf_tensor(f"{name}_act1", [P, 3, BT], F32))
                hid = c2.enter_context(nc.sbuf_tensor(f"{name}_hid", [P, 3, BT], F32))
                U = HM * E
                U0, E0, A0 = before * U, before * E, before * (E + 1)
                first = 1 if b_down else 0
                with nc.Block() as block:
                    @block.tensor
                    def _(pe):
                        def up(u):
                            e, m = divmod(u, HM)
                            if u >= 3:
                                pe.wait_ge(hid_ready, U0 + u - 2)
                            nc.tensor.matmul(bank[2 * (u % 3)][:], up1(e, m), xT[:], start=True, stop=True)
                            nc.tensor.matmul(bank[2 * (u % 3) + 1][:], up2(e, m), xT[:], start=True,
                                             stop=True).then_inc(up_summed, 1)

                        def down_(u):
                            e, m = divmod(u, HM)
                            pe.wait_ge(hid_ready, U0 + u + 1)
                            if m == 0 and e + first >= 2:
                                pe.wait_ge(added, A0 + e + first - 1)
                            for b in range(B):
                                last = nc.tensor.matmul(bank[6 + (e + first) % 2][:, b * D:(b + 1) * D],
                                                        hid[:, u % 3, b * P:(b + 1) * P], down(e, m),
                                                        start=(m == 0 and b == 0), stop=(m == HM - 1 and b == B - 1),
                                                        skip_group_check=True)
                            if m == HM - 1:
                                last.then_inc(down_summed, 1)

                        up(0)
                        if b_down:
                            gT, rows = b_down
                            for b in range(B):
                                last = nc.tensor.matmul(bank[6][:, b * D:(b + 1) * D], gT[:, b * P:(b + 1) * P], rows[:],
                                                        start=(b == 0), stop=(b == B - 1), skip_group_check=True)
                            last.then_inc(b_down_summed, 1)
                        up(1)
                        for u in range(2, U + 2):
                            if u < U:
                                up(u)
                            down_(u - 2)

                    @block.scalar
                    def _(act):
                        for u in range(U):
                            e, m = divmod(u, HM)
                            act.wait_ge(up_summed, U0 + u + 1)
                            if u >= 3:
                                act.wait_ge(hid_ready, U0 + u - 2)
                            nc.scalar.activation(act1[:, u % 3, :], bank[2 * (u % 3)][:], ACT.Silu,
                                                 bias=bias1(e, m) if bias1 else 0.0).then_inc(silu_ready, 1)

                    @block.vector
                    def _(dve):
                        def add(e):
                            dve.wait_ge(down_summed, E0 + e + 1)
                            if e + first >= 1:
                                dve.wait_ge(added, A0 + e + first)
                            for b in range(B):
                                last = nc.vector.scalar_tensor_tensor(
                                    out=x[:, b, :], in0=bank[6 + (e + first) % 2][:, b * D:(b + 1) * D],
                                    scalar=gates(b, e), in1=x[:, b, :], op0=ALU.mult, op1=ALU.add)
                            last.then_inc(added, 1)

                        if b_down:
                            dve.wait_ge(b_down_summed, 1)
                            nc.vector.tensor_tensor(x[:], bank[6][:].rearrange("p (b d) -> p b d", b=B), x[:],
                                                    ALU.add).then_inc(added, 1)
                        for u in range(U):
                            e, m = divmod(u, HM)
                            dve.wait_ge(silu_ready, U0 + u + 1)
                            if u >= 3:
                                if (u - 3) % HM == HM - 1:
                                    dve.wait_ge(down_summed, E0 + (u - 3) // HM + 1)
                                else:
                                    dve.wait_ge(up_summed, U0 + u + 1)
                            if bias2:
                                nc.vector.scalar_tensor_tensor(
                                    out=hid[:, u % 3, :], in0=bank[2 * (u % 3) + 1][:], scalar=bias2(e, m),
                                    in1=act1[:, u % 3, :], op0=ALU.add, op1=ALU.mult).then_inc(hid_ready, 1)
                            else:
                                nc.vector.tensor_tensor(hid[:, u % 3, :], bank[2 * (u % 3) + 1][:], act1[:, u % 3, :],
                                                        ALU.mult).then_inc(hid_ready, 1)
                            if m == HM - 1 and e >= 1:
                                add(e - 1)
                        add(E - 1)

        def lora_ffn(name, w):
            with ExitStack() as c2:
                def sb(n, shape, dt=F32):
                    return c2.enter_context(nc.sbuf_tensor(f"{name}_{n}", shape, dt))

                def sem(n):
                    return ctx.enter_context(nc.semaphore(f"{name}_{n}"))

                EM = E * HM
                up_rows = [sb("w1", [P, EM, D]), sb("w3", [P, EM, D])]
                up_a = [sb("a1", [R, E, D]), sb("a3", [R, E, D])]
                up_b = [sb("b1l", [P, EM, R]), sb("b3l", [P, EM, R])]
                down_rows = sb("w2", [P, E, HID])
                down_a, down_b = sb("a2", [R, E, HID]), sb("b2l", [P, E, R])
                bias_rows = sb("bias_rows", [2 * EM, P])
                b_down = sb("b_down", [E, D])
                wg = sb("wg", [E, D])
                upT = [sb("w1T", [P, EM, P]), sb("w3T", [P, EM, P])]
                downT = sb("w2T", [P, EM, D])
                up_bT = [sb("b1T", [R, EM, P]), sb("b3T", [R, EM, P])]
                down_bT = sb("b2T", [R, E, P])
                biases = sb("biases", [P, 2 * EM])
                wgT = sb("wgT", [P, E])
                w_loaded = sem("w_loaded")
                turned, turned_out, folded, folded_out = (
                    sem(n) for n in ("turned", "turned_out", "folded", "folded_out"))

                with nc.Block() as block:
                    @block.sync
                    def _(sp):
                        n = 0
                        for k, (ww, aa, bb) in enumerate((("w1", "a1", "b1l"), ("w3", "a3", "b3l"))):
                            sp.dma_start(up_rows[k][:], w[ww].rearrange("e (m p) d -> p (e m) d", p=P)).then_inc(w_loaded, 16)
                            sp.dma_start(up_a[k][:], w[aa].rearrange("e r d -> r e d")).then_inc(w_loaded, 16)
                            sp.dma_start(up_b[k][:], w[bb].rearrange("e (m p) r -> p (e m) r", p=P)).then_inc(w_loaded, 16)
                        sp.dma_start(down_rows[:], w["w2"].rearrange("e d h -> d e h")).then_inc(w_loaded, 16)
                        sp.dma_start(down_a[:], w["a2"].rearrange("e r h -> r e h")).then_inc(w_loaded, 16)
                        sp.dma_start(down_b[:], w["b2l"].rearrange("e d r -> d e r")).then_inc(w_loaded, 16)
                        sp.dma_start(bias_rows[0:EM, :], w["b1"].rearrange("e (m p) -> (e m) p", p=P)).then_inc(w_loaded, 16)
                        sp.dma_start(bias_rows[EM:2 * EM, :], w["b3"].rearrange("e (m p) -> (e m) p", p=P)).then_inc(w_loaded, 16)
                        sp.dma_start(b_down[:], w["b2"]).then_inc(w_loaded, 16)
                        sp.dma_start(wg[:], w["wg"]).then_inc(w_loaded, 16)

                    turns = [(up_b[k][:, i, :], up_bT[k][:, i, :]) for k in range(2) for i in range(EM)]
                    turns += [(down_b[:, e, :], down_bT[:, e, :]) for e in range(E)]
                    folds = [(up_rows[k][:, i, :], up_a[k][:, i // HM, :], up_bT[k][:, i, :], False)
                             for k in range(2) for i in range(EM)]
                    folds += [(down_rows[:, i // HM, i % HM * P:(i % HM + 1) * P],
                               down_a[:, i // HM, i % HM * P:(i % HM + 1) * P], down_bT[:, i // HM, :], True)
                              for i in range(EM)]
                    TG, FG = len(turns) // 4, len(folds) // 4

                    @block.tensor
                    def _(pe):
                        pe.wait_ge(w_loaded, 16 * 13)
                        nc.tensor.transpose(bank[6][:, 0:2 * EM], bias_rows[:, :], ident[0:2 * EM, 0:2 * EM])
                        nc.tensor.transpose(bank[6][:, 2 * EM:2 * EM + E], wg[:, :],
                                            ident[0:E, 0:E]).then_inc(turned, 1)
                        for g in range(TG):
                            if g >= 2:
                                pe.wait_ge(turned_out, g)
                            for j in range(4):
                                last = nc.tensor.transpose(bank[g % 2][0:R, j * P:(j + 1) * P], turns[4 * g + j][0],
                                                           ident[:])
                            last.then_inc(turned, 1)
                        pe.wait_ge(turned_out, TG + 1)
                        for g in range(FG):
                            if g >= 2:
                                pe.wait_ge(folded_out, g - 1)
                            for j in range(4):
                                rows, a, bT, _ = folds[4 * g + j]
                                ps = bank[2 + g % 2][:, j * P:(j + 1) * P]
                                nc.tensor.matmul(ps, rows, ident[:], start=True, stop=False)
                                last = nc.tensor.matmul(ps, a, bT, start=False, stop=True)
                            last.then_inc(folded, 1)

                    @block.scalar
                    def _(act):
                        for g in range(FG):
                            act.wait_ge(folded, g + 1)
                            k, i = divmod(4 * g, EM)
                            dst = (upT[0], upT[1], downT)[k]
                            nc.scalar.activation(dst[:, i:i + 4, :], bank[2 + g % 2][:].rearrange(
                                "p (i h) -> p i h", i=4), ACT.Copy).then_inc(folded_out, 1)

                    @block.vector
                    def _(dve):
                        dve.wait_ge(turned, 1)
                        nc.vector.tensor_copy(biases[:], bank[6][:, 0:2 * EM])
                        nc.vector.tensor_copy(wgT[:], bank[6][:, 2 * EM:2 * EM + E]).then_inc(turned_out, 1)
                        for g in range(TG):
                            dve.wait_ge(turned, g + 2)
                            k, i = divmod(4 * g, EM)
                            dst = (up_bT[0], up_bT[1], down_bT)[k]
                            nc.vector.tensor_copy(dst[:, i:i + 4, :], bank[g % 2][0:R, :].rearrange(
                                "p (i h) -> p i h", i=4)).then_inc(turned_out, 1)

                logits = sb("logits", [P, B, E])
                nmax, den = sb("nmax", [P, B]), sb("den", [P, B])
                top = sb("top", [P, B, 8])
                at = sb("at", [P, B, 8], U32)
                atf = sb("atf", [P, B, 8])
                wsum = sb("wsum", [P, B])
                hot = sb("hot", [P, B, E])
                gates = sb("gates", [P, B, E])
                numbers = sb("numbers", [P, E])
                gatesT = sb("gatesT", [E, BT])
                routed, gsteps, lmax_ready, lexp_ready, gates_ready, gates_turned = (
                    sem(n) for n in ("routed", "gsteps", "lmax_ready", "lexp_ready", "gates_ready", "gates_turned"))
                numbers_ready = sem("numbers_ready")
                with nc.Block() as block:
                    @block.gpsimd
                    def _(pool):
                        nc.gpsimd.iota(numbers[:], pattern=[[1, E]], base=0, channel_multiplier=0,
                                       allow_small_or_imprecise_dtypes=True).then_inc(numbers_ready, 1)

                    @block.tensor
                    def _(pe):
                        for b in range(B):
                            last = nc.tensor.matmul(bank[0][:, b * E:(b + 1) * E], xT[:, b * P:(b + 1) * P], wgT[:],
                                                    start=True, stop=True)
                        last.then_inc(routed, 1)
                        pe.wait_ge(gates_ready, 1)
                        for b in range(B):
                            last = nc.tensor.transpose(bank[1][0:E, b * P:(b + 1) * P], gates[:, b, :], ident[:])
                        last.then_inc(gates_turned, 1)

                    @block.scalar
                    def _(act):
                        for b in range(B):
                            act.wait_ge(lmax_ready, 1)
                            nc.scalar.activation(logits[:, b, :], bank[0][:, b * E:(b + 1) * E], ACT.Exp,
                                                 bias=nmax[:, b:b + 1], accum_out=den[:, b:b + 1]).then_inc(lexp_ready, 1)

                    @block.vector
                    def _(dve):
                        dve.wait_ge(routed, 1)
                        nc.vector.tensor_reduce(nmax[:], bank[0][:, 0:B * E].rearrange("p (b e) -> p b e", b=B), AX_X,
                                                ALU.max, negate=True).then_inc(lmax_ready, 1)
                        dve.wait_ge(lexp_ready, B)
                        dve.wait_ge(numbers_ready, 1)
                        chain = Chain(dve, gsteps)
                        chain(nc.vector.reciprocal(den[:], den[:]))
                        chain(nc.vector.tensor_tensor(logits[:], logits[:], bcast(den[:], 2, E), ALU.mult))
                        for b in range(B):
                            chain(nc.vector.max(top[:, b, :], logits[:, b, :]))
                            chain(nc.vector.max_index(at[:, b, :], top[:, b, :], logits[:, b, :]))
                        chain(nc.vector.tensor_copy(atf[:], at[:]))
                        chain(nc.vector.tensor_tensor(wsum[:], top[:, :, 0], top[:, :, 1], ALU.add))
                        chain(nc.vector.reciprocal(wsum[:], wsum[:]))
                        chain(nc.vector.tensor_tensor(top[:], top[:], bcast(wsum[:], 2, 8), ALU.mult))
                        for k, dst in ((0, gates), (1, hot)):
                            chain(nc.vector.tensor_tensor(dst[:], bcast(numbers[:], 1, B), bcast(atf[:, :, k], 2, E),
                                                          ALU.is_equal))
                            chain(nc.vector.tensor_tensor(dst[:], dst[:], bcast(top[:, :, k], 2, E), ALU.mult))
                        nc.vector.tensor_tensor(gates[:], gates[:], hot[:], ALU.add).then_inc(gates_ready, 1)
                        dve.wait_ge(gates_turned, 1)
                        nc.vector.tensor_copy(gatesT[:], bank[1][0:E, :])

                expert_sum(name, lambda e, m: upT[0][:, HM * e + m, :], lambda e, m: upT[1][:, HM * e + m, :],
                           lambda e, m: downT[:, HM * e + m, :],
                           lambda e, m: biases[:, HM * e + m:HM * e + m + 1],
                           lambda e, m: biases[:, EM + HM * e + m:EM + HM * e + m + 1],
                           lambda b, e: gates[:, b, e:e + 1], (gatesT, b_down), 0)

        def banded_attention(name, w):
            with ExitStack() as c2:
                def sb(n, shape, dt=F32):
                    return c2.enter_context(nc.sbuf_tensor(f"{name}_{n}", shape, dt))

                def sem(n):
                    return ctx.enter_context(nc.semaphore(f"{name}_{n}"))

                BAND = D // 4
                qkv_w = sb("qkv_w", [P, 3 * D])
                w_high = sb("w_high", [P, 3 * D])
                w_low = [sb("w_low1", [P, 3 * D], F16), sb("w_low2", [P, 3 * D], F16)]
                xT16 = sb("xT16", [P, BT], F16)
                out_w, out_wT, out_b = sb("out_w", [P, D]), sb("out_wT", [P, D]), sb("out_b", [P, D])
                part = [sb("part1", [P, BT], F16), sb("part2", [P, BT], F16)]
                qkv = [sb("qT", [P, BT]), sb("kT", [P, BT]), sb("v", [P, BT])]
                probs, pT, yT = sb("probs", [P, B, T]), sb("pT", [P, B, T]), sb("yT", [P, BT])
                nmax, den = sb("nmax", [P, B]), sb("den", [P, B])
                loaded, cleared, bands_ready, x16_ready, turned, out_wT_ready = (
                    sem(n) for n in ("loaded", "cleared", "bands_ready", "x16_ready", "turned", "out_wT_ready"))
                projected, part_ready, sum_ready, qkv_ready = (
                    sem(n) for n in ("projected", "part_ready", "sum_ready", "qkv_ready"))
                scored, max_ready, exp_ready, p_turned, pT_ready, mixed, yT_ready, done = (
                    sem(n) for n in ("scored", "max_ready", "exp_ready", "p_turned", "pT_ready", "mixed", "yT_ready",
                                     "done"))
                osteps = sem("osteps")
                SCALE = D ** -0.5
                with nc.Block() as block:
                    @block.sync
                    def _(sp):
                        sp.dma_start(qkv_w[:], w["qkv"]).then_inc(loaded, 16)
                        sp.dma_start(out_w[:], w["out_w"]).then_inc(loaded, 16)
                        sp.dma_start(out_b[:], w["out_b"].partition_broadcast(P)).then_inc(loaded, 16)

                    @block.gpsimd
                    def _(pool):
                        nc.gpsimd.memset(w_high[:], 0.0).then_inc(cleared, 1)
                        nc.gpsimd.memset(w_low[0][:], 0.0).then_inc(cleared, 1)
                        nc.gpsimd.memset(w_low[1][:], 0.0).then_inc(cleared, 1)

                    @block.vector
                    def _(dve):
                        dve.wait_ge(loaded, 48)
                        dve.wait_ge(cleared, 3)
                        nc.vector.tensor_copy(w_high[BAND:2 * BAND, :], qkv_w[BAND:2 * BAND, :]).then_inc(bands_ready, 1)
                        nc.vector.tensor_copy(w_high[2 * BAND:3 * BAND, :], qkv_w[2 * BAND:3 * BAND, :]).then_inc(bands_ready, 1)
                        nc.vector.tensor_copy(w_low[0][0:BAND, :], qkv_w[0:BAND, :]).then_inc(bands_ready, 1)
                        nc.vector.tensor_copy(w_low[1][3 * BAND:D, :], qkv_w[3 * BAND:D, :]).then_inc(bands_ready, 1)
                        nc.vector.tensor_copy(xT16[:], xT[:]).then_inc(x16_ready, 1)
                        dve.wait_ge(turned, 1)
                        nc.vector.tensor_copy(out_wT[:], bank[7][:, 0:D]).then_inc(out_wT_ready, 1)
                        for i in range(3):
                            dve.wait_ge(part_ready, 2 * i + 1)
                            nc.vector.tensor_tensor(qkv[i][:], bank[1 + 3 * (i % 2)][:], part[0][:], ALU.add).then_inc(sum_ready, 1)
                            dve.wait_ge(sum_ready, i + 1)
                            dve.wait_ge(part_ready, 2 * i + 2)
                            nc.vector.tensor_tensor(qkv[i][:], qkv[i][:], part[1][:], ALU.add).then_inc(qkv_ready, 1)
                        dve.wait_ge(scored, 1)
                        nc.vector.tensor_reduce(nmax[:], bank[6][:].rearrange("p (b k) -> p b k", b=B), AX_X, ALU.max,
                                                negate=True).then_inc(osteps, 1)
                        dve.wait_ge(osteps, 1)
                        nc.vector.tensor_scalar(nmax[:], nmax[:], SCALE, None, ALU.mult).then_inc(max_ready, 1)
                        dve.wait_ge(exp_ready, B)
                        nc.vector.reciprocal(den[:], den[:]).then_inc(osteps, 1)
                        nc.vector.tensor_tensor(x[:], x[:], bcast(out_b[:], 1, B), ALU.add).then_inc(osteps, 1)
                        dve.wait_ge(osteps, 3)
                        dve.wait_ge(done, 1)
                        for b in range(B):
                            nc.vector.scalar_tensor_tensor(out=x[:, b, :], in0=bank[3][:, b * D:(b + 1) * D],
                                                           scalar=den[:, b:b + 1], in1=x[:, b, :], op0=ALU.mult,
                                                           op1=ALU.add)

                    @block.tensor
                    def _(pe):
                        pe.wait_ge(loaded, 48)
                        nc.tensor.transpose(bank[7][:, 0:D], out_w[:], ident[:]).then_inc(turned, 1)
                        pe.wait_ge(bands_ready, 4)
                        pe.wait_ge(x16_ready, 1)
                        for i in range(3):
                            if i == 2:
                                pe.wait_ge(qkv_ready, 1)
                            for k, (ww, xx) in enumerate(((w_low[0], xT16), (w_high, xT), (w_low[1], xT16))):
                                ps = bank[k + 3 * (i % 2)]
                                if i < 2:
                                    last = nc.tensor.matmul(ps[:], ww[:, i * D:(i + 1) * D], xx[:], start=True, stop=True)
                                else:
                                    for b in range(B):
                                        last = nc.tensor.matmul(ps[:, b * D:(b + 1) * D], xx[:, b * P:(b + 1) * P],
                                                                ww[:, i * D:(i + 1) * D], start=True, stop=True)
                            last.then_inc(projected, 1)
                        pe.wait_ge(qkv_ready, 2)
                        for b in range(B):
                            cols = slice(b * P, (b + 1) * P)
                            last = nc.tensor.matmul(bank[6][:, cols], qkv[0][:, cols], qkv[1][:, cols], start=True, stop=True)
                        last.then_inc(scored, 1)
                        pe.wait_ge(exp_ready, B)
                        pe.wait_ge(out_wT_ready, 1)
                        for b in range(B):
                            last = nc.tensor.transpose(bank[7][:, b * P:(b + 1) * P], probs[:, b, :], ident[:])
                        last.then_inc(p_turned, 1)
                        pe.wait_ge(pT_ready, 1)
                        pe.wait_ge(qkv_ready, 3)
                        for b in range(B):
                            last = nc.tensor.matmul(bank[5][:, b * P:(b + 1) * P], qkv[2][:, b * D:(b + 1) * D], pT[:, b, :],
                                                    start=True, stop=True)
                        last.then_inc(mixed, 1)
                        pe.wait_ge(yT_ready, 1)
                        for b in range(B):
                            last = nc.tensor.matmul(bank[3][:, b * D:(b + 1) * D], yT[:, b * P:(b + 1) * P], out_wT[:],
                                                    start=True, stop=True)
                        last.then_inc(done, 1)

                    @block.scalar
                    def _(act):
                        for i in range(3):
                            act.wait_ge(projected, i + 1)
                            for k in range(2):
                                if i:
                                    act.wait_ge(qkv_ready, i)
                                nc.scalar.activation(part[k][:], bank[2 * k + 3 * (i % 2)][:], ACT.Copy).then_inc(part_ready, 1)
                        act.wait_ge(max_ready, 1)
                        for b in range(B):
                            nc.scalar.activation(probs[:, b, :], bank[6][:, b * P:(b + 1) * P], ACT.Exp, scale=SCALE,
                                                 bias=nmax[:, b:b + 1], accum_out=den[:, b:b + 1]).then_inc(exp_ready, 1)
                        act.wait_ge(p_turned, 1)
                        nc.scalar.activation(pT[:], bank[7][:].rearrange("p (b q) -> p b q", b=B), ACT.Copy).then_inc(pT_ready, 1)
                        act.wait_ge(mixed, 1)
                        nc.scalar.activation(yT[:], bank[5][:], ACT.Copy).then_inc(yT_ready, 1)

        def choice_ffn(name, w):
            with ExitStack() as c2:
                def sb(n, shape, dt=F32):
                    return c2.enter_context(nc.sbuf_tensor(f"{name}_{n}", shape, dt))

                def sem(n):
                    return ctx.enter_context(nc.semaphore(f"{name}_{n}"))

                up1, up2 = sb("wg", [P, E, HID]), sb("wu", [P, E, HID])
                down = sb("wd", [P, E * HM, D])
                gate_w = sb("gate_w", [P, E])
                aff, nmax, den = sb("aff", [P, B, E]), sb("nmax", [P, B]), sb("den", [P, B])
                loaded, routed, max_ready, exp_ready, steps = (
                    sem(n) for n in ("loaded", "routed", "max_ready", "exp_ready", "steps"))
                with nc.Block() as block:
                    @block.sync
                    def _(sp):
                        sp.dma_start(gate_w[:], w["gate_w"]).then_inc(loaded, 16)
                        sp.dma_start(up1[:], w["wg"].rearrange("e d i -> d e i")).then_inc(loaded, 16)
                        sp.dma_start(up2[:], w["wu"].rearrange("e d i -> d e i")).then_inc(loaded, 16)
                        sp.dma_start(down[:], w["wd"].rearrange("e (m p) d -> p (e m) d", p=P)).then_inc(loaded, 16)

                    @block.tensor
                    def _(pe):
                        pe.wait_ge(loaded, 64)
                        for b in range(B):
                            last = nc.tensor.matmul(bank[0][:, b * E:(b + 1) * E], xT[:, b * P:(b + 1) * P], gate_w[:],
                                                    start=True, stop=True)
                        last.then_inc(routed, 1)

                    @block.scalar
                    def _(act):
                        act.wait_ge(max_ready, 1)
                        for b in range(B):
                            nc.scalar.activation(aff[:, b, :], bank[0][:, b * E:(b + 1) * E], ACT.Exp,
                                                 bias=nmax[:, b:b + 1], accum_out=den[:, b:b + 1]).then_inc(exp_ready, 1)

                    @block.vector
                    def _(dve):
                        dve.wait_ge(routed, 1)
                        nc.vector.tensor_reduce(nmax[:], bank[0][:, 0:B * E].rearrange("p (b e) -> p b e", b=B), AX_X,
                                                ALU.max, negate=True).then_inc(max_ready, 1)
                        dve.wait_ge(exp_ready, B)
                        chain = Chain(dve, steps)
                        chain(nc.vector.reciprocal(den[:], den[:]))
                        chain(nc.vector.tensor_tensor(aff[:], aff[:], bcast(den[:], 2, E), ALU.mult))

                expert_sum(name, lambda e, m: up1[:, e, m * P:(m + 1) * P], lambda e, m: up2[:, e, m * P:(m + 1) * P],
                           lambda e, m: down[:, HM * e + m, :], None, None, lambda b, e: aff[:, b, e:e + 1], None, 1)


        layer_norm()
        cross_attention(0, dict(wq=A["L0_xattn_wq_k"], bq=A["L0_xattn_wq_b"], wk=A["L0_xattn_wk_k"],
                                    bk=A["L0_xattn_wk_b"], wv=A["L0_xattn_wv_k"], bv=A["L0_xattn_wv_b"],
                                    wo=A["L0_xattn_wo_k"], bo=A["L0_xattn_wo_b"]), True)
        layer_norm()
        retention("ret", dict(wq=A["L0_attn_Wq"], wk=A["L0_attn_Wk"], wv=A["L0_attn_Wv"], wo=A["L0_attn_Wo"],
                              wg=A["L0_attn_Wg"], bg=A["L0_attn_bg"], wdl=A["L0_attn_Wdl"],
                              lparam=A["L0_attn_Lparam"], ln_g=A["L0_attn_ln_g"], ln_b=A["L0_attn_ln_b"]))
        layer_norm()
        lora_ffn("ffn0", dict(w1=A["L0_ffn_W1"], w2=A["L0_ffn_W2"], w3=A["L0_ffn_W3"], a1=A["L0_ffn_A1"],
                              a2=A["L0_ffn_A2"], a3=A["L0_ffn_A3"], b1l=A["L0_ffn_B1"], b2l=A["L0_ffn_B2"],
                              b3l=A["L0_ffn_B3"], b1=A["L0_ffn_b1"], b2=A["L0_ffn_b2"], b3=A["L0_ffn_b3"],
                              wg=A["L0_ffn_Wg"]))
        layer_norm()
        cross_attention(1, dict(wq=A["L1_xattn_Wq"], bq=A["L1_xattn_bq"], wk=A["L1_xattn_Wk"],
                                    bk=A["L1_xattn_bk"], wv=A["L1_xattn_Wv"], bv=A["L1_xattn_bv"]), False)
        layer_norm()
        banded_attention("att1", dict(qkv=A["L1_attn_weight_qkv"], out_w=A["L1_attn_out_w"],
                                      out_b=A["L1_attn_out_b"]))
        layer_norm()
        choice_ffn("ffn1", dict(gate_w=A["L1_ffn_gate_w"], wg=A["L1_ffn_Wg"], wu=A["L1_ffn_Wu"],
                                wd=A["L1_ffn_Wd"]))

        with nc.Block() as block:
            @block.sync
            def _(sp):
                sp.dma_start(out.rearrange("b t d -> t b d"), x[:]).then_inc(x_moved, 16)
                sp.wait_ge(x_moved, 32)


_INS = [
    "x", "ctx_1024", "fside_BxSxS2_0", "mask_BxSxS2_ik1",
    "L0_xattn_wq_k", "L0_xattn_wq_b", "L0_xattn_wk_k", "L0_xattn_wk_b",
    "L0_xattn_wv_k", "L0_xattn_wv_b", "L0_xattn_wo_k", "L0_xattn_wo_b",
    "L0_attn_Wq", "L0_attn_Wk", "L0_attn_Wv", "L0_attn_Wg",
    "L0_attn_bg", "L0_attn_Wdl", "L0_attn_Lparam", "L0_attn_Wo",
    "L0_attn_ln_g", "L0_attn_ln_b", "L0_ffn_Wg", "L0_ffn_W1",
    "L0_ffn_b1", "L0_ffn_A1", "L0_ffn_B1", "L0_ffn_W2",
    "L0_ffn_b2", "L0_ffn_A2", "L0_ffn_B2", "L0_ffn_W3",
    "L0_ffn_b3", "L0_ffn_A3", "L0_ffn_B3", "L1_xattn_Wq",
    "L1_xattn_bq", "L1_xattn_Wk", "L1_xattn_bk", "L1_xattn_Wv",
    "L1_xattn_bv", "L1_attn_weight_qkv", "L1_attn_out_w", "L1_attn_out_b",
    "L1_ffn_gate_w", "L1_ffn_Wg", "L1_ffn_Wu", "L1_ffn_Wd",
]
_OUTS = [((4, 128, 128), "float32")]


def kernel(**inputs):
    import numpy as _np
    import concourse.bacc as _bacc
    from concourse import mybir as _mybir
    from concourse.bass_utils import run_bass_kernel_spmd as _run

    nc = _bacc.Bacc("TRN2", target_bir_lowering=False, num_devices=1)
    arrays, aps = {}, {}
    for name in _INS:
        a = _np.ascontiguousarray(inputs[name])
        arrays[f"in_{name}_dram"] = a
        aps[name] = nc.dram_tensor(f"in_{name}_dram", a.shape, _mybir.dt.from_np(a.dtype), kind="ExternalInput").ap()
    outs = []
    for i, (shape, dtype) in enumerate(_OUTS):
        dt = _mybir.dt.from_np(_np.dtype(dtype))
        outs.append(nc.dram_tensor(f"out_{i}_dram", shape, dt, kind="ExternalOutput").ap())
    perceiver_kernel(nc, aps, outs[0])
    r = _run(nc, [arrays], core_ids=[0])
    return r.results[0]["out_0_dram"]
```

```python
from contextlib import ExitStack

import concourse.bass as bass
from concourse import mybir

ALU = mybir.AluOpType
ACT = mybir.ActivationFunctionType
F32 = mybir.dt.float32
F16 = mybir.dt.float16
BF16 = mybir.dt.bfloat16
I32 = mybir.dt.int32
U32 = mybir.dt.uint32
AX_X = mybir.AxisListType.X

P = 128
BIG_NEG = -1.0e30
EPS = 1e-5


def bcast(ap, axis, n):
    dims = list(ap.ap)
    dims.insert(axis, (0, n))
    return bass.AP(ap.tensor, ap.offset, dims)


def repeat(ap, n):
    return bass.AP(ap.tensor, ap.offset, [list(ap.ap)[0], (0, n)])


class Chain:

    def __init__(self, eng, sem, at=0):
        self.eng, self.sem, self.at = eng, sem, at

    def __call__(self, ins):
        ins.then_inc(self.sem, 1)
        self.at = self.at + 1
        self.eng.wait_ge(self.sem, self.at)


def perceiver_kernel(nc, A, out):
    B, T, D = A["x"].shape
    S2 = A["ctx_1024"].shape[1]
    NCH = S2 // P
    H, DH = 16, 8
    HA = A["L0_attn_Wg"].shape[0]
    LV = A["L0_attn_Lparam"].shape[1]
    LVU = 8
    E = A["L0_ffn_Wg"].shape[0]
    HID = A["L0_ffn_W1"].shape[1]
    R = A["L0_ffn_A1"].shape[1]
    HM = HID // P
    BT = B * T
    GK = 512
    NG = B * S2 // GK
    CPG = GK // P
    assert T == P and D == P and BT == 512 and HID == 2 * P

    with ExitStack() as ctx:
        def sb(name, shape, dt=F32):
            return ctx.enter_context(nc.sbuf_tensor(name, shape, dt))

        def sem(name):
            return ctx.enter_context(nc.semaphore(name))

        banks = ctx.enter_context(nc.psum_tensor("banks", [P, 8, 512], F32))
        bank = [banks[:, i, :] for i in range(8)]

        x = sb("x", [P, B, D])
        xn = sb("xn", [P, B, D])
        xT = sb("xT", [P, BT])
        ident = sb("ident", [P, P])
        ident_bf = sb("ident_bf", [P, P], BF16)
        upper = sb("upper", [P, P])
        neg_upper = sb("neg_upper", [P, P])
        future_bf = sb("future_bf", [P, P], BF16)
        head_rows = sb("head_rows", [P, H])
        quarter_rows = sb("quarter_rows", [P, 4])
        zero_bf = sb("zero_bf", [P, P], BF16)
        ones32 = sb("ones32", [P, 32])
        spread_den = sb("spread_den", [P, P])
        bn = sb("bn", [P, B, 6])
        mv = sb("mv", [P, B, 2])
        var_eps = sb("var_eps", [P, B])
        rstd = sb("rstd", [P, B])
        minus_half = sb("minus_half", [P, B])

        const_ready = sem("const_ready")
        pool_const_ready = sem("pool_const_ready")
        head_rows_ready = sem("head_rows_ready")
        x_moved = sem("x_moved")

        ident_dram = nc.dram_tensor("ident_scratch", [P, P], F32).ap()
        k_dram = nc.dram_tensor("k_scratch", [2, P, S2], F16).ap()
        ident_ready, ident_stored = sem("ident_ready"), sem("ident_stored")

        with nc.Block() as block:
            @block.sync
            def _(sp):
                sp.dma_start(x[:], A["x"].rearrange("b t d -> t b d")).then_inc(x_moved, 16)
                sp.wait_ge(ident_ready, 1)
                sp.dma_start(ident_dram, ident[:]).then_inc(ident_stored, 16)
                sp.wait_ge(ident_stored, 16)

            @block.vector
            def _(dve):
                chain = Chain(dve, const_ready)
                chain(nc.vector.memset(minus_half[:], -0.5))
                chain(nc.vector.memset(zero_bf[:], 0.0))
                chain(nc.vector.memset(ones32[:], 1.0))
                dve.wait_ge(head_rows_ready, 1)
                chain(nc.vector.tensor_reduce(quarter_rows[:], head_rows[:].rearrange("p (g j) -> p j g", g=4), AX_X,
                                              ALU.add))

            @block.gpsimd
            def _(pool):
                chain = Chain(pool, pool_const_ready)
                chain(nc.gpsimd.memset(ident[:], 0.0))
                chain(nc.gpsimd.affine_select(out=ident[:], in_=ident[:], compare_op=ALU.not_equal, fill=1.0,
                                              base=0, pattern=[[-1, P]], channel_multiplier=1))
                nc.gpsimd.engine_nop().then_inc(ident_ready, 1)
                chain(nc.gpsimd.tensor_copy(ident_bf[:], ident[:]))
                chain(nc.gpsimd.memset(upper[:], 1.0))
                chain(nc.gpsimd.affine_select(out=upper[:], in_=upper[:], compare_op=ALU.is_ge, fill=0.0,
                                              base=0, pattern=[[1, P]], channel_multiplier=-1))
                chain(nc.gpsimd.tensor_scalar(neg_upper[:], upper[:], -1.0, None, ALU.mult))
                chain(nc.gpsimd.memset(future_bf[:], 0.0))
                chain(nc.gpsimd.affine_select(out=future_bf[:], in_=future_bf[:], compare_op=ALU.is_ge, fill=BIG_NEG,
                                              base=0, pattern=[[-1, P]], channel_multiplier=1))
                chain(nc.gpsimd.memset(head_rows[:], 1.0))
                chain(nc.gpsimd.affine_select(out=head_rows[:], in_=head_rows[:], compare_op=ALU.is_ge, fill=0.0,
                                              base=0, pattern=[[-DH, H]], channel_multiplier=1))
                nc.gpsimd.affine_select(out=head_rows[:], in_=head_rows[:], compare_op=ALU.is_ge, fill=0.0,
                                        base=DH - 1, pattern=[[DH, H]],
                                        channel_multiplier=-1).then_inc(head_rows_ready, 1)
                chain(nc.gpsimd.memset(spread_den[:], 0.0))
                chain(nc.gpsimd.affine_select(out=spread_den[:].rearrange("p (c i) -> p c i", c=4),
                                              in_=spread_den[:].rearrange("p (c i) -> p c i", c=4),
                                              compare_op=ALU.not_equal, fill=1.0, base=-DH,
                                              pattern=[[-32, 4], [0, 32]], channel_multiplier=1))

        ln_stats, ln_var_ready, ln_rstd_ready, xn_ready, xn_transposed, xT_ready = (
            sem(n) for n in ("ln_stats", "ln_var_ready", "ln_rstd_ready", "xn_ready", "xn_transposed", "xT_ready"))

        norms = []

        def layer_norm(load):
            k = len(norms)
            norms.append(k)
            with nc.Block() as block:
                @block.sync
                def _(sp):
                    load(sp)

                @block.vector
                def _(dve):
                    dve.wait_ge(x_moved, 16)
                    for b in range(B):
                        nc.vector.bn_stats(bn[:, b, :], x[:, b, :]).then_inc(ln_stats, 1)
                    dve.wait_ge(ln_stats, (2 * k + 1) * B)
                    for b in range(B):
                        nc.vector.bn_aggr(mv[:, b, :], bn[:, b, :]).then_inc(ln_stats, 1)
                    dve.wait_ge(ln_stats, (2 * k + 2) * B)
                    nc.vector.tensor_scalar(var_eps[:], mv[:, :, 1], EPS, None, ALU.add).then_inc(ln_var_ready, 1)
                    dve.wait_ge(ln_rstd_ready, k + 1)
                    for b in range(B):
                        nc.vector.tensor_scalar(xn[:, b, :], x[:, b, :], mv[:, b, 0:1], rstd[:, b:b + 1],
                                                ALU.subtract, ALU.mult).then_inc(xn_ready, 1)

                @block.gpsimd
                def _(pool):
                    pool.wait_ge(ln_var_ready, k + 1)
                    nc.gpsimd.tensor_tensor(rstd[:], var_eps[:], minus_half[:], ALU.pow).then_inc(ln_rstd_ready, 1)

                @block.tensor
                def _(pe):
                    for b in range(B):
                        pe.wait_ge(xn_ready, k * B + b + 1)
                        last = nc.tensor.transpose(bank[0][:, b * P:(b + 1) * P], xn[:, b, :], ident[:])
                    last.then_inc(xn_transposed, 1)

                @block.scalar
                def _(act):
                    act.wait_ge(xn_transposed, k + 1)
                    nc.scalar.activation(xT[:], bank[0][:], ACT.Copy).then_inc(xT_ready, 1)

        general_sems = {}

        def general_attention(name, w, masked, safe):
            with ExitStack() as c2:
                def sb(n, shape, dt=F32):
                    return c2.enter_context(nc.sbuf_tensor(f"{name}_{n}", shape, dt))

                def sem(n):
                    if n not in general_sems:
                        general_sems[n] = ctx.enter_context(nc.semaphore(f"general_{n}"))
                    return general_sems[n]

                def unless_safe(on_engine):
                    def put(program):
                        @on_engine
                        def _(eng):
                            within = eng.value_load(safe[0:1, 0:1], min_val=0, max_val=1)
                            with eng.If(within < 1):
                                program(eng)
                    return put

                kT = sb("kT", [P, B * S2])
                v = sb("v", [P, B * NCH, D])
                qT = sb("qT", [P, BT])
                o = sb("o", [P, B, D])
                wq, wk, wv = (sb(n, [P, D]) for n in ("wq", "wk", "wv"))
                bq, bk = sb("bq", [P, 1]), sb("bk", [P, 1])
                bv = sb("bv", [P, D])
                wo, bo = sb("wo", [P, D]), sb("bo", [P, D])
                ctx_rows = sb("ctx_rows", [P, 2, CPG, D])
                ctxT = sb("ctxT", [P, 2, GK])
                w_loaded = sem("w_loaded")
                ctx_moved = [sem("ctx_moved0"), sem("ctx_moved1")]
                rows_transposed = sem("rows_transposed")
                ctxT_ready = sem("ctxT_ready")
                k_projected = sem("k_projected")
                v_projected = sem("v_projected")
                k_ready = sem("k_ready")
                v_ready = sem("v_ready")
                q_projected, q_ready = sem("q_projected"), sem("q_ready")
                n_w = 8 if masked else 6
                rows_dram = A["ctx_1024"].rearrange("b (g c p) d -> (b g) p c d", p=P, c=CPG)

                with nc.Block() as block:
                    @unless_safe(block.sync)
                    def _(sp):
                        for dst, src in ((wq, w["wq"]), (wk, w["wk"]), (wv, w["wv"])):
                            sp.dma_start(dst[:], src).then_inc(w_loaded, 16)
                        for dst, src in ((bq, w["bq"]), (bk, w["bk"])):
                            sp.dma_start(dst[:], src.rearrange("(d a) -> d a", a=1)).then_inc(w_loaded, 16)
                        sp.dma_start(bv[:], w["bv"].partition_broadcast(P)).then_inc(w_loaded, 16)
                        if masked:
                            sp.dma_start(wo[:], w["wo"]).then_inc(w_loaded, 16)
                            sp.dma_start(bo[:], w["bo"].partition_broadcast(P)).then_inc(w_loaded, 16)
                        for u in range(2):
                            sp.dma_start(ctx_rows[:, u, :, :], rows_dram[u]).then_inc(ctx_moved[u], 16)
                        with sp.Fori(1, NG // 2) as i:
                            for u in range(2):
                                sp.wait_ge(rows_transposed, 2 * i + u - 1)
                                sp.dma_start(ctx_rows[:, u, :, :], rows_dram[bass.ds(2 * i + u, 1)].rearrange(
                                    "a p c d -> p (a c) d")).then_inc(ctx_moved[u], 16)

                    @unless_safe(block.tensor)
                    def _(pe):
                        pe.sem_inc(v_projected, 1)
                        pe.wait_ge(w_loaded, 16 * n_w)
                        nc.tensor.matmul(bank[7][:], wq[:], xT[:], start=True, stop=True).then_inc(q_projected, 1)
                        with pe.Fori(0, NG // 2) as i:
                            for u in range(2):
                                pe.wait_ge(ctx_moved[u], 16 * i + 16)
                                pe.wait_ge(ctxT_ready, 2 * i + u + 1)
                                for c in range(CPG):
                                    last = nc.tensor.transpose(bank[u][:, c * P:(c + 1) * P],
                                                               ctx_rows[:, u, c, :], ident[:])
                                last.then_inc(rows_transposed, 1)
                                pe.wait_ge(ctxT_ready, 2 * i + u + 2)
                                pe.wait_ge(k_ready, 2 * i + u + 1)
                                nc.tensor.matmul(bank[2 + u][:], wk[:], ctxT[:, u, :], start=True,
                                                 stop=True).then_inc(k_projected, 1)
                                pe.wait_ge(v_ready, 2 * i + u + 1)
                                for c in range(CPG):
                                    last = nc.tensor.matmul(bank[4 + u][:, c * P:(c + 1) * P],
                                                            ctxT[:, u, c * P:(c + 1) * P], wv[:],
                                                            start=True, stop=True)
                                last.then_inc(v_projected, 1)

                    @unless_safe(block.scalar)
                    def _(act):
                        act.sem_inc(ctxT_ready, 1)
                        with act.Fori(0, NG // 2) as i:
                            for u in range(2):
                                act.wait_ge(rows_transposed, 2 * i + u + 1)
                                act.wait_ge(v_projected, 2 * i + u + 1)
                                nc.scalar.activation(ctxT[:, u, :], bank[u][:], ACT.Copy).then_inc(ctxT_ready, 1)

                    @unless_safe(block.vector)
                    def _(dve):
                        dve.sem_inc(k_ready, 1)
                        dve.sem_inc(v_ready, 1)
                        dve.wait_ge(w_loaded, 16 * n_w)
                        dve.wait_ge(q_projected, 1)
                        nc.vector.tensor_scalar(qT[:], bank[7][:], bq[:], None, ALU.add).then_inc(q_ready, 1)
                        with dve.Fori(0, NG // 2) as i:
                            for u in range(2):
                                dve.wait_ge(k_projected, 2 * i + u + 1)
                                nc.vector.tensor_scalar(kT[:, bass.ds((2 * i + u) * GK, GK)], bank[2 + u][:],
                                                        bk[:], None, ALU.add).then_inc(k_ready, 1)
                                dve.wait_ge(v_projected, 2 * i + u + 2)
                                nc.vector.tensor_tensor(
                                    v[:, bass.ds((2 * i + u) * CPG, CPG), :],
                                    bank[4 + u][:].rearrange("p (c d) -> p c d", c=CPG),
                                    bcast(bv[:], 1, CPG), ALU.add).then_inc(v_ready, 1)

                qz = sb("qz", [P, P])
                s = sb("s", [P, S2])
                neg = sb("neg", [P, S2])
                gp = sb("gp", [P, S2])
                mask_i = sb("mask_i", [P, S2], I32)
                pT = sb("pT", [P, NCH, P])
                nmax, den, rden = sb("nmax", [P, 1]), sb("den", [P, 1]), sb("rden", [P, 1])
                sides_loaded = sem("sides_loaded")
                q_head_ready = sem("q_head_ready")
                scored = sem("scored")
                neg_ready, s_ready, rden_ready = sem("neg_ready"), sem("s_ready"), sem("rden_ready")
                max_ready = sem("max_ready")
                exp_ready = sem("exp_ready")
                probs_ready = sem("probs_ready")
                p_transposed = sem("p_transposed")
                pT_ready = sem("pT_ready")
                head_out = sem("head_out")
                head_done = sem("head_done")
                SCALE = DH ** -0.5
                NB4 = S2 // 512
                with nc.Block() as block:
                    @unless_safe(block.sync)
                    def _(sp):
                        if masked:
                            with sp.Fori(0, B) as b:
                                sp.wait_ge(head_done, b * H + 1)
                                sp.dma_start(mask_i[:], A["mask_BxSxS2_ik1"][bass.ds(b, 1)].rearrange(
                                    "a q k -> q (a k)")).then_inc(sides_loaded, 16)
                                sp.dma_start(gp[:], A["fside_BxSxS2_0"][bass.ds(b, 1)].rearrange(
                                    "a q k -> q (a k)")).then_inc(sides_loaded, 16)

                    @unless_safe(block.vector)
                    def _(dve):
                        dve.sem_inc(head_done, 1)
                        with dve.Fori(0, B) as b:
                            if masked:
                                dve.wait_ge(sides_loaded, 32 * b + 32)
                                nc.vector.tensor_scalar(neg[:], mask_i[:], -1.0, 1.0e9, ALU.add,
                                                        ALU.mult).then_inc(neg_ready, 1)
                            with dve.Fori(0, H) as h:
                                n = b * H + h
                                nc.vector.tensor_scalar(qz[:], qT[:, bass.ds(b * P, P)],
                                                        head_rows[:, bass.ds(h, 1)], None,
                                                        ALU.mult).then_inc(q_head_ready, 1)
                                dve.wait_ge(scored, n + 1)
                                if masked:
                                    dve.wait_ge(neg_ready, b + 1)
                                for j in range(NB4):
                                    cols = slice(j * 512, (j + 1) * 512)
                                    if masked:
                                        last = nc.vector.scalar_tensor_tensor(
                                            out=s[:, cols], in0=bank[j][:], scalar=SCALE, in1=neg[:, cols],
                                            op0=ALU.mult, op1=ALU.add)
                                    else:
                                        last = nc.vector.tensor_scalar(s[:, cols], bank[j][:], SCALE, None, ALU.mult)
                                last.then_inc(s_ready, 1)
                                dve.wait_ge(s_ready, n + 1)
                                nc.vector.tensor_reduce(nmax[:], s[:], AX_X, ALU.max, negate=True).then_inc(max_ready, 1)
                                dve.wait_ge(exp_ready, n + 1)
                                nc.vector.reciprocal(rden[:], den[:]).then_inc(rden_ready, 1)
                                if masked:
                                    nc.vector.tensor_tensor(s[:], s[:], gp[:], ALU.mult).then_inc(probs_ready, 1)
                                dve.wait_ge(head_out, n + 1)
                                dve.wait_ge(rden_ready, n + 1)
                                nc.vector.tensor_scalar(o[:, bass.ds(b, 1), bass.ds(h * DH, DH)],
                                                        bank[6][:, bass.ds(h * DH, DH)], rden[:], None,
                                                        ALU.mult).then_inc(head_done, 1)

                    @unless_safe(block.tensor)
                    def _(pe):
                        with pe.Fori(0, B) as b:
                            with pe.Fori(0, H) as h:
                                n = b * H + h
                                pe.wait_ge(q_head_ready, n + 1)
                                for j in range(NB4):
                                    last = nc.tensor.matmul(bank[j][:], qz[:], kT[:, bass.ds(b * S2 + j * 512, 512)],
                                                            start=True, stop=True)
                                last.then_inc(scored, 1)
                                pe.wait_ge(probs_ready if masked else exp_ready, n + 1)
                                for g in range(NB4):
                                    pe.wait_ge(pT_ready, NB4 * n + g + 1)
                                    for c in range(4):
                                        ch = 4 * g + c
                                        last = nc.tensor.transpose(bank[4 + g % 2][:, c * P:(c + 1) * P],
                                                                   s[:, ch * P:(ch + 1) * P], ident[:])
                                    last.then_inc(p_transposed, 1)
                                pe.wait_ge(pT_ready, NB4 * n + NB4 + 1)
                                pe.wait_ge(head_done, n + 1)
                                for c in range(NCH):
                                    last = nc.tensor.matmul(bank[6][:, 0:D], pT[:, c, :],
                                                            v[:, bass.ds(b * NCH + c, 1), :].rearrange("p a d -> p (a d)"),
                                                            start=(c == 0), stop=(c == NCH - 1))
                                last.then_inc(head_out, 1)

                    @unless_safe(block.scalar)
                    def _(act):
                        act.sem_inc(pT_ready, 1)
                        with act.Fori(0, B) as b:
                            with act.Fori(0, H) as h:
                                n = b * H + h
                                act.wait_ge(max_ready, n + 1)
                                nc.scalar.activation(s[:], s[:], ACT.Exp, bias=nmax[:],
                                                     accum_out=den[:]).then_inc(exp_ready, 1)
                                for g in range(NB4):
                                    act.wait_ge(p_transposed, NB4 * n + g + 1)
                                    nc.scalar.activation(pT[:, 4 * g:4 * g + 4, :], bank[4 + g % 2][:].rearrange(
                                        "p (c q) -> p c q", c=4), ACT.Copy).then_inc(pT_ready, 1)

                oT = sb("oT", [P, BT])
                o_transposed, oT_ready = sem("o_transposed"), sem("oT_ready")
                projected, xsteps = sem("projected"), sem("xsteps")
                with nc.Block() as block:
                    @unless_safe(block.tensor)
                    def _(pe):
                        if masked:
                            for b in range(B):
                                last = nc.tensor.transpose(bank[0][:, b * P:(b + 1) * P], o[:, b, :], ident[:])
                            last.then_inc(o_transposed, 1)
                            pe.wait_ge(oT_ready, 1)
                            for b in range(B):
                                last = nc.tensor.matmul(bank[1][:, b * D:(b + 1) * D], oT[:, b * P:(b + 1) * P], wo[:],
                                                        start=True, stop=True)
                            last.then_inc(projected, 1)

                    @unless_safe(block.scalar)
                    def _(act):
                        if masked:
                            act.wait_ge(o_transposed, 1)
                            nc.scalar.activation(oT[:], bank[0][:], ACT.Copy).then_inc(oT_ready, 1)

                    @unless_safe(block.vector)
                    def _(dve):
                        chain = Chain(dve, xsteps)
                        if masked:
                            chain(nc.vector.tensor_tensor(x[:], x[:], bcast(bo[:], 1, B), ALU.add))
                            dve.wait_ge(projected, 1)
                            chain(nc.vector.tensor_tensor(x[:], x[:], bank[1][:].rearrange("p (b d) -> p b d", b=B),
                                                          ALU.add))
                        else:
                            chain(nc.vector.tensor_tensor(x[:], x[:], o[:], ALU.add))
                with nc.Block() as block:
                    @unless_safe(block.sync)
                    def _(sp):
                        for s_ in general_sems.values():
                            sp.sem_clear(s_)

        NU = 2 * NCH
        GPB = S2 // GK
        RT = 4
        (w_in, ctx_in, side_in, k_stored, rows_turned, ctxT_out, k_summed, v_summed, k1_out, k2_out, mask_in,
         v_out, stack_in, q_summed, q_out, q_turned, q_hi_out, q_parts_out, q_blocks_out) = (
            sem(n) for n in ("w_in", "ctx_in", "side_in", "k_stored", "rows_turned", "ctxT_out", "k_summed",
                             "v_summed", "k1_out", "k2_out", "mask_in", "v_out", "stack_in", "q_summed", "q_out",
                             "q_turned", "q_hi_out", "q_parts_out", "q_blocks_out"))
        alive_out, neg_out, sides_turned, gpT_out, negT_out = (
            sem(n) for n in ("alive_out", "neg_out", "sides_turned", "gpT_out", "negT_out"))
        scores_out, exp_out, weighted_out, v_staged, mixed_out, acc_out = (
            sem(n) for n in ("scores_out", "exp_out", "weighted_out", "v_staged", "mixed_out", "acc_out"))
        (rings_ready, wo_in, q_rows_turned, den_spread, attended, attended_steps, output_summed, q_bound_out,
         q_abs_out, bounds_summed, limits_out, limits_turned, safe_steps) = (
            sem(n) for n in ("rings_ready", "wo_in", "q_rows_turned", "den_spread", "attended", "attended_steps",
                             "output_summed", "q_bound_out", "q_abs_out", "bounds_summed", "limits_out",
                             "limits_turned", "safe_steps"))
        safe = sb("safe", [1, 1], I32)
        x_steps = [sem("x_steps0"), sem("x_steps1")]
        N_SAFE = 10
        NW = 6

        def cross_attention(layer, w, masked):
            RANGE, FP16_RANGE, DEAD_RANGE = 80.0, 1000.0, 32.0
            SCALE = DH ** -0.5
            W0 = 16 * NW * layer
            with ExitStack() as c2:
                def sb(n, shape, dt=F32):
                    return c2.enter_context(nc.sbuf_tensor(f"xa{layer}_{n}", shape, dt))

                wq, wk, wv = (sb(n, [P, D]) for n in ("wq", "wk", "wv"))
                bq, bv, bo = sb("bq", [P, D]), sb("bv", [P, D]), sb("bo", [P, D])
                bk = sb("bk", [P, 1])
                wo_rows = sb("wo_rows", [P, RT, D])
                ctx_rows = sb("ctx_rows", [P, CPG, D])
                ctxT = sb("ctxT", [P, GK])
                k1, k2 = sb("k1", [P, S2], F16), sb("k2", [P, S2], F16)
                kstack = sb("kstack", [P, 2, RT, S2], F16)
                v = sb("v", [P, 2, NCH, D])
                v_ring = sb("v_ring", [P, 2, H, 32])
                kmax = sb("kmax", [P, B * GPB])
                q_rows = sb("q_rows", [P, B, D])
                q_live = sb("q_live", [P, RT, 4, 32])
                q_parts = sb("q_parts", [P, RT, P], F16)
                q_blocks = sb("q_blocks", [P, 2, RT, 4, P], F16)
                e_ring = sb("e_ring", [P, 4, 8, P])
                alive = sb("alive", [P, B])
                if masked:
                    gp = sb("gp", [P, GK])
                    mask_i = sb("mask_i", [P, 2, S2], I32)
                    neg = sb("neg", [P, S2], BF16)
                    neg_scale, neg_bias = sb("neg_scale", [P, B]), sb("neg_bias", [P, B])
                    gpT = sb("gpT", [P, 2, NCH, P])
                    negT = sb("negT", [P, 2, NCH, P], BF16)
                    g_ring = sb("g_ring", [P, 4, 8, P])
                    e_sum = sb("e_sum", [P, 2, 8, P])
                num = sb("num", [P, B, 512])
                den = sb("den", [P, B, 512])
                pv_in = g_ring if masked else e_ring
                pv_ready = weighted_out if masked else exp_out

                rows_dram = A["ctx_1024"].rearrange("b (g c p) d -> (b g) p c d", p=P, c=CPG)
                G0, U0, C0, B0 = layer * B * GPB, layer * B * NU, layer * B * NCH, layer * B
                EXP_AHEAD, MIXED_AHEAD = 2, 4
                last_exp = lambda b: U0 + (b + 1) * NU + EXP_AHEAD
                last_mixed = lambda b: U0 + (b + 1) * NU + MIXED_AHEAD
                neg_bank = banks[:, 7, :].bitcast(BF16)[:, 0:GK]
                HALF_STACK = 16 * 4
                D0 = layer * (4 * (B - 1) + 1)
                ACC, A0 = 2 if masked else 1, layer * (2 * B - 1)

                def cols(t, i, n):
                    return t[:, i * n:(i + 1) * n] if isinstance(i, int) else t[:, bass.ds(i * n, n)]

                def chunks(t, b, g):
                    return t[:, b % 2, CPG * g:CPG * (g + 1), :] if isinstance(g, int) else t[
                        :, b % 2, bass.ds(CPG * g, CPG), :]

                q_abs, q_bound = sb("q_abs", [P, BT]), sb("q_bound", [P, BT])
                k_most, q_most = sb("k_most", [P, 1]), sb("q_most", [P, 1])
                limits = sb("limits", [P, 3])
                worst = sb("worst", [1, 3])

                def load(sp):
                    for dst, src in ((wq[:], w["wq"]), (wk[:], w["wk"]), (wv[:], w["wv"]),
                                     (bk[:], w["bk"].rearrange("(d a) -> d a", a=1)),
                                     (bq[:], w["bq"].partition_broadcast(P)),
                                     (bv[:], w["bv"].partition_broadcast(P))):
                        sp.dma_start(dst, src).then_inc(w_in, 16)
                    sp.dma_start(ctx_rows[:], rows_dram[0]).then_inc(ctx_in, 16)
                    if masked:
                        sp.dma_start(mask_i[:, 0, :], A["mask_BxSxS2_ik1"][0]).then_inc(mask_in, 16)

                layer_norm(load)
                with nc.Block() as block:
                    @block.sync
                    def _(sp):
                        def store_keys(b, half):
                            sp.wait_ge(k2_out, G0 + b * GPB + 2 * half + 2)
                            if B0 + b:
                                sp.wait_ge(stack_in, HALF_STACK * (2 * (B0 + b) + half - 1))
                            keys = slice(half * S2 // 2, (half + 1) * S2 // 2)
                            for i, part in enumerate((k1, k2)):
                                sp.dma_start(k_dram[i][:, keys], part[:, keys]).then_inc(k_stored, 16)

                        def stack(b, half):
                            keys = slice(half * S2 // 2, (half + 1) * S2 // 2)
                            if b >= 2:
                                sp.wait_ge(scores_out, U0 + (b - 1) * NU)
                            if half:
                                sp.wait_ge(stack_in, HALF_STACK * (2 * (B0 + b) + 1))
                            sp.wait_ge(k_stored, 32 * (2 * (B0 + b) + half + 1))
                            for i in range(2):
                                rows = k_dram[i].rearrange("(r p) s -> p r s", r=RT)[:, :, keys]
                                for g in (2 * i, 2 * i + 1):
                                    sp.dma_start(kstack[32 * g:32 * g + 32, b % 2, :, keys], rows).then_inc(stack_in, 16)

                        for m in range(B * GPB + 1):
                            b = m // GPB
                            if 0 < m < B * GPB:
                                sp.wait_ge(rows_turned, G0 + m)
                                sp.dma_start(ctx_rows[:], rows_dram[m]).then_inc(ctx_in, 16)
                            if m % GPB == 2:
                                store_keys(b, 0)
                            if m % GPB == 0 and m:
                                store_keys(b - 1, 1)
                            if m == 1 and masked:
                                sp.wait_ge(mask_in, 16)
                                sp.dma_start(mask_i[:, 1, :], A["mask_BxSxS2_ik1"][1]).then_inc(mask_in, 16)
                            if m == 0:
                                sp.wait_ge(rings_ready, 3 * layer + 1)
                                src = (w["wo"] if masked else ident_dram).rearrange("(r c d) n -> c d r n", r=RT, c=4)
                                for c in range(4):
                                    sp.dma_start(wo_rows[32 * c:32 * c + DH, :, :], src[c]).then_inc(wo_in, 16)
                                if masked:
                                    sp.dma_start(bo[:], w["bo"].partition_broadcast(P)).then_inc(wo_in, 16)
                            if masked and m < B * GPB:
                                if m:
                                    sp.wait_ge(sides_turned, 2 * m)
                                sp.dma_start(gp[:], A["fside_BxSxS2_0"][b][:, m % GPB * GK:(m % GPB + 1) * GK]
                                             ).then_inc(side_in, 16)
                            if m % GPB == 3:
                                stack(b, 0)
                            if m % GPB == 0 and m:
                                stack(b - 1, 1)
                            if m % GPB == 1 and masked and m > 1 and b + 1 < B:
                                sp.wait_ge(neg_out, GPB * b)
                                sp.wait_ge(mask_in, 16 * (b + 1))
                                sp.dma_start(mask_i[:, (b + 1) % 2, :],
                                             A["mask_BxSxS2_ik1"][b + 1]).then_inc(mask_in, 16)

                    @block.gpsimd
                    def _(pool):
                        nc.gpsimd.memset(wo_rows[:], 0.0).then_inc(rings_ready, 1)
                        nc.gpsimd.memset(v_ring[:], 0.0).then_inc(rings_ready, 1)
                        pool.wait_ge(rings_ready, 3 * layer + 2)
                        if not masked:
                            nc.gpsimd.memset(v_ring[:, :, :, DH:DH + 1], 1.0).then_inc(rings_ready, 1)
                        else:
                            nc.gpsimd.engine_nop().then_inc(rings_ready, 1)
                        pool.wait_ge(rings_ready, 3 * layer + 3)
                        for b in range(B):
                            with pool.Fori(0, GPB) as g:
                                pool.wait_ge(v_out, G0 + b * GPB + g + 1)
                                for c in range(CPG):
                                    pool.wait_ge(mixed_out, U0 + b * NU + 8 * g + 2 * c - 2 + MIXED_AHEAD)
                                    nc.gpsimd.tensor_copy(
                                        v_ring[:, c % 2, :, 0:DH],
                                        v[:, b % 2, bass.ds(CPG * g + c, 1), :].rearrange("p a (h d) -> p (a h) d", h=H)
                                    ).then_inc(v_staged, 1)

                    AFTER = (2, 5, 7)

                    def is_last(g):
                        return isinstance(g, int) and g == GPB - 1

                    def rows_bank(m):
                        return bank[m] if isinstance(m, int) and m < GPB else bank[6]

                    def queries_bank(b):
                        return bank[7] if b else bank[4]

                    @block.tensor
                    def _(pe):
                        if layer == 0:
                            pe.sem_inc(mixed_out, MIXED_AHEAD)

                        def turn(m):
                            if not isinstance(m, int) or m >= GPB:
                                if masked:
                                    pe.wait_ge(gpT_out, m)
                                else:
                                    pe.wait_ge(k2_out, G0 + m)
                            pe.wait_ge(ctx_in, 16 * (G0 + m + 1))
                            for c in range(CPG):
                                last = nc.tensor.transpose(rows_bank(m)[:, c * P:(c + 1) * P], ctx_rows[:, c, :],
                                                           ident[:])
                            last.then_inc(rows_turned, 1)

                        def bank7_read(b, g):
                            n = G0 + b * GPB + g
                            if not isinstance(n, int) or n:
                                pe.wait_ge(v_out, n)
                            if b and is_last(g):
                                pe.wait_ge(q_parts_out, 2 * (B0 + b + 1))

                        def keys_step(b, g):
                            n = G0 + b * GPB + g
                            pe.wait_ge(ctxT_out, n + 1)
                            nc.tensor.matmul(bank[6][:], wk[:], ctxT[:], start=True, stop=True).then_inc(k_summed, 1)
                            if masked:
                                bank7_read(b, g)
                                pe.wait_ge(neg_out, n + 1)
                                for c in range(CPG):
                                    last = nc.tensor.transpose(neg_bank[:, c * P:(c + 1) * P],
                                                               cols(neg, CPG * g + c, P), ident_bf[:])
                                last.then_inc(sides_turned, 1)

                        def values_step(b, g):
                            n = G0 + b * GPB + g
                            if masked:
                                pe.wait_ge(negT_out, n + 1)
                            else:
                                bank7_read(b, g)
                            for c in range(CPG):
                                last = nc.tensor.matmul(bank[7][:, c * P:(c + 1) * P], ctxT[:, c * P:(c + 1) * P],
                                                        wv[:], start=True, stop=True)
                            last.then_inc(v_summed, 1)
                            if masked:
                                pe.wait_ge(k2_out, n + 1)
                                pe.wait_ge(side_in, 16 * (n + 1))
                                for c in range(CPG):
                                    last = nc.tensor.transpose(bank[6][:, c * P:(c + 1) * P],
                                                               gp[:, c * P:(c + 1) * P], ident[:])
                                last.then_inc(sides_turned, 1)

                        def rows_step(b, g):
                            if not (b + 1 == B and is_last(g)):
                                turn(b * GPB + g + 1)

                        def queries(b):
                            pe.wait_ge(q_out, layer * (2 + B) + 2 + b + 1)
                            if b:
                                pe.wait_ge(v_out, G0 + b * GPB + GPB - 1)
                            for r in range(RT):
                                last = nc.tensor.transpose(queries_bank(b)[:, r * P:(r + 1) * P],
                                                           q_live[:, r, :, :].rearrange("p g i -> p (g i)"), ident[:])
                            last.then_inc(q_turned, 1)

                        def score(b, n, c, hf):
                            pe.wait_ge(exp_out, n - 1 + EXP_AHEAD)
                            for rr in range(2):
                                r = 2 * hf + rr
                                last = nc.tensor.matmul(
                                    bank[r][:], cols(kstack[:, b % 2, r, :], c, P),
                                    q_blocks[:, b % 2, r, :, :].rearrange("p j t -> p (j t)"), start=True,
                                    stop=not masked)
                                if masked:
                                    mask_cols = negT[:, b % 2, c, :] if isinstance(c, int) else negT[
                                        :, b % 2, bass.ds(c, 1), :].rearrange("p a q -> p (a q)")
                                    last = nc.tensor.matmul(bank[r][:], ident_bf[:], bcast(mask_cols, 1, 4),
                                                            start=False, stop=True)
                            last.then_inc(scores_out, 1)

                        def mix(b, n, chunk, k):
                            hf = k % 2
                            pe.wait_ge(v_staged, chunk + 1)
                            pe.wait_ge(pv_ready, n + 1 + (0 if masked else EXP_AHEAD))
                            for rr in range(2):
                                for c in range(4):
                                    r = 2 * hf + rr
                                    last = nc.tensor.matmul(bank[4][32 * c:32 * c + 32, r * P:(r + 1) * P],
                                                            v_ring[:, k // 2, 4 * r + c, :], pv_in[:, k, 4 * rr + c, :],
                                                            start=False, stop=False, skip_group_check=True)
                            if masked and k >= 2:
                                for c in range(4):
                                    last = nc.tensor.matmul(
                                        bank[5][32 * c:32 * c + 32, 2 * hf * P:(2 * hf + 2) * P], ones32[:],
                                        e_sum[:, hf, :, :].rearrange("p (r c) t -> p r c t", r=2)[:, :, c, :],
                                        start=False, stop=False, skip_group_check=True)
                            last.then_inc(mixed_out, 1)

                        def first_scores(b, u):
                            if u == 0:
                                pe.wait_ge(stack_in, HALF_STACK * (2 * (B0 + b) + 1))
                                pe.wait_ge(q_blocks_out, B0 + b + 1)
                                if masked:
                                    pe.wait_ge(negT_out, b * GPB + 1)
                            score(b, U0 + b * NU + u, 0, u)

                        def eight_units(b, g):
                            n0, ch0 = U0 + b * NU, C0 + b * NCH
                            for u in range(8):
                                if is_last(g) and u >= 6:
                                    if b + 1 < B:
                                        first_scores(b + 1, u - 6)
                                else:
                                    score(b, n0 + 8 * g + u + 2, 4 * g + u // 2 + 1, u % 2)
                                mix(b, n0 + 8 * g + u, ch0 + 4 * g + u // 2, u % 4)
                                if b + 1 < B and u in AFTER:
                                    (keys_step, values_step, rows_step)[AFTER.index(u)](b + 1, g)
                                if b + 1 == B and is_last(g) and u == 2:
                                    pe.wait_ge(q_bound_out, layer + 1)
                                    nc.tensor.matmul(bank[7][0:H, :], head_rows[:], q_bound[:], start=True,
                                                     stop=True).then_inc(bounds_summed, 1)
                                if b + 1 == B and is_last(g) and u == 6:
                                    pe.wait_ge(limits_out, 3 * layer + 3)
                                    nc.tensor.transpose(bank[6][0:1, 0:P], limits[:, 0:1], ident[:])
                                    nc.tensor.transpose(bank[6][0:1, P:2 * P], limits[:, 1:2], ident[:])
                                    nc.tensor.transpose(bank[6][0:1, 2 * P:2 * P + H], limits[0:H, 2:3],
                                                        ident[0:H, 0:H]).then_inc(limits_turned, 1)

                        pe.wait_ge(w_in, W0 + 16 * NW)
                        for b in range(B):
                            last = nc.tensor.matmul(bank[5][:, b * D:(b + 1) * D], xT[:, b * P:(b + 1) * P], wq[:],
                                                    start=True, stop=True)
                        last.then_inc(q_summed, 1)
                        turn(0)
                        for g in range(GPB):
                            if g:
                                if masked:
                                    pe.wait_ge(gpT_out, g)
                                else:
                                    pe.wait_ge(k2_out, G0 + g)
                            keys_step(0, g)
                            if g + 1 < GPB:
                                turn(g + 1)
                            values_step(0, g)
                            if g == 0:
                                queries(0)
                        turn(GPB)
                        pe.wait_ge(ctxT_out, G0 + GPB)
                        first_scores(0, 0)
                        first_scores(0, 1)
                        for b in range(B):
                            if masked:
                                pe.wait_ge(negT_out, (b + 1) * GPB)
                            if b >= 1:
                                pe.wait_ge(acc_out, A0 + ACC * b)
                            for acc in (4, 5) if masked else (4,):
                                nc.tensor.matmul(bank[acc][:], zero_bf[:], bcast(ident_bf[:], 1, 4), start=True,
                                                 stop=False, skip_group_check=True)
                            eight_units(b, 0)
                            pe.wait_ge(stack_in, HALF_STACK * 2 * (B0 + b + 1))
                            with pe.Fori(1, GPB - 1) as g:
                                eight_units(b, g)
                            if not masked and b >= 1:
                                if b >= 2:
                                    pe.wait_ge(attended_steps, D0 + b - 1)
                                nc.tensor.matmul(bank[5][:], spread_den[:], num[:, b - 1, :], start=True,
                                                 stop=True).then_inc(den_spread, 1)
                            if b + 1 < B:
                                queries(b + 1)
                            else:
                                pe.wait_ge(ctxT_out, G0 + B * GPB)
                                pe.wait_ge(gpT_out if masked else k2_out, G0 + B * GPB)
                                for bb in range(B):
                                    last = nc.tensor.transpose(bank[6][:, bb * P:(bb + 1) * P], q_rows[:, bb, :],
                                                               ident[:])
                                last.then_inc(q_rows_turned, 1)
                            eight_units(b, GPB - 1)

                    @block.scalar
                    def _(act):
                        if layer == 0:
                            act.sem_inc(exp_out, EXP_AHEAD)

                        def rows_copy(m):
                            act.wait_ge(rows_turned, G0 + m + 1)
                            if not isinstance(m, int) or m:
                                act.wait_ge(v_summed, G0 + m)
                            nc.scalar.activation(ctxT[:], rows_bank(m), ACT.Copy).then_inc(ctxT_out, 1)

                        def keys_step(b, g):
                            n = G0 + b * GPB + g
                            act.wait_ge(k_summed, n + 1)
                            nc.scalar.activation(cols(k1, g, GK), bank[6][:], ACT.Identity,
                                                 bias=bk[:]).then_inc(k1_out, 1)
                            if masked:
                                if isinstance(n, int) and n == 0:
                                    mask(0, 0)
                                act.wait_ge(sides_turned, 2 * n + 1)
                                nc.scalar.activation(
                                    chunks(negT, b, g), neg_bank.rearrange("p (c q) -> p c q", c=CPG),
                                    ACT.Copy).then_inc(negT_out, 1)

                        def sides_step(b, g):
                            if masked:
                                act.wait_ge(sides_turned, 2 * (G0 + b * GPB + g) + 2)
                                nc.scalar.activation(chunks(gpT, b, g), bank[6][:].rearrange(
                                    "p (c q) -> p c q", c=CPG), ACT.Copy).then_inc(gpT_out, 1)
                                if not is_last(g):
                                    mask(b, g + 1)

                        def rows_step(b, g):
                            if not (b + 1 == B and is_last(g)):
                                rows_copy(b * GPB + g + 1)

                        def mask(b, g):
                            act.wait_ge(alive_out, 3 * b + 3)
                            if b >= 1:
                                act.wait_ge(sides_turned, 2 * GPB * (b - 1) + 2 * g + 1)
                            nc.scalar.activation(cols(neg, g, GK), cols(mask_i[:, b % 2, :], g, GK), ACT.Identity,
                                                 bias=neg_bias[:, b:b + 1],
                                                 scale=neg_scale[:, b:b + 1]).then_inc(neg_out, 1)

                        def queries(b):
                            act.wait_ge(q_turned, B0 + b + 1)
                            if b >= 1:
                                act.wait_ge(q_blocks_out, B0 + b)
                            nc.scalar.activation(q_parts[:], queries_bank(b).rearrange("p (r t) -> p r t", r=RT),
                                                 ACT.Copy).then_inc(q_hi_out, 1)

                        def spread_queries(b):
                            act.wait_ge(q_parts_out, 2 * (B0 + b) + 2)
                            if b >= 2:
                                act.wait_ge(scores_out, U0 + (b - 1) * NU)
                            for j in range(4):
                                last = nc.scalar.activation(q_blocks[:, b % 2, :, j, :], q_parts[:], ACT.Copy,
                                                            scale=quarter_rows[:, j:j + 1])
                            last.then_inc(q_blocks_out, 1)

                        def exponentials(n, k):
                            act.wait_ge(scores_out, n + 1)
                            act.wait_ge(mixed_out, n - 3 + MIXED_AHEAD)
                            if masked and k < 2 and not (isinstance(n, int) and n < 2):
                                act.wait_ge(weighted_out, n - 1)
                            nc.scalar.activation(e_ring[:, k, :, :].rearrange("p (r c) t -> p r (c t)", r=2),
                                                 banks[:, 2 * (k % 2):2 * (k % 2) + 2, :], ACT.Exp).then_inc(exp_out, 1)

                        def eight_units(b, g):
                            for u in range(8):
                                if not (is_last(g) and u >= 6 and b + 1 == B):
                                    exponentials(U0 + b * NU + 8 * g + u + 2, (u + 2) % 4)
                                if b + 1 < B and u == AFTER[0]:
                                    keys_step(b + 1, g)
                                if b + 1 < B and is_last(g) and u == 4:
                                    spread_queries(b + 1)
                                if b + 1 < B and u == AFTER[1]:
                                    sides_step(b + 1, g)
                                if b + 1 < B and u == AFTER[2]:
                                    rows_step(b + 1, g)

                        act.wait_ge(w_in, W0 + 16 * NW)
                        rows_copy(0)
                        for g in range(GPB):
                            keys_step(0, g)
                            if g + 1 < GPB:
                                rows_copy(g + 1)
                            sides_step(0, g)
                            if g == 0:
                                queries(0)
                            if g == 1:
                                spread_queries(0)
                        rows_copy(GPB)
                        exponentials(U0, 0)
                        exponentials(U0 + 1, 1)
                        for b in range(B):
                            if masked and b >= 1:
                                act.wait_ge(mixed_out, last_mixed(b - 1))
                                nc.scalar.activation(num[:, b - 1, :], bank[4][:], ACT.Copy).then_inc(acc_out, 1)
                                nc.scalar.activation(den[:, b - 1, :], bank[5][:], ACT.Copy).then_inc(acc_out, 1)
                            if b + 1 < B:
                                if masked:
                                    mask(b + 1, 0)
                                act.wait_ge(k_stored, 64 * (B0 + b + 1))
                                if b >= 1:
                                    act.wait_ge(scores_out, U0 + b * NU)
                                    if masked:
                                        act.wait_ge(weighted_out, U0 + b * NU)
                            with act.Fori(0, GPB - 1) as g:
                                eight_units(b, g)
                            if b + 1 < B:
                                queries(b + 1)
                            else:
                                act.wait_ge(q_rows_turned, layer + 1)
                                nc.scalar.activation(q_abs[:], bank[6][:], ACT.Abs).then_inc(q_abs_out, 1)
                            eight_units(b, GPB - 1)

                    @block.vector
                    def _(dve):
                        Q0 = layer * (2 + B)

                        def alive_rows(b):
                            dve.wait_ge(mask_in, 16 * (b + 1))
                            nc.vector.tensor_reduce(alive[:, b:b + 1], mask_i[:, b % 2, :], AX_X,
                                                    ALU.max).then_inc(alive_out, 1)
                            dve.wait_ge(alive_out, 3 * b + 1)
                            nc.vector.tensor_scalar(neg_scale[:, b:b + 1], alive[:, b:b + 1], 1.0e9, None,
                                                    ALU.mult).then_inc(alive_out, 1)
                            nc.vector.tensor_scalar(neg_bias[:, b:b + 1], alive[:, b:b + 1], -1.0e9, None,
                                                    ALU.mult).then_inc(alive_out, 1)

                        def live_queries(b):
                            if b >= 1:
                                dve.wait_ge(q_turned, B0 + b)
                            q_four = bcast(q_rows[:, b, :].rearrange("p (r i) -> p r i", r=RT), 2, 4)
                            if masked:
                                nc.vector.tensor_scalar(q_live[:], q_four, alive[:, b:b + 1], None,
                                                        ALU.mult).then_inc(q_out, 1)
                            else:
                                nc.vector.tensor_copy(q_live[:], q_four).then_inc(q_out, 1)

                        def keys_step(b, g):
                            n = G0 + b * GPB + g
                            dve.wait_ge(k1_out, n + 1)
                            nc.vector.scalar_tensor_tensor(out=cols(k2, g, GK), in0=bank[6][:], scalar=bk[:],
                                                           in1=cols(k1, g, GK), op0=ALU.add,
                                                           op1=ALU.subtract).then_inc(k2_out, 1)
                            nc.vector.tensor_reduce(cols(kmax, b * GPB + g, 1), cols(k1, g, GK), AX_X, ALU.max,
                                                    apply_absolute_value=True)

                        def values_step(b, g):
                            n = G0 + b * GPB + g
                            dve.wait_ge(v_summed, n + 1)
                            nc.vector.tensor_tensor(chunks(v, b, g), bank[7][:].rearrange("p (c d) -> p c d", c=CPG),
                                                    bcast(bv[:], 1, CPG), ALU.add).then_inc(v_out, 1)

                        def queries(b):
                            dve.wait_ge(q_hi_out, B0 + b + 1)
                            for p0 in (32, 96):
                                rows = slice(p0, p0 + 32)
                                nc.vector.tensor_tensor(q_parts[rows, :, :],
                                                        queries_bank(b)[rows, :].rearrange("p (r t) -> p r t", r=RT),
                                                        q_parts[rows, :, :], ALU.subtract).then_inc(q_parts_out, 1)

                        def weigh(b, n, c, k):
                            dve.wait_ge(exp_out, n + 1 + EXP_AHEAD)
                            dve.wait_ge(mixed_out, n - 3 + MIXED_AHEAD)
                            weights = gpT[:, b % 2, c, :] if isinstance(c, int) else gpT[
                                :, b % 2, bass.ds(c, 1), :].rearrange("p a q -> p (a q)")
                            last = nc.vector.tensor_tensor(g_ring[:, k, :, :], e_ring[:, k, :, :],
                                                           bcast(weights, 1, 8), ALU.mult)
                            if k >= 2:
                                last = nc.vector.tensor_tensor(e_sum[:, k - 2, :, :], e_ring[:, k - 2, :, :],
                                                               e_ring[:, k, :, :], ALU.add)
                            last.then_inc(weighted_out, 1)

                        def first_weights(b, u):
                            dve.wait_ge(gpT_out, b * GPB + 1)
                            weigh(b, U0 + b * NU + u, 0, u)

                        def eight_units(b, g):
                            for u in range(8):
                                if masked:
                                    if is_last(g) and u >= 6:
                                        if b + 1 < B:
                                            first_weights(b + 1, u - 6)
                                    else:
                                        weigh(b, U0 + b * NU + 8 * g + u + 2, 4 * g + u // 2 + 1, (u + 2) % 4)
                                if b + 1 < B and u == AFTER[0]:
                                    keys_step(b + 1, g)
                                if b + 1 < B and u == AFTER[1]:
                                    values_step(b + 1, g)
                                if masked and b + 2 < B and is_last(g) and u == 6:
                                    alive_rows(b + 2)
                                if masked and b >= 1 and is_last(g) and u < 4:
                                    dve.wait_ge(acc_out, A0 + ACC * b)
                                    part = slice(u * P, (u + 1) * P)
                                    nc.vector.reciprocal(den[:, b - 1, part],
                                                         den[:, b - 1, part]).then_inc(attended_steps, 1)
                                if masked and b >= 1 and is_last(g) and u == 4:
                                    dve.wait_ge(attended_steps, 4 * b)
                                    nc.vector.tensor_tensor(num[:, b - 1, :], num[:, b - 1, :], den[:, b - 1, :],
                                                            ALU.mult).then_inc(attended, 1)
                                if b + 1 == B and is_last(g) and u == 3:
                                    dve.wait_ge(bounds_summed, layer + 1)
                                    nc.vector.tensor_reduce(limits[0:H, 2:3], bank[7][0:H, :], AX_X,
                                                            ALU.max).then_inc(limits_out, 1)
                                if b + 1 == B and is_last(g) and u == 7:
                                    range_decision()

                        chain = Chain(dve, safe_steps, layer * N_SAFE)

                        def range_check():
                            chain(nc.vector.tensor_reduce(k_most[:], kmax[:], AX_X, ALU.max))
                            dve.wait_ge(q_abs_out, layer + 1)
                            nc.vector.tensor_scalar(q_bound[:], q_abs[:], k_most[:], None,
                                                    ALU.mult).then_inc(q_bound_out, 1)
                            chain(nc.vector.tensor_reduce(q_most[:], q_abs[:], AX_X, ALU.max))
                            chain(nc.vector.tensor_tensor(q_most[:], q_most[:], k_most[:], ALU.max))
                            nc.vector.tensor_scalar(limits[:, 0:1], q_most[:], RANGE / FP16_RANGE, None,
                                                    ALU.mult).then_inc(limits_out, 1)
                            if masked:
                                chain(nc.vector.tensor_reduce(k_most[:], alive[:], AX_X, ALU.min))
                                nc.vector.tensor_scalar(limits[:, 1:2], k_most[:], -(RANGE - DEAD_RANGE),
                                                        RANGE - DEAD_RANGE, ALU.mult, ALU.add).then_inc(limits_out, 1)
                            else:
                                chain(nc.vector.memset(k_most[:], 0.0))
                                nc.vector.memset(limits[:, 1:2], 0.0).then_inc(limits_out, 1)

                        def range_decision():
                            dve.wait_ge(limits_turned, layer + 1)
                            chain(nc.vector.tensor_reduce(worst[0:1, 0:1], bank[6][0:1, 0:P], AX_X, ALU.max))
                            chain(nc.vector.tensor_reduce(worst[0:1, 1:2], bank[6][0:1, P:2 * P], AX_X, ALU.max))
                            chain(nc.vector.tensor_reduce(worst[0:1, 2:3], bank[6][0:1, 2 * P:2 * P + H], AX_X, ALU.max))
                            chain(nc.vector.tensor_tensor(worst[0:1, 2:3], worst[0:1, 2:3], worst[0:1, 1:2], ALU.add))
                            chain(nc.vector.tensor_tensor(worst[0:1, 2:3], worst[0:1, 2:3], worst[0:1, 0:1], ALU.max))
                            chain(nc.vector.tensor_scalar(safe[:], worst[0:1, 2:3], RANGE, None, ALU.is_le))

                        dve.wait_ge(w_in, W0 + 16 * NW)
                        dve.wait_ge(q_summed, layer + 1)
                        nc.vector.tensor_tensor(q_rows[:], bank[5][:].rearrange("p (b d) -> p b d", b=B),
                                                bcast(bq[:], 1, B), ALU.add).then_inc(q_out, 1)
                        dve.wait_ge(q_out, Q0 + 1)
                        nc.vector.tensor_scalar(q_rows[:], q_rows[:], SCALE, None, ALU.mult).then_inc(q_out, 1)
                        if masked:
                            alive_rows(0)
                        dve.wait_ge(q_out, Q0 + 2)
                        live_queries(0)
                        for g in range(GPB):
                            keys_step(0, g)
                            values_step(0, g)
                            if g == 0:
                                queries(0)
                            if masked and g == 1:
                                alive_rows(1)
                        if masked:
                            first_weights(0, 0)
                            first_weights(0, 1)
                        for b in range(B):
                            if b >= 1 and not masked:
                                dve.wait_ge(mixed_out, last_mixed(b - 1))
                                nc.vector.tensor_copy(num[:, b - 1, :], bank[4][:]).then_inc(acc_out, 1)
                            if b + 1 < B:
                                live_queries(b + 1)
                                dve.wait_ge(k_stored, 64 * (B0 + b + 1))
                                if b >= 1:
                                    dve.wait_ge(v_staged, C0 + b * NCH)
                            if masked:
                                dve.wait_ge(gpT_out, (b + 1) * GPB)
                            if masked or b + 1 < B:
                                with dve.Fori(0, GPB - 1) as g:
                                    eight_units(b, g)
                            if b >= 1 and not masked:
                                dve.wait_ge(den_spread, b)
                                nc.vector.reciprocal(den[:, b - 1, :], bank[5][:]).then_inc(attended_steps, 1)
                                dve.wait_ge(attended_steps, D0 + b)
                                nc.vector.tensor_tensor(num[:, b - 1, :], num[:, b - 1, :], den[:, b - 1, :],
                                                        ALU.mult).then_inc(attended, 1)
                            if b + 1 == B:
                                range_check()
                            if b + 1 < B:
                                queries(b + 1)
                            eight_units(b, GPB - 1)

                with nc.Block() as block:
                    @block.tensor
                    def _(pe):
                        pe.wait_ge(wo_in, 80 + 64 * layer)
                        for b in range(B):
                            if b == B - 1 and not masked:
                                pe.wait_ge(acc_out, A0 + B)
                                nc.tensor.matmul(bank[0][:], spread_den[:], num[:, b, :], start=True,
                                                 stop=True).then_inc(den_spread, 1)
                            pe.wait_ge(attended, B0 + b + 1)
                            for r in range(RT):
                                last = nc.tensor.matmul(bank[6][:, b * D:(b + 1) * D], num[:, b, r * P:(r + 1) * P],
                                                        wo_rows[:, r, :], start=(r == 0), stop=(r == RT - 1))
                        last.then_inc(output_summed, 1)

                    @block.vector
                    def _(dve):
                        b = B - 1
                        dve.wait_ge(mixed_out, last_mixed(b))
                        nc.vector.tensor_copy(num[:, b, :], bank[4][:]).then_inc(acc_out, 1)
                        if not masked:
                            dve.wait_ge(den_spread, B)
                        nc.vector.reciprocal(den[:, b, :], bank[5 if masked else 0][:]).then_inc(attended_steps, 1)
                        dve.wait_ge(attended_steps, D0 + (4 * (B - 1) + 1 if masked else B))
                        nc.vector.tensor_tensor(num[:, b, :], num[:, b, :], den[:, b, :], ALU.mult).then_inc(attended, 1)
                        dve.wait_ge(output_summed, layer + 1)
                        within = dve.value_load(safe[0:1, 0:1], min_val=0, max_val=1)
                        with dve.If(within > 0):
                            nc.vector.tensor_tensor(x[:], x[:], bank[6][:].rearrange("p (b d) -> p b d", b=B),
                                                    ALU.add).then_inc(x_steps[layer], 1)
                            if masked:
                                dve.wait_ge(x_steps[layer], 1)
                                nc.vector.tensor_tensor(x[:], x[:], bcast(bo[:], 1, B), ALU.add)
            general_attention(f"general{layer}", w, masked, safe)

        def small_sems(c2, name, *names):
            return [ctx.enter_context(nc.semaphore(f"{name}_{n}")) for n in names]

        def retention(name, w):
            with ExitStack() as c2:
                def sb(n, shape, dt=F32):
                    return c2.enter_context(nc.sbuf_tensor(f"{name}_{n}", shape, dt))

                def sem(n):
                    return ctx.enter_context(nc.semaphore(f"{name}_{n}"))

                NZ = HA + HA * LV
                wq, wk, wv = (sb(n, [P, HA, D]) for n in ("wq", "wk", "wv"))
                wo = sb("wo", [P, HA * P])
                wz = sb("wz", [NZ, D])
                z_bias = sb("z_bias", [P, NZ])
                ln_g, ln_b = sb("ln_g", [P, D]), sb("ln_b", [P, D])
                wqk = sb("wqk", [P, HA, D])
                woT = sb("woT", [P, HA, D])
                wvo = sb("wvo", [P, HA * D])
                wzT = sb("wzT", [P, NZ])
                w_loaded = sem("w_loaded")
                qk_merged, wo_transposed, woT_ready, vo_merged = (
                    sem(n) for n in ("qk_merged", "wo_transposed", "woT_ready", "vo_merged"))
                folded = sem("folded")

                def load(sp):
                    for dst, src in ((wq, w["wq"]), (wk, w["wk"]), (wv, w["wv"])):
                        sp.dma_start(dst[:], src.rearrange("(h s) d -> s h d", h=HA)).then_inc(w_loaded, 16)
                    sp.dma_start(wo[:], w["wo"]).then_inc(w_loaded, 16)
                    sp.dma_start(wz[0:HA, :], w["wg"]).then_inc(w_loaded, 16)
                    sp.dma_start(wz[HA:NZ, :], w["wdl"]).then_inc(w_loaded, 16)
                    sp.dma_start(z_bias[:, 0:HA], w["bg"].partition_broadcast(P)).then_inc(w_loaded, 16)
                    sp.dma_start(z_bias[:, HA:NZ], w["lparam"].rearrange("h l -> (h l)").partition_broadcast(P)
                                 ).then_inc(w_loaded, 16)
                    sp.dma_start(ln_g[:], w["ln_g"].partition_broadcast(P)).then_inc(w_loaded, 16)
                    sp.dma_start(ln_b[:], w["ln_b"].partition_broadcast(P)).then_inc(w_loaded, 16)

                layer_norm(load)
                with nc.Block() as block:
                    @block.tensor
                    def _(pe):
                        pe.wait_ge(w_loaded, 160)
                        for h in range(HA):
                            last = nc.tensor.matmul(bank[h // 4][:, h % 4 * P:h % 4 * P + P], wq[:, h, :], wk[:, h, :],
                                                    start=True, stop=True)
                        last.then_inc(qk_merged, 1)
                        for h in range(HA):
                            nc.tensor.transpose(bank[2 + h // 4][:, h % 4 * P:h % 4 * P + P],
                                                wo[:, h * P:(h + 1) * P], ident[:])
                        nc.tensor.transpose(bank[6][:, 0:NZ], wz[:, :], ident[0:NZ, 0:NZ]).then_inc(wo_transposed, 1)
                        pe.wait_ge(woT_ready, 2)
                        for h in range(HA):
                            last = nc.tensor.matmul(bank[4 + h // 4][:, h % 4 * P:h % 4 * P + P], wv[:, h, :],
                                                    woT[:, h, :], start=True, stop=True)
                        last.then_inc(vo_merged, 1)

                    @block.scalar
                    def _(act):
                        act.wait_ge(qk_merged, 1)
                        for g in range(2):
                            nc.scalar.activation(wqk[:, 4 * g:4 * g + 4, :], bank[g][:].rearrange(
                                "p (h d) -> p h d", h=4), ACT.Copy).then_inc(folded, 1)
                        act.wait_ge(vo_merged, 1)
                        for g in range(2):
                            nc.scalar.activation(wvo[:, g * 512:(g + 1) * 512], bank[4 + g][:],
                                                 ACT.Copy).then_inc(folded, 1)

                    @block.vector
                    def _(dve):
                        dve.wait_ge(wo_transposed, 1)
                        for g in range(2):
                            nc.vector.tensor_copy(woT[:, 4 * g:4 * g + 4, :], bank[2 + g][:].rearrange(
                                "p (h d) -> p h d", h=4)).then_inc(woT_ready, 1)
                        nc.vector.tensor_copy(wzT[:], bank[6][:, 0:NZ]).then_inc(folded, 1)

                z = sb("z", [P, B, NZ])
                z_abs = sb("z_abs", [P, B, NZ])
                z_exp = sb("z_exp", [P, B, NZ])
                sp_z = sb("softplus", [P, B, NZ])
                xqk = sb("xqk", [P, HA, BT])
                xvo = sb("xvo", [P, B, HA * D])
                decay = sb("decay", [P, B, HA, T])
                lam = sb("lam", [P, B, HA, T])
                lamw = sb("lamw", [P, B, HA, T])
                att = sb("att", [P, B, HA, T])
                attT = sb("attT", [P, B, HA, T])
                y = sb("y", [P, B, D])
                scratch = nc.dram_tensor(f"{name}_lam_scratch", [B, T * HA * T], F32)
                z_projected, z_ready, abs_ready, exp_ready, ln_ready, gates_ready = (
                    sem(n) for n in ("z_projected", "z_ready", "abs_ready", "exp_ready", "ln_ready", "gates_ready"))
                xqk_projected, xqk_ready, xvo_projected, xvo_ready = (
                    sem(n) for n in ("xqk_projected", "xqk_ready", "xvo_projected", "xvo_ready"))
                decay_summed, decay_ready, lam_ready, lam_stored, lamw_ready = (
                    sem(n) for n in ("decay_summed", "decay_ready", "lam_ready", "lam_stored", "lamw_ready"))
                dl_ready, scored, att_ready, att_transposed, attT_ready, summed = (
                    sem(n) for n in ("dl_ready", "scored", "att_ready", "att_transposed", "attT_ready", "summed"))
                y_steps, y_var_ready, y_rstd_ready = sem("y_steps"), sem("y_var_ready"), sem("y_rstd_ready")
                HALVES = [(b, g) for b in range(B) for g in range(2)]
                SCALE = P ** -0.5

                with nc.Block() as block:
                    @block.tensor
                    def _(pe):
                        for b in range(B):
                            last = nc.tensor.matmul(bank[7][:, b * NZ:(b + 1) * NZ], xT[:, b * P:(b + 1) * P], wzT[:],
                                                    start=True, stop=True)
                        last.then_inc(z_projected, 1)
                        for h in range(HA):
                            if h >= 2:
                                pe.wait_ge(xqk_ready, h - 1)
                            nc.tensor.matmul(bank[h % 2][:], wqk[:, h, :], xT[:], start=True,
                                             stop=True).then_inc(xqk_projected, 1)
                        pe.wait_ge(gates_ready, 1)
                        for i, (b, g) in enumerate(HALVES):
                            if i >= 2:
                                pe.wait_ge(decay_ready, i - 1)
                            ps = bank[2 + i % 2]
                            nc.tensor.matmul(ps[:], ident_bf[:], bcast(future_bf[:], 1, 4), start=True, stop=False,
                                             skip_group_check=True)
                            for j in range(4):
                                h = 4 * g + j
                                nc.tensor.matmul(ps[:, j * P:(j + 1) * P], repeat(sp_z[:, b, h:h + 1], P),
                                                 upper[:], start=False, stop=False, skip_group_check=True)
                            nc.tensor.matmul(ps[:], neg_upper[:], bcast(sp_z[:, b, 4 * g:4 * g + 4], 2, P),
                                             start=False, stop=True, skip_group_check=True).then_inc(decay_summed, 1)
                        pe.wait_ge(xqk_ready, HA)
                        for i, (b, g) in enumerate(HALVES):
                            if i >= 2:
                                pe.wait_ge(xvo_ready, i - 1)
                            nc.tensor.matmul(bank[i % 2][:], xT[:, b * P:(b + 1) * P], wvo[:, g * 512:(g + 1) * 512],
                                             start=True, stop=True).then_inc(xvo_projected, 1)
                        for i, (b, g) in enumerate(HALVES):
                            if i >= 2:
                                pe.wait_ge(att_ready, i - 1)
                            for j in range(4):
                                h = 4 * g + j
                                last = nc.tensor.matmul(bank[4 + i % 2][:, j * P:(j + 1) * P],
                                                        xqk[:, h, b * P:(b + 1) * P], xT[:, b * P:(b + 1) * P],
                                                        start=True, stop=True)
                            last.then_inc(scored, 1)
                        pe.wait_ge(decay_ready, 8)
                        for i, (b, g) in enumerate(HALVES):
                            pe.wait_ge(att_ready, i + 1)
                            if i >= 2:
                                pe.wait_ge(attT_ready, i - 1)
                            for j in range(4):
                                last = nc.tensor.transpose(bank[2 + i % 2][:, j * P:(j + 1) * P],
                                                           att[:, b, 4 * g + j, :], ident[:])
                            last.then_inc(att_transposed, 1)
                        pe.wait_ge(xvo_ready, 8)
                        for i, (b, g) in enumerate(HALVES):
                            pe.wait_ge(attT_ready, i + 1)
                            for j in range(4):
                                h = 4 * g + j
                                last = nc.tensor.matmul(bank[6][:, b * D:(b + 1) * D], attT[:, b, h, :],
                                                        xvo[:, b, h * D:(h + 1) * D], start=(h == 0), stop=(h == HA - 1))
                        last.then_inc(summed, 1)

                    @block.scalar
                    def _(act):
                        act.wait_ge(z_ready, 1)
                        nc.scalar.activation(z_abs[:], z[:], ACT.Abs).then_inc(abs_ready, 1)
                        act.wait_ge(abs_ready, 1)
                        nc.scalar.activation(z_exp[:], z_abs[:], ACT.Exp, scale=-1.0).then_inc(exp_ready, 1)
                        act.wait_ge(exp_ready, 1)
                        nc.scalar.activation(z_exp[:], z_exp[:], ACT.Ln, bias=1.0).then_inc(ln_ready, 1)
                        for h in range(HA):
                            act.wait_ge(xqk_projected, h + 1)
                            nc.scalar.activation(xqk[:, h, :], bank[h % 2][:], ACT.Copy).then_inc(xqk_ready, 1)
                        for i, (b, g) in enumerate(HALVES):
                            act.wait_ge(decay_summed, i + 1)
                            nc.scalar.activation(decay[:, b, 4 * g:4 * g + 4, :], bank[2 + i % 2][:].rearrange(
                                "p (h s) -> p h s", h=4), ACT.Exp).then_inc(decay_ready, 1)
                        for i, (b, g) in enumerate(HALVES):
                            act.wait_ge(xvo_projected, i + 1)
                            nc.scalar.activation(xvo[:, b, g * 512:(g + 1) * 512], bank[i % 2][:],
                                                 ACT.Copy).then_inc(xvo_ready, 1)
                        for i, (b, g) in enumerate(HALVES):
                            act.wait_ge(att_transposed, i + 1)
                            nc.scalar.activation(attT[:, b, 4 * g:4 * g + 4, :], bank[2 + i % 2][:].rearrange(
                                "p (h s) -> p h s", h=4), ACT.Copy).then_inc(attT_ready, 1)

                    @block.sync
                    def _(sp):
                        for b in range(B):
                            sp.wait_ge(lam_ready, LVU)
                            sp.dma_start(scratch[b].rearrange("(t c) -> t c", t=T),
                                         lam[:, b, :, :].rearrange("p h c -> p (h c)")).then_inc(lam_stored, 16)
                        for b in range(B):
                            sp.wait_ge(lam_stored, 16 * B)
                            skewed = bass.AP(scratch, b * T * HA * T + T - 1,
                                             [(HA * T - 1, T), (T, HA), (1, T)])
                            sp.dma_start(lamw[:, b, :, :], skewed).then_inc(lamw_ready, 16)

                    @block.vector
                    def _(dve):
                        dve.wait_ge(z_projected, 1)
                        nc.vector.tensor_tensor(z[:], bank[7][:, 0:B * NZ].rearrange("p (b n) -> p b n", b=B),
                                                bcast(z_bias[:], 1, B), ALU.add).then_inc(z_ready, 1)
                        dve.wait_ge(ln_ready, 1)
                        nc.vector.scalar_tensor_tensor(out=sp_z[:], in0=z[:], scalar=0.0, in1=z_exp[:], op0=ALU.max,
                                                       op1=ALU.add).then_inc(gates_ready, 1)
                        dve.wait_ge(gates_ready, 1)
                        lvs = sp_z[:, :, HA:NZ].rearrange("p b (h l) -> p b h l", h=HA)
                        for l in range(LVU):
                            d0, d1 = (0, 1) if l == 0 else (2 ** (l - 1), 2 ** l)
                            nc.vector.tensor_copy(lam[:, :, :, T - d1:T - d0],
                                                  bcast(lvs[:, :, :, l], 3, d1 - d0)).then_inc(lam_ready, 1)
                        for b in range(B):
                            dve.wait_ge(decay_ready, 2 * b + 2)
                            dve.wait_ge(lamw_ready, 16 * B)
                            nc.vector.tensor_tensor(lamw[:, b, :, :], lamw[:, b, :, :], decay[:, b, :, :],
                                                    ALU.mult).then_inc(dl_ready, 1)
                        for i, (b, g) in enumerate(HALVES):
                            dve.wait_ge(scored, i + 1)
                            dve.wait_ge(dl_ready, b + 1)
                            hs = slice(4 * g, 4 * g + 4)
                            nc.vector.scalar_tensor_tensor(
                                out=att[:, b, hs, :], in0=bank[4 + i % 2][:].rearrange("p (h s) -> p h s", h=4),
                                scalar=SCALE, in1=lamw[:, b, hs, :], op0=ALU.mult, op1=ALU.mult).then_inc(att_ready, 1)
                        dve.wait_ge(summed, 1)
                        chain = Chain(dve, y_steps)
                        chain(nc.vector.tensor_tensor(y[:], bank[6][:].rearrange("p (b d) -> p b d", b=B), xn[:],
                                                      ALU.add))
                        for b in range(B):
                            nc.vector.bn_stats(bn[:, b, :], y[:, b, :]).then_inc(y_steps, 1)
                        dve.wait_ge(y_steps, 1 + B)
                        for b in range(B):
                            nc.vector.bn_aggr(mv[:, b, :], bn[:, b, :]).then_inc(y_steps, 1)
                        dve.wait_ge(y_steps, 1 + 2 * B)
                        nc.vector.tensor_scalar(var_eps[:], mv[:, :, 1], EPS, None, ALU.add).then_inc(y_var_ready, 1)
                        dve.wait_ge(y_rstd_ready, 1)
                        for b in range(B):
                            nc.vector.tensor_scalar(y[:, b, :], y[:, b, :], mv[:, b, 0:1], rstd[:, b:b + 1],
                                                    ALU.subtract, ALU.mult).then_inc(y_steps, 1)
                        chain.at = 1 + 3 * B
                        dve.wait_ge(y_steps, chain.at)
                        chain(nc.vector.tensor_tensor(y[:], y[:], bcast(ln_g[:], 1, B), ALU.mult))
                        chain(nc.vector.tensor_tensor(y[:], y[:], bcast(ln_b[:], 1, B), ALU.add))
                        chain(nc.vector.tensor_tensor(x[:], x[:], y[:], ALU.add))

                    @block.gpsimd
                    def _(pool):
                        pool.wait_ge(y_var_ready, 1)
                        nc.gpsimd.tensor_tensor(rstd[:], var_eps[:], minus_half[:], ALU.pow).then_inc(y_rstd_ready, 1)

        up_summed, silu_ready, hid_ready, down_summed, added, b_down_summed = (
            sem(n) for n in ("up_summed", "silu_ready", "hid_ready", "down_summed", "added", "b_down_summed"))

        def expert_sum(name, up1, up2, down, bias1, bias2, gates, b_down, before):
            with ExitStack() as c2:
                act1 = c2.enter_context(nc.sbuf_tensor(f"{name}_act1", [P, 3, BT], F32))
                hid = c2.enter_context(nc.sbuf_tensor(f"{name}_hid", [P, 3, BT], F32))
                U = HM * E
                U0, E0, A0 = before * U, before * E, before * (E + 1)
                first = 1 if b_down else 0
                with nc.Block() as block:
                    @block.tensor
                    def _(pe):
                        def up(u):
                            e, m = divmod(u, HM)
                            if u >= 3:
                                pe.wait_ge(hid_ready, U0 + u - 2)
                            nc.tensor.matmul(bank[2 * (u % 3)][:], up1(e, m), xT[:], start=True, stop=True)
                            nc.tensor.matmul(bank[2 * (u % 3) + 1][:], up2(e, m), xT[:], start=True,
                                             stop=True).then_inc(up_summed, 1)

                        def down_(u):
                            e, m = divmod(u, HM)
                            pe.wait_ge(hid_ready, U0 + u + 1)
                            if m == 0 and e + first >= 2:
                                pe.wait_ge(added, A0 + e + first - 1)
                            for b in range(B):
                                last = nc.tensor.matmul(bank[6 + (e + first) % 2][:, b * D:(b + 1) * D],
                                                        hid[:, u % 3, b * P:(b + 1) * P], down(e, m),
                                                        start=(m == 0 and b == 0), stop=(m == HM - 1 and b == B - 1),
                                                        skip_group_check=True)
                            if m == HM - 1:
                                last.then_inc(down_summed, 1)

                        up(0)
                        if b_down:
                            gT, rows = b_down
                            for b in range(B):
                                last = nc.tensor.matmul(bank[6][:, b * D:(b + 1) * D], gT[:, b * P:(b + 1) * P], rows[:],
                                                        start=(b == 0), stop=(b == B - 1), skip_group_check=True)
                            last.then_inc(b_down_summed, 1)
                        up(1)
                        for u in range(2, U + 2):
                            if u < U:
                                up(u)
                            down_(u - 2)

                    @block.scalar
                    def _(act):
                        for u in range(U):
                            e, m = divmod(u, HM)
                            act.wait_ge(up_summed, U0 + u + 1)
                            if u >= 3:
                                act.wait_ge(hid_ready, U0 + u - 2)
                            nc.scalar.activation(act1[:, u % 3, :], bank[2 * (u % 3)][:], ACT.Silu,
                                                 bias=bias1(e, m) if bias1 else 0.0).then_inc(silu_ready, 1)

                    @block.vector
                    def _(dve):
                        def add(e):
                            dve.wait_ge(down_summed, E0 + e + 1)
                            if e + first >= 1:
                                dve.wait_ge(added, A0 + e + first)
                            for b in range(B):
                                last = nc.vector.scalar_tensor_tensor(
                                    out=x[:, b, :], in0=bank[6 + (e + first) % 2][:, b * D:(b + 1) * D],
                                    scalar=gates(b, e), in1=x[:, b, :], op0=ALU.mult, op1=ALU.add)
                            last.then_inc(added, 1)

                        if b_down:
                            dve.wait_ge(b_down_summed, 1)
                            nc.vector.tensor_tensor(x[:], bank[6][:].rearrange("p (b d) -> p b d", b=B), x[:],
                                                    ALU.add).then_inc(added, 1)
                        for u in range(U):
                            e, m = divmod(u, HM)
                            dve.wait_ge(silu_ready, U0 + u + 1)
                            if u >= 3:
                                if (u - 3) % HM == HM - 1:
                                    dve.wait_ge(down_summed, E0 + (u - 3) // HM + 1)
                                else:
                                    dve.wait_ge(up_summed, U0 + u + 1)
                            if bias2:
                                nc.vector.scalar_tensor_tensor(
                                    out=hid[:, u % 3, :], in0=bank[2 * (u % 3) + 1][:], scalar=bias2(e, m),
                                    in1=act1[:, u % 3, :], op0=ALU.add, op1=ALU.mult).then_inc(hid_ready, 1)
                            else:
                                nc.vector.tensor_tensor(hid[:, u % 3, :], bank[2 * (u % 3) + 1][:], act1[:, u % 3, :],
                                                        ALU.mult).then_inc(hid_ready, 1)
                            if m == HM - 1 and e >= 1:
                                add(e - 1)
                        add(E - 1)

        def lora_ffn(name, w):
            with ExitStack() as c2:
                def sb(n, shape, dt=F32):
                    return c2.enter_context(nc.sbuf_tensor(f"{name}_{n}", shape, dt))

                def sem(n):
                    return ctx.enter_context(nc.semaphore(f"{name}_{n}"))

                EM = E * HM
                up_rows = [sb("w1", [P, EM, D]), sb("w3", [P, EM, D])]
                up_a = [sb("a1", [R, E, D]), sb("a3", [R, E, D])]
                up_b = [sb("b1l", [P, EM, R]), sb("b3l", [P, EM, R])]
                down_rows = sb("w2", [P, E, HID])
                down_a, down_b = sb("a2", [R, E, HID]), sb("b2l", [P, E, R])
                bias_rows = sb("bias_rows", [2 * EM, P])
                b_down = sb("b_down", [E, D])
                wg = sb("wg", [E, D])
                upT = [sb("w1T", [P, EM, P]), sb("w3T", [P, EM, P])]
                downT = sb("w2T", [P, EM, D])
                up_bT = [sb("b1T", [R, EM, P]), sb("b3T", [R, EM, P])]
                down_bT = sb("b2T", [R, E, P])
                biases = sb("biases", [P, 2 * EM])
                wgT = sb("wgT", [P, E])
                w_loaded = sem("w_loaded")
                turned, turned_out, folded, folded_out = (
                    sem(n) for n in ("turned", "turned_out", "folded", "folded_out"))

                logits = sb("logits", [P, B, E])
                nmax, den = sb("nmax", [P, B]), sb("den", [P, B])
                top = sb("top", [P, B, 8])
                at = sb("at", [P, B, 8], U32)
                atf = sb("atf", [P, B, 8])
                wsum = sb("wsum", [P, B])
                hot = sb("hot", [P, B, E])
                gates = sb("gates", [P, B, E])
                numbers = sb("numbers", [P, E])
                gatesT = sb("gatesT", [E, BT])
                routed, gsteps, lmax_ready, lexp_ready, gates_ready, gates_turned = (
                    sem(n) for n in ("routed", "gsteps", "lmax_ready", "lexp_ready", "gates_ready", "gates_turned"))
                numbers_ready = sem("numbers_ready")

                def load(sp):
                    for k, (ww, aa, bb) in enumerate((("w1", "a1", "b1l"), ("w3", "a3", "b3l"))):
                        sp.dma_start(up_rows[k][:], w[ww].rearrange("e (m p) d -> p (e m) d", p=P)).then_inc(w_loaded, 16)
                        sp.dma_start(up_a[k][:], w[aa].rearrange("e r d -> r e d")).then_inc(w_loaded, 16)
                        sp.dma_start(up_b[k][:], w[bb].rearrange("e (m p) r -> p (e m) r", p=P)).then_inc(w_loaded, 16)
                    sp.dma_start(down_rows[:], w["w2"].rearrange("e d h -> d e h")).then_inc(w_loaded, 16)
                    sp.dma_start(down_a[:], w["a2"].rearrange("e r h -> r e h")).then_inc(w_loaded, 16)
                    sp.dma_start(down_b[:], w["b2l"].rearrange("e d r -> d e r")).then_inc(w_loaded, 16)
                    sp.dma_start(bias_rows[0:EM, :], w["b1"].rearrange("e (m p) -> (e m) p", p=P)).then_inc(w_loaded, 16)
                    sp.dma_start(bias_rows[EM:2 * EM, :], w["b3"].rearrange("e (m p) -> (e m) p", p=P)).then_inc(w_loaded, 16)
                    sp.dma_start(b_down[:], w["b2"]).then_inc(w_loaded, 16)
                    sp.dma_start(wg[:], w["wg"]).then_inc(w_loaded, 16)

                layer_norm(load)
                with nc.Block() as block:
                    turns = [(up_b[k][:, i, :], up_bT[k][:, i, :]) for k in range(2) for i in range(EM)]
                    turns += [(down_b[:, e, :], down_bT[:, e, :]) for e in range(E)]
                    folds = [(up_rows[k][:, i, :], up_a[k][:, i // HM, :], up_bT[k][:, i, :], False)
                             for k in range(2) for i in range(EM)]
                    folds += [(down_rows[:, i // HM, i % HM * P:(i % HM + 1) * P],
                               down_a[:, i // HM, i % HM * P:(i % HM + 1) * P], down_bT[:, i // HM, :], True)
                              for i in range(EM)]
                    TG, FG = len(turns) // 4, len(folds) // 4

                    @block.tensor
                    def _(pe):
                        pe.wait_ge(w_loaded, 16 * 13)
                        nc.tensor.transpose(bank[6][:, 0:2 * EM], bias_rows[:, :], ident[0:2 * EM, 0:2 * EM])
                        nc.tensor.transpose(bank[6][:, 2 * EM:2 * EM + E], wg[:, :],
                                            ident[0:E, 0:E]).then_inc(turned, 1)
                        pe.wait_ge(turned_out, 1)
                        for b in range(B):
                            last = nc.tensor.matmul(bank[4][:, b * E:(b + 1) * E], xT[:, b * P:(b + 1) * P], wgT[:],
                                                    start=True, stop=True)
                        last.then_inc(routed, 1)
                        for g in range(TG):
                            if g >= 2:
                                pe.wait_ge(turned_out, g)
                            for j in range(4):
                                last = nc.tensor.transpose(bank[g % 2][0:R, j * P:(j + 1) * P], turns[4 * g + j][0],
                                                           ident[:])
                            last.then_inc(turned, 1)
                        pe.wait_ge(turned_out, TG + 1)
                        for g in range(FG):
                            if g >= 2:
                                pe.wait_ge(folded_out, g - 1)
                            for j in range(4):
                                rows, a, bT, _ = folds[4 * g + j]
                                ps = bank[2 + g % 2][:, j * P:(j + 1) * P]
                                nc.tensor.matmul(ps, rows, ident[:], start=True, stop=False)
                                last = nc.tensor.matmul(ps, a, bT, start=False, stop=True)
                            last.then_inc(folded, 1)
                        pe.wait_ge(gates_ready, 1)
                        for b in range(B):
                            last = nc.tensor.transpose(bank[5][0:E, b * P:(b + 1) * P], gates[:, b, :], ident[:])
                        last.then_inc(gates_turned, 1)

                    @block.gpsimd
                    def _(pool):
                        nc.gpsimd.iota(numbers[:], pattern=[[1, E]], base=0, channel_multiplier=0,
                                       allow_small_or_imprecise_dtypes=True).then_inc(numbers_ready, 1)

                    @block.scalar
                    def _(act):
                        for b in range(B):
                            act.wait_ge(lmax_ready, 1)
                            nc.scalar.activation(logits[:, b, :], bank[4][:, b * E:(b + 1) * E], ACT.Exp,
                                                 bias=nmax[:, b:b + 1], accum_out=den[:, b:b + 1]).then_inc(lexp_ready, 1)
                        for g in range(FG):
                            act.wait_ge(folded, g + 1)
                            k, i = divmod(4 * g, EM)
                            dst = (upT[0], upT[1], downT)[k]
                            nc.scalar.activation(dst[:, i:i + 4, :], bank[2 + g % 2][:].rearrange(
                                "p (i h) -> p i h", i=4), ACT.Copy).then_inc(folded_out, 1)

                    @block.vector
                    def _(dve):
                        dve.wait_ge(turned, 1)
                        nc.vector.tensor_copy(biases[:], bank[6][:, 0:2 * EM])
                        nc.vector.tensor_copy(wgT[:], bank[6][:, 2 * EM:2 * EM + E]).then_inc(turned_out, 1)
                        for g in range(TG):
                            dve.wait_ge(turned, g + 2)
                            k, i = divmod(4 * g, EM)
                            dst = (up_bT[0], up_bT[1], down_bT)[k]
                            nc.vector.tensor_copy(dst[:, i:i + 4, :], bank[g % 2][0:R, :].rearrange(
                                "p (i h) -> p i h", i=4)).then_inc(turned_out, 1)
                        dve.wait_ge(routed, 1)
                        nc.vector.tensor_reduce(nmax[:], bank[4][:, 0:B * E].rearrange("p (b e) -> p b e", b=B), AX_X,
                                                ALU.max, negate=True).then_inc(lmax_ready, 1)
                        dve.wait_ge(lexp_ready, B)
                        dve.wait_ge(numbers_ready, 1)
                        chain = Chain(dve, gsteps)
                        chain(nc.vector.reciprocal(den[:], den[:]))
                        chain(nc.vector.tensor_tensor(logits[:], logits[:], bcast(den[:], 2, E), ALU.mult))
                        for b in range(B):
                            chain(nc.vector.max(top[:, b, :], logits[:, b, :]))
                            chain(nc.vector.max_index(at[:, b, :], top[:, b, :], logits[:, b, :]))
                        chain(nc.vector.tensor_copy(atf[:], at[:]))
                        chain(nc.vector.tensor_tensor(wsum[:], top[:, :, 0], top[:, :, 1], ALU.add))
                        chain(nc.vector.reciprocal(wsum[:], wsum[:]))
                        chain(nc.vector.tensor_tensor(top[:], top[:], bcast(wsum[:], 2, 8), ALU.mult))
                        for k, dst in ((0, gates), (1, hot)):
                            chain(nc.vector.tensor_tensor(dst[:], bcast(numbers[:], 1, B), bcast(atf[:, :, k], 2, E),
                                                          ALU.is_equal))
                            chain(nc.vector.tensor_tensor(dst[:], dst[:], bcast(top[:, :, k], 2, E), ALU.mult))
                        nc.vector.tensor_tensor(gates[:], gates[:], hot[:], ALU.add).then_inc(gates_ready, 1)
                        dve.wait_ge(gates_turned, 1)
                        nc.vector.tensor_copy(gatesT[:], bank[5][0:E, :])

                expert_sum(name, lambda e, m: upT[0][:, HM * e + m, :], lambda e, m: upT[1][:, HM * e + m, :],
                           lambda e, m: downT[:, HM * e + m, :],
                           lambda e, m: biases[:, HM * e + m:HM * e + m + 1],
                           lambda e, m: biases[:, EM + HM * e + m:EM + HM * e + m + 1],
                           lambda b, e: gates[:, b, e:e + 1], (gatesT, b_down), 0)

        def banded_attention(name, w):
            with ExitStack() as c2:
                def sb(n, shape, dt=F32):
                    return c2.enter_context(nc.sbuf_tensor(f"{name}_{n}", shape, dt))

                def sem(n):
                    return ctx.enter_context(nc.semaphore(f"{name}_{n}"))

                BAND = D // 4
                qkv_w = sb("qkv_w", [P, 3 * D])
                w_high = sb("w_high", [P, 3 * D])
                w_low = [sb("w_low1", [P, 3 * D], F16), sb("w_low2", [P, 3 * D], F16)]
                xT16 = sb("xT16", [P, BT], F16)
                out_w, out_wT, out_b = sb("out_w", [P, D]), sb("out_wT", [P, D]), sb("out_b", [P, D])
                part = [sb("part1", [P, BT], F16), sb("part2", [P, BT], F16)]
                qkv = [sb("qT", [P, BT]), sb("kT", [P, BT]), sb("v", [P, BT])]
                probs, pT, yT = sb("probs", [P, B, T]), sb("pT", [P, B, T]), sb("yT", [P, BT])
                nmax, den = sb("nmax", [P, B]), sb("den", [P, B])
                loaded, cleared, bands_ready, x16_ready, turned, out_wT_ready = (
                    sem(n) for n in ("loaded", "cleared", "bands_ready", "x16_ready", "turned", "out_wT_ready"))
                projected, part_ready, sum_ready, qkv_ready = (
                    sem(n) for n in ("projected", "part_ready", "sum_ready", "qkv_ready"))
                scored, max_ready, exp_ready, p_turned, pT_ready, mixed, yT_ready, done = (
                    sem(n) for n in ("scored", "max_ready", "exp_ready", "p_turned", "pT_ready", "mixed", "yT_ready",
                                     "done"))
                osteps = sem("osteps")
                SCALE = D ** -0.5
                def load(sp):
                    sp.dma_start(qkv_w[:], w["qkv"]).then_inc(loaded, 16)
                    sp.dma_start(out_w[:], w["out_w"]).then_inc(loaded, 16)
                    sp.dma_start(out_b[:], w["out_b"].partition_broadcast(P)).then_inc(loaded, 16)

                layer_norm(load)
                with nc.Block() as block:
                    @block.gpsimd
                    def _(pool):
                        nc.gpsimd.memset(w_high[:], 0.0).then_inc(cleared, 1)
                        nc.gpsimd.memset(w_low[0][:], 0.0).then_inc(cleared, 1)
                        nc.gpsimd.memset(w_low[1][:], 0.0).then_inc(cleared, 1)

                    @block.vector
                    def _(dve):
                        dve.wait_ge(loaded, 48)
                        dve.wait_ge(cleared, 3)
                        nc.vector.tensor_copy(w_high[BAND:2 * BAND, :], qkv_w[BAND:2 * BAND, :]).then_inc(bands_ready, 1)
                        nc.vector.tensor_copy(w_high[2 * BAND:3 * BAND, :], qkv_w[2 * BAND:3 * BAND, :]).then_inc(bands_ready, 1)
                        nc.vector.tensor_copy(w_low[0][0:BAND, :], qkv_w[0:BAND, :]).then_inc(bands_ready, 1)
                        nc.vector.tensor_copy(w_low[1][3 * BAND:D, :], qkv_w[3 * BAND:D, :]).then_inc(bands_ready, 1)
                        nc.vector.tensor_copy(xT16[:], xT[:]).then_inc(x16_ready, 1)
                        dve.wait_ge(turned, 1)
                        nc.vector.tensor_copy(out_wT[:], bank[7][:, 0:D]).then_inc(out_wT_ready, 1)
                        for i in range(3):
                            dve.wait_ge(part_ready, 2 * i + 1)
                            nc.vector.tensor_tensor(qkv[i][:], bank[1 + 3 * (i % 2)][:], part[0][:], ALU.add).then_inc(sum_ready, 1)
                            dve.wait_ge(sum_ready, i + 1)
                            dve.wait_ge(part_ready, 2 * i + 2)
                            nc.vector.tensor_tensor(qkv[i][:], qkv[i][:], part[1][:], ALU.add).then_inc(qkv_ready, 1)
                        dve.wait_ge(scored, 1)
                        nc.vector.tensor_reduce(nmax[:], bank[6][:].rearrange("p (b k) -> p b k", b=B), AX_X, ALU.max,
                                                negate=True).then_inc(osteps, 1)
                        dve.wait_ge(osteps, 1)
                        nc.vector.tensor_scalar(nmax[:], nmax[:], SCALE, None, ALU.mult).then_inc(max_ready, 1)
                        dve.wait_ge(exp_ready, B)
                        nc.vector.reciprocal(den[:], den[:]).then_inc(osteps, 1)
                        nc.vector.tensor_tensor(x[:], x[:], bcast(out_b[:], 1, B), ALU.add).then_inc(osteps, 1)
                        dve.wait_ge(osteps, 3)
                        dve.wait_ge(done, 1)
                        for b in range(B):
                            nc.vector.scalar_tensor_tensor(out=x[:, b, :], in0=bank[3][:, b * D:(b + 1) * D],
                                                           scalar=den[:, b:b + 1], in1=x[:, b, :], op0=ALU.mult,
                                                           op1=ALU.add)

                    @block.tensor
                    def _(pe):
                        pe.wait_ge(loaded, 48)
                        nc.tensor.transpose(bank[7][:, 0:D], out_w[:], ident[:]).then_inc(turned, 1)
                        pe.wait_ge(bands_ready, 4)
                        pe.wait_ge(x16_ready, 1)
                        for i in range(3):
                            if i == 2:
                                pe.wait_ge(qkv_ready, 1)
                            for k, (ww, xx) in enumerate(((w_low[0], xT16), (w_high, xT), (w_low[1], xT16))):
                                ps = bank[k + 3 * (i % 2)]
                                if i < 2:
                                    last = nc.tensor.matmul(ps[:], ww[:, i * D:(i + 1) * D], xx[:], start=True, stop=True)
                                else:
                                    for b in range(B):
                                        last = nc.tensor.matmul(ps[:, b * D:(b + 1) * D], xx[:, b * P:(b + 1) * P],
                                                                ww[:, i * D:(i + 1) * D], start=True, stop=True)
                            last.then_inc(projected, 1)
                        pe.wait_ge(qkv_ready, 2)
                        for b in range(B):
                            cols = slice(b * P, (b + 1) * P)
                            last = nc.tensor.matmul(bank[6][:, cols], qkv[0][:, cols], qkv[1][:, cols], start=True, stop=True)
                        last.then_inc(scored, 1)
                        pe.wait_ge(exp_ready, B)
                        pe.wait_ge(out_wT_ready, 1)
                        for b in range(B):
                            last = nc.tensor.transpose(bank[7][:, b * P:(b + 1) * P], probs[:, b, :], ident[:])
                        last.then_inc(p_turned, 1)
                        pe.wait_ge(pT_ready, 1)
                        pe.wait_ge(qkv_ready, 3)
                        for b in range(B):
                            last = nc.tensor.matmul(bank[5][:, b * P:(b + 1) * P], qkv[2][:, b * D:(b + 1) * D], pT[:, b, :],
                                                    start=True, stop=True)
                        last.then_inc(mixed, 1)
                        pe.wait_ge(yT_ready, 1)
                        for b in range(B):
                            last = nc.tensor.matmul(bank[3][:, b * D:(b + 1) * D], yT[:, b * P:(b + 1) * P], out_wT[:],
                                                    start=True, stop=True)
                        last.then_inc(done, 1)

                    @block.scalar
                    def _(act):
                        for i in range(3):
                            act.wait_ge(projected, i + 1)
                            for k in range(2):
                                if i:
                                    act.wait_ge(qkv_ready, i)
                                nc.scalar.activation(part[k][:], bank[2 * k + 3 * (i % 2)][:], ACT.Copy).then_inc(part_ready, 1)
                        act.wait_ge(max_ready, 1)
                        for b in range(B):
                            nc.scalar.activation(probs[:, b, :], bank[6][:, b * P:(b + 1) * P], ACT.Exp, scale=SCALE,
                                                 bias=nmax[:, b:b + 1], accum_out=den[:, b:b + 1]).then_inc(exp_ready, 1)
                        act.wait_ge(p_turned, 1)
                        nc.scalar.activation(pT[:], bank[7][:].rearrange("p (b q) -> p b q", b=B), ACT.Copy).then_inc(pT_ready, 1)
                        act.wait_ge(mixed, 1)
                        nc.scalar.activation(yT[:], bank[5][:], ACT.Copy).then_inc(yT_ready, 1)

        def choice_ffn(name, w):
            with ExitStack() as c2:
                def sb(n, shape, dt=F32):
                    return c2.enter_context(nc.sbuf_tensor(f"{name}_{n}", shape, dt))

                def sem(n):
                    return ctx.enter_context(nc.semaphore(f"{name}_{n}"))

                up1, up2 = sb("wg", [P, E, HID]), sb("wu", [P, E, HID])
                down = sb("wd", [P, E * HM, D])
                gate_w = sb("gate_w", [P, E])
                aff, nmax, den = sb("aff", [P, B, E]), sb("nmax", [P, B]), sb("den", [P, B])
                loaded, routed, max_ready, exp_ready, steps = (
                    sem(n) for n in ("loaded", "routed", "max_ready", "exp_ready", "steps"))
                def load(sp):
                    sp.dma_start(gate_w[:], w["gate_w"]).then_inc(loaded, 16)
                    sp.dma_start(up1[:], w["wg"].rearrange("e d i -> d e i")).then_inc(loaded, 16)
                    sp.dma_start(up2[:], w["wu"].rearrange("e d i -> d e i")).then_inc(loaded, 16)
                    sp.dma_start(down[:], w["wd"].rearrange("e (m p) d -> p (e m) d", p=P)).then_inc(loaded, 16)

                layer_norm(load)
                with nc.Block() as block:
                    @block.tensor
                    def _(pe):
                        pe.wait_ge(loaded, 64)
                        for b in range(B):
                            last = nc.tensor.matmul(bank[0][:, b * E:(b + 1) * E], xT[:, b * P:(b + 1) * P], gate_w[:],
                                                    start=True, stop=True)
                        last.then_inc(routed, 1)

                    @block.scalar
                    def _(act):
                        act.wait_ge(max_ready, 1)
                        for b in range(B):
                            nc.scalar.activation(aff[:, b, :], bank[0][:, b * E:(b + 1) * E], ACT.Exp,
                                                 bias=nmax[:, b:b + 1], accum_out=den[:, b:b + 1]).then_inc(exp_ready, 1)

                    @block.vector
                    def _(dve):
                        dve.wait_ge(routed, 1)
                        nc.vector.tensor_reduce(nmax[:], bank[0][:, 0:B * E].rearrange("p (b e) -> p b e", b=B), AX_X,
                                                ALU.max, negate=True).then_inc(max_ready, 1)
                        dve.wait_ge(exp_ready, B)
                        chain = Chain(dve, steps)
                        chain(nc.vector.reciprocal(den[:], den[:]))
                        chain(nc.vector.tensor_tensor(aff[:], aff[:], bcast(den[:], 2, E), ALU.mult))

                expert_sum(name, lambda e, m: up1[:, e, m * P:(m + 1) * P], lambda e, m: up2[:, e, m * P:(m + 1) * P],
                           lambda e, m: down[:, HM * e + m, :], None, None, lambda b, e: aff[:, b, e:e + 1], None, 1)


        cross_attention(0, dict(wq=A["L0_xattn_wq_k"], bq=A["L0_xattn_wq_b"], wk=A["L0_xattn_wk_k"],
                                    bk=A["L0_xattn_wk_b"], wv=A["L0_xattn_wv_k"], bv=A["L0_xattn_wv_b"],
                                    wo=A["L0_xattn_wo_k"], bo=A["L0_xattn_wo_b"]), True)
        retention("ret", dict(wq=A["L0_attn_Wq"], wk=A["L0_attn_Wk"], wv=A["L0_attn_Wv"], wo=A["L0_attn_Wo"],
                              wg=A["L0_attn_Wg"], bg=A["L0_attn_bg"], wdl=A["L0_attn_Wdl"],
                              lparam=A["L0_attn_Lparam"], ln_g=A["L0_attn_ln_g"], ln_b=A["L0_attn_ln_b"]))
        lora_ffn("ffn0", dict(w1=A["L0_ffn_W1"], w2=A["L0_ffn_W2"], w3=A["L0_ffn_W3"], a1=A["L0_ffn_A1"],
                              a2=A["L0_ffn_A2"], a3=A["L0_ffn_A3"], b1l=A["L0_ffn_B1"], b2l=A["L0_ffn_B2"],
                              b3l=A["L0_ffn_B3"], b1=A["L0_ffn_b1"], b2=A["L0_ffn_b2"], b3=A["L0_ffn_b3"],
                              wg=A["L0_ffn_Wg"]))
        cross_attention(1, dict(wq=A["L1_xattn_Wq"], bq=A["L1_xattn_bq"], wk=A["L1_xattn_Wk"],
                                    bk=A["L1_xattn_bk"], wv=A["L1_xattn_Wv"], bv=A["L1_xattn_bv"]), False)
        banded_attention("att1", dict(qkv=A["L1_attn_weight_qkv"], out_w=A["L1_attn_out_w"],
                                      out_b=A["L1_attn_out_b"]))
        choice_ffn("ffn1", dict(gate_w=A["L1_ffn_gate_w"], wg=A["L1_ffn_Wg"], wu=A["L1_ffn_Wu"],
                                wd=A["L1_ffn_Wd"]))

        with nc.Block() as block:
            @block.sync
            def _(sp):
                sp.dma_start(out.rearrange("b t d -> t b d"), x[:]).then_inc(x_moved, 16)
                sp.wait_ge(x_moved, 32)


_INS = [
    "x", "ctx_1024", "fside_BxSxS2_0", "mask_BxSxS2_ik1",
    "L0_xattn_wq_k", "L0_xattn_wq_b", "L0_xattn_wk_k", "L0_xattn_wk_b",
    "L0_xattn_wv_k", "L0_xattn_wv_b", "L0_xattn_wo_k", "L0_xattn_wo_b",
    "L0_attn_Wq", "L0_attn_Wk", "L0_attn_Wv", "L0_attn_Wg",
    "L0_attn_bg", "L0_attn_Wdl", "L0_attn_Lparam", "L0_attn_Wo",
    "L0_attn_ln_g", "L0_attn_ln_b", "L0_ffn_Wg", "L0_ffn_W1",
    "L0_ffn_b1", "L0_ffn_A1", "L0_ffn_B1", "L0_ffn_W2",
    "L0_ffn_b2", "L0_ffn_A2", "L0_ffn_B2", "L0_ffn_W3",
    "L0_ffn_b3", "L0_ffn_A3", "L0_ffn_B3", "L1_xattn_Wq",
    "L1_xattn_bq", "L1_xattn_Wk", "L1_xattn_bk", "L1_xattn_Wv",
    "L1_xattn_bv", "L1_attn_weight_qkv", "L1_attn_out_w", "L1_attn_out_b",
    "L1_ffn_gate_w", "L1_ffn_Wg", "L1_ffn_Wu", "L1_ffn_Wd",
]
_OUTS = [((4, 128, 128), "float32")]


def kernel(**inputs):
    import numpy as _np
    import concourse.bacc as _bacc
    from concourse import mybir as _mybir
    from concourse.bass_utils import run_bass_kernel_spmd as _run

    nc = _bacc.Bacc("TRN2", target_bir_lowering=False, num_devices=1)
    arrays, aps = {}, {}
    for name in _INS:
        a = _np.ascontiguousarray(inputs[name])
        arrays[f"in_{name}_dram"] = a
        aps[name] = nc.dram_tensor(f"in_{name}_dram", a.shape, _mybir.dt.from_np(a.dtype), kind="ExternalInput").ap()
    outs = []
    for i, (shape, dtype) in enumerate(_OUTS):
        dt = _mybir.dt.from_np(_np.dtype(dtype))
        outs.append(nc.dram_tensor(f"out_{i}_dram", shape, dt, kind="ExternalOutput").ap())
    perceiver_kernel(nc, aps, outs[0])
    r = _run(nc, [arrays], core_ids=[0])
    return r.results[0]["out_0_dram"]
```
